# Optimizing a Trainium2 kernel written in Bass

```python
import numpy as np
import jax
import jax.numpy as jnp

def _softmax(x, axis=-1):
    return jax.nn.softmax(x, axis=axis)

def _gelu(x):
    return jax.nn.gelu(x, approximate=True)

def _silu(x):
    return jax.nn.silu(x)

def _sigmoid(x):
    return jax.nn.sigmoid(x)

def _layernorm(x, axis=-1, eps=1e-05):
    m = jnp.mean(x, axis=axis, keepdims=True)
    v = jnp.var(x, axis=axis, keepdims=True)
    return (x - m) / jnp.sqrt(v + eps)

def _scatter_add(tgt, idx, src, axis=0):
    return tgt.at[idx].add(src)

def _segment_sum(src, seg, n):
    return jax.ops.segment_sum(src, seg, n)
kernel_name = 'mk_adaln_d1_jaxref_r4_f0308b'

def setup_inputs(seed: int=0):
    np.random.seed(seed)
    _w = jnp.asarray

    def _L0_attn_setup():
        import jax, jax.numpy as jnp
        import numpy as np
        import math
        HIDDEN = 512
        NUM_HEADS = 32
        HEAD_DIM = 64
        WINDOW = 256
        GLOBAL_HEADS = 2
        LOCAL_HEADS = NUM_HEADS - GLOBAL_HEADS
        ROPE_BASE = 10000.0

        def rotate_half(x):
            x1, x2 = jnp.split(x, 2, axis=-1)
            return jnp.concatenate([-x2, x1], axis=-1)

        def rope_cos_sin(positions, dim):
            inv_freq = 1.0 / ROPE_BASE ** (jnp.arange(0, dim, 2, dtype=jnp.float32) / dim)
            freqs = positions[:, None].astype(jnp.float32) * inv_freq[None, :]
            emb = jnp.concatenate([freqs, freqs], axis=-1)
            return (jnp.cos(emb)[None, None], jnp.sin(emb)[None, None])

        def apply_rope(q, k, q_pos, k_pos):
            cos_q, sin_q = rope_cos_sin(q_pos, q.shape[-1])
            cos_k, sin_k = rope_cos_sin(k_pos, k.shape[-1])
            return (q * cos_q + rotate_half(q) * sin_q, k * cos_k + rotate_half(k) * sin_k)

        def sliding_window_attention_blockwise(q, k, v, window_size):
            B, H, L, D = q.shape
            block = min(window_size, 256)
            scale = 1.0 / math.sqrt(D)
            outs = []
            for start in range(0, L, block):
                end = min(start + block, L)
                ks = max(0, start - window_size // 2)
                ke = end
                qb = q[:, :, start:end]
                kb = k[:, :, ks:ke]
                vb = v[:, :, ks:ke]
                s = jnp.einsum('bhqd,bhkd->bhqk', qb, kb) * scale
                qi = jnp.arange(start, end)[:, None]
                ki = jnp.arange(ks, ke)[None, :]
                s = jnp.where(qi >= ki, s, -jnp.inf)
                a = jax.nn.softmax(s, axis=-1)
                outs.append(jnp.einsum('bhqk,bhkd->bhqd', a, vb))
            return jnp.concatenate(outs, axis=2)

        def global_attention(q, k, v):
            B, H, L, D = q.shape
            scale = 1.0 / math.sqrt(D)
            s = jnp.einsum('bhqd,bhkd->bhqk', q, k) * scale
            causal = jnp.tril(jnp.ones((L, L), dtype=bool))
            s = jnp.where(causal[None, None], s, -jnp.inf)
            a = jax.nn.softmax(s, axis=-1)
            return jnp.einsum('bhqk,bhkd->bhqd', a, v)
        key = jax.random.key(seed)
        k1, k2, k3, k4, k5, k6 = jax.random.split(key, 6)
        B, L = (2, 1024)
        P = NUM_HEADS * HEAD_DIM
        return {'hidden_states': jax.random.normal(k1, (B, L, HIDDEN), dtype=jnp.float32), 'Wq': jax.random.normal(k2, (P, HIDDEN), dtype=jnp.float32) * 0.02, 'Wk': jax.random.normal(k3, (P, HIDDEN), dtype=jnp.float32) * 0.02, 'Wv': jax.random.normal(k4, (P, HIDDEN), dtype=jnp.float32) * 0.02, 'Wo': jax.random.normal(k5, (HIDDEN, P), dtype=jnp.float32) * 0.02, 'bo': jax.random.normal(k6, (HIDDEN,), dtype=jnp.float32) * 0.02}
    _L0_attn_in = _L0_attn_setup()

    def _L0_ffn_setup():
        import jax, jax.numpy as jnp
        import numpy as np

        def _sparsify_2to4(h):
            B, S, I = h.shape
            g = h.reshape(B, S, I // 4, 4)
            a = jnp.abs(g)
            _, idx = jax.lax.top_k(a, 2)
            pos = jnp.arange(4)
            mask = (pos == idx[..., 0:1]) | (pos == idx[..., 1:2])
            return (g * mask.astype(g.dtype)).reshape(B, S, I)
        key = jax.random.key(seed)
        k1, k2, k3, k4 = jax.random.split(key, 4)
        B, S, H, I = (4, 512, 512, 2048)
        x = jax.random.normal(k1, (B, S, H), dtype=jnp.float32)
        w_gate = jax.random.normal(k2, (H, I), dtype=jnp.float32) / np.sqrt(H)
        w_up = jax.random.normal(k3, (H, I), dtype=jnp.float32) / np.sqrt(H)
        w_down = jax.random.normal(k4, (I, H), dtype=jnp.float32) / np.sqrt(I)
        return {'x': x, 'w_gate': w_gate, 'w_up': w_up, 'w_down': w_down}
    _L0_ffn_in = _L0_ffn_setup()
    _L0_c = _w((lambda *s: np.random.randn(*s).astype(np.float32) * 0.05)(1, 512))
    _L0_wmod = _w((lambda *s: np.random.randn(*s).astype(np.float32) * 0.05)(512, 6 * 512) * 512 ** (-0.5))
    _d = {'L0_attn_hidden_states': _L0_attn_in['hidden_states'], 'L0_attn_Wq': _L0_attn_in['Wq'], 'L0_attn_Wk': _L0_attn_in['Wk'], 'L0_attn_Wv': _L0_attn_in['Wv'], 'L0_attn_Wo': _L0_attn_in['Wo'], 'L0_attn_bo': _L0_attn_in['bo'], 'L0_ffn_w_gate': _L0_ffn_in['w_gate'], 'L0_ffn_w_up': _L0_ffn_in['w_up'], 'L0_ffn_w_down': _L0_ffn_in['w_down'], 'L0_c': _L0_c, 'L0_wmod': _L0_wmod}
    _x0 = _d['L0_attn_hidden_states']
    _d['L0_attn_hidden_states'] = jax.random.normal(jax.random.fold_in(jax.random.key(seed), 1), (1, 2048, 512), dtype=_x0.dtype)
    del _x0
    return _d

def reference(L0_attn_hidden_states, L0_attn_Wq, L0_attn_Wk, L0_attn_Wv, L0_attn_Wo, L0_attn_bo, L0_ffn_w_gate, L0_ffn_w_up, L0_ffn_w_down, L0_c, L0_wmod):

    def _L0_attn_ref(hidden_states, Wq, Wk, Wv, Wo, bo):
        import jax, jax.numpy as jnp
        import numpy as np
        import math
        HIDDEN = 512
        NUM_HEADS = 32
        HEAD_DIM = 64
        WINDOW = 256
        GLOBAL_HEADS = 2
        LOCAL_HEADS = NUM_HEADS - GLOBAL_HEADS
        ROPE_BASE = 10000.0

        def rotate_half(x):
            x1, x2 = jnp.split(x, 2, axis=-1)
            return jnp.concatenate([-x2, x1], axis=-1)

        def rope_cos_sin(positions, dim):
            inv_freq = 1.0 / ROPE_BASE ** (jnp.arange(0, dim, 2, dtype=jnp.float32) / dim)
            freqs = positions[:, None].astype(jnp.float32) * inv_freq[None, :]
            emb = jnp.concatenate([freqs, freqs], axis=-1)
            return (jnp.cos(emb)[None, None], jnp.sin(emb)[None, None])

        def apply_rope(q, k, q_pos, k_pos):
            cos_q, sin_q = rope_cos_sin(q_pos, q.shape[-1])
            cos_k, sin_k = rope_cos_sin(k_pos, k.shape[-1])
            return (q * cos_q + rotate_half(q) * sin_q, k * cos_k + rotate_half(k) * sin_k)

        def sliding_window_attention_blockwise(q, k, v, window_size):
            B, H, L, D = q.shape
            block = min(window_size, 256)
            scale = 1.0 / math.sqrt(D)
            outs = []
            for start in range(0, L, block):
                end = min(start + block, L)
                ks = max(0, start - window_size // 2)
                ke = end
                qb = q[:, :, start:end]
                kb = k[:, :, ks:ke]
                vb = v[:, :, ks:ke]
                s = jnp.einsum('bhqd,bhkd->bhqk', qb, kb) * scale
                qi = jnp.arange(start, end)[:, None]
                ki = jnp.arange(ks, ke)[None, :]
                s = jnp.where(qi >= ki, s, -jnp.inf)
                a = jax.nn.softmax(s, axis=-1)
                outs.append(jnp.einsum('bhqk,bhkd->bhqd', a, vb))
            return jnp.concatenate(outs, axis=2)

        def global_attention(q, k, v):
            B, H, L, D = q.shape
            scale = 1.0 / math.sqrt(D)
            s = jnp.einsum('bhqd,bhkd->bhqk', q, k) * scale
            causal = jnp.tril(jnp.ones((L, L), dtype=bool))
            s = jnp.where(causal[None, None], s, -jnp.inf)
            a = jax.nn.softmax(s, axis=-1)
            return jnp.einsum('bhqk,bhkd->bhqd', a, v)
        B, L, _ = hidden_states.shape
        q = jnp.einsum('blh,ph->blp', hidden_states, Wq).reshape(B, L, NUM_HEADS, HEAD_DIM).transpose(0, 2, 1, 3)
        k = jnp.einsum('blh,ph->blp', hidden_states, Wk).reshape(B, L, NUM_HEADS, HEAD_DIM).transpose(0, 2, 1, 3)
        v = jnp.einsum('blh,ph->blp', hidden_states, Wv).reshape(B, L, NUM_HEADS, HEAD_DIM).transpose(0, 2, 1, 3)
        pos = jnp.arange(L)
        q, k = apply_rope(q, k, pos, pos)
        ql, qg = (q[:, :LOCAL_HEADS], q[:, LOCAL_HEADS:])
        kl, kg = (k[:, :LOCAL_HEADS], k[:, LOCAL_HEADS:])
        vl, vg = (v[:, :LOCAL_HEADS], v[:, LOCAL_HEADS:])
        out_local = sliding_window_attention_blockwise(ql, kl, vl, WINDOW)
        out_global = global_attention(qg, kg, vg)
        out = jnp.concatenate([out_local, out_global], axis=1)
        out = out.transpose(0, 2, 1, 3).reshape(B, L, NUM_HEADS * HEAD_DIM)
        return jnp.einsum('blp,hp->blh', out, Wo) + bo

    def _L0_ffn_ref(x, w_gate, w_up, w_down):
        import jax, jax.numpy as jnp
        import numpy as np

        def _sparsify_2to4(h):
            B, S, I = h.shape
            g = h.reshape(B, S, I // 4, 4)
            a = jnp.abs(g)
            _, idx = jax.lax.top_k(a, 2)
            pos = jnp.arange(4)
            mask = (pos == idx[..., 0:1]) | (pos == idx[..., 1:2])
            return (g * mask.astype(g.dtype)).reshape(B, S, I)
        h = jax.nn.silu(jnp.einsum('bsh,hi->bsi', x, w_gate)) * jnp.einsum('bsh,hi->bsi', x, w_up)
        h_sparse = _sparsify_2to4(h)
        return jnp.einsum('bsi,ih->bsh', h_sparse, w_down)
    x = L0_attn_hidden_states
    mod = (_silu(L0_c) @ L0_wmod).reshape(L0_c.shape[0], 6, 1, -1)
    sa, ca, ga, sb, cb, gb = (mod[:, 0], mod[:, 1], mod[:, 2], mod[:, 3], mod[:, 4], mod[:, 5])
    ga = (2 * (ga >= 0) - 1) * jnp.maximum(jnp.abs(ga), 0.25)
    gb = (2 * (gb >= 0) - 1) * jnp.maximum(jnp.abs(gb), 0.25)
    h = _layernorm(x, axis=-1) * (1 + ca) + sa
    x = x + ga * _L0_attn_ref(h, L0_attn_Wq, L0_attn_Wk, L0_attn_Wv, L0_attn_Wo, L0_attn_bo)
    h = _layernorm(x, axis=-1) * (1 + cb) + sb
    x = x + gb * _L0_ffn_ref(h, L0_ffn_w_gate, L0_ffn_w_up, L0_ffn_w_down)
    return x

_drawn_inputs = setup_inputs


def setup_inputs(seed=0):
    import zlib

    import numpy as np

    out = dict(_drawn_inputs(seed))
    spreads = {}
    factors = {'L0_attn_Wq': 8.0,
     'L0_attn_Wk': 8.0,
     'L0_attn_Wv': 6.206,
     'L0_attn_Wo': 6.117,
     'L0_attn_bo': 39.605}
    for name, (base, spread) in spreads.items():
        noise = np.random.default_rng([zlib.crc32(name.encode()), seed]).standard_normal(out[name].shape)
        drawn = base * np.exp(spread * noise) if base else spread * noise
        out[name] = jnp.asarray(drawn.astype(out[name].dtype))
    for name, factor in factors.items():
        out[name] = (out[name] * factor).astype(out[name].dtype)
    return out
```

```python
from contextlib import ExitStack

import numpy as np

import concourse.bass as bass
from concourse import mybir

F32 = mybir.dt.float32
F32R = mybir.dt.float32r
BF16 = mybir.dt.bfloat16
ALU = mybir.AluOpType
ACT = mybir.ActivationFunctionType
AX_X = mybir.AxisListType.X

P = 128
TOK = 2048
HID = 512
HC = HID // P
NT = TOK // P
UT = 512
UNITS = TOK // UT
HEADS = 32
D = 64
PAIRS = HEADS // 2
LOCAL_PAIRS = PAIRS - 1
INNER = 2048
BLOCK = 256
LOOKBACK = 128
EPS = 1e-5
GATE_MIN = 0.25
MASKED = -1e30
SCALE = 1.0 / D ** 0.5
NEG_SCALE = -SCALE


def f32(ap):
    return ap.bitcast(F32)


def settle(eng, begun):
    eng.sem_inc(begun, 1)


def make_identity(pool, ident, done):
    pool.memset(ident[:, :], 0.0).then_inc(done, 1)
    pool.wait_ge(done, 1)
    pool.affine_select(out=ident[:, :], in_=ident[:, :], compare_op=ALU.not_equal, fill=1.0,
                       base=0, pattern=[[-1, P]], channel_multiplier=1).then_inc(done, 1)


def stage_a(nc, x, c_cols, wmod, mods_dram, hT_hi, hT_lo):
    with ExitStack() as ctx:
        def sb(name, shape, dt=F32):
            return ctx.enter_context(nc.sbuf_tensor(name, shape, dt))

        def sem(name):
            return ctx.enter_context(nc.semaphore(name))

        ident = sb("a_ident", [P, P])
        c_sb = sb("c_sb", [P, HC])
        silu_c = sb("silu_c", [P, HC])
        ones = sb("ones", [P, P])
        silu_rep = sb("silu_rep", [P, HC, P])
        wm = sb("wm", [P, HC, 6 * HID])
        mods = sb("mods_sb", [P, 6, HID])
        sign = sb("sign", [P, 2, HID])
        mag = sb("mag", [P, 2, HID])
        xt = sb("xt", [P, 2, HID])
        stats = sb("stats", [P, 2, 6])
        mv = sb("mv", [P, 2, 2])
        std = sb("std", [P, 2])
        rstd = sb("rstd", [P, 2])
        xn = sb("xn", [P, 2, HID])
        scaled = sb("scaled", [P, 2, HID])
        h = sb("h", [P, 2, HID])
        ps_mod = [ctx.enter_context(nc.psum_tensor(f"ps_mod{i}", [P, HID], F32)) for i in range(2)]
        ps_t = [ctx.enter_context(nc.psum_tensor(f"ps_t{i}", [P, HID], F32)) for i in range(2)]

        c_loaded, wm_loaded, ident_ready = sem("c_loaded"), sem("wm_loaded"), sem("a_ident_ready")
        silu_ready, ones_ready, rep_ready = sem("silu_ready"), sem("ones_ready"), sem("rep_ready")
        mod_done, mod_copied, gate_step, gates_ready = sem("mod_done"), sem("mod_copied"), sem("gate_step"), sem("gates_ready")
        mods_stored, dve_begun, sp_begun = sem("mods_stored"), sem("a_dve_begun"), sem("a_sp_begun")
        x_loaded = [sem(f"x_loaded{i}") for i in range(2)]
        stats_done, mv_done, std_done, rstd_done = sem("stats_done"), sem("mv_done"), sem("std_done"), sem("rstd_done")
        xn_done, scaled_done, h_done = sem("xn_done"), sem("scaled_done"), sem("h_done")
        t_done, hi_done, lo_done = sem("t_done"), sem("hi_done"), sem("lo_done")

        with nc.Block() as block:
            @block.sync
            def _(sp):
                sp.dma_start(c_sb[:, :], c_cols).then_inc(c_loaded, 16)
                for i in range(2):
                    sp.dma_start(xt[:, i, :], x[i]).then_inc(x_loaded[i], 16)
                sp.dma_start(wm[:, :, :], wmod.rearrange("(c p) n -> p c n", p=P)).then_inc(wm_loaded, 16)
                with sp.Fori(1, NT // 2) as n:
                    for i in range(2):
                        used = sp.snap(n * 2 + (i - 1))
                        tile = sp.snap(n * 2 + i)
                        sp.wait_ge(xn_done, used)
                        settle(sp, sp_begun)
                        sp.dma_start(xt[:, i, :], x[bass.ds(tile, 1)].rearrange("a p n -> p (a n)")).then_inc(x_loaded[i], 16)
                sp.wait_ge(gates_ready, 4)
                sp.dma_start(mods_dram.rearrange("i p n -> p i n"), mods[:, :, :]).then_inc(mods_stored, 16)
                sp.wait_ge(mods_stored, 16)

            @block.gpsimd
            def _(pool):
                make_identity(pool, ident, ident_ready)

            @block.scalar
            def _(act):
                act.wait_ge(c_loaded, 16)
                nc.scalar.activation(silu_c[:, :], c_sb[:, :], ACT.Silu).then_inc(silu_ready, 1)
                for j in range(6):
                    act.wait_ge(mod_done, j + 1)
                    nc.scalar.activation(mods[:, j, :], ps_mod[j % 2][:, :], ACT.Copy).then_inc(mod_copied, 1)
                with act.Fori(0, NT // 2) as n:
                    for i in range(2):
                        act.wait_ge(mv_done, n * 2 + (i + 1))
                        nc.scalar.activation(std[:, i:i + 1], mv[:, i, 1:2], ACT.Sqrt).then_inc(std_done, 1)
                    for i in range(2):
                        act.wait_ge(t_done, n * 2 + (i + 1))
                        act.wait_ge(ident_ready, 2)
                        nc.scalar.activation(hT_hi[:, :, bass.ds((n * 2 + i) * P, P)],
                                             ps_t[i][:, :].rearrange("p (c t) -> p c t", c=HC), ACT.Copy).then_inc(hi_done, 1)

            @block.tensor
            def _(pe):
                pe.wait_ge(rep_ready, HC)
                pe.wait_ge(wm_loaded, 16)
                for j in range(6):
                    if j >= 2:
                        pe.wait_ge(mod_copied, j - 1)
                    for c in range(HC):
                        last = nc.tensor.matmul(ps_mod[j % 2][:, :], silu_rep[:, c, :], wm[:, c, j * HID:(j + 1) * HID],
                                                start=(c == 0), stop=(c == HC - 1))
                    last.then_inc(mod_done, 1)
                pe.wait_ge(ident_ready, 2)
                with pe.Fori(0, NT // 2) as n:
                    for i in range(2):
                        pe.wait_ge(h_done, n * 2 + (i + 1))
                        pe.wait_ge(lo_done, n * 2 + (i + 1))
                        for c in range(HC):
                            last = nc.tensor.transpose(ps_t[i][:, c * P:(c + 1) * P], h[:, i, c * P:(c + 1) * P], ident[:, :])
                        last.then_inc(t_done, 1)

            @block.vector
            def _(dve):
                dve.sem_inc(lo_done, 2)
                nc.vector.memset(ones[:, :], 1.0).then_inc(ones_ready, 1)
                dve.wait_ge(ones_ready, 1)
                dve.wait_ge(silu_ready, 1)
                for c in range(HC):
                    nc.vector.tensor_scalar(silu_rep[:, c, :], ones[:, :], silu_c[:, c:c + 1], None, ALU.mult).then_inc(rep_ready, 1)
                dve.wait_ge(mod_copied, 6)
                for k, j in enumerate((1, 4)):
                    nc.vector.tensor_scalar(mods[:, j, :], mods[:, j, :], 1.0, None, ALU.add).then_inc(gates_ready, 1)
                for k, j in enumerate((2, 5)):
                    nc.vector.tensor_scalar(sign[:, k, :], mods[:, j, :], 0.0, 2.0, ALU.is_ge, ALU.mult).then_inc(gate_step, 1)
                    nc.vector.scalar_tensor_tensor(mag[:, k, :], mods[:, j, :], -1.0, mods[:, j, :], ALU.mult, ALU.max).then_inc(gate_step, 1)
                    dve.wait_ge(gate_step, 3 * k + 2)
                    nc.vector.tensor_scalar(mag[:, k, :], mag[:, k, :], GATE_MIN, None, ALU.max).then_inc(gate_step, 1)
                    dve.wait_ge(gate_step, 3 * k + 3)
                    nc.vector.scalar_tensor_tensor(mods[:, j, :], sign[:, k, :], -1.0, mag[:, k, :], ALU.add, ALU.mult).then_inc(gates_ready, 1)
                dve.wait_ge(gates_ready, 4)
                with dve.Fori(0, NT // 2) as n:
                    for i in range(2):
                        dve.wait_ge(x_loaded[i], n * 16 + 16)
                        nc.vector.bn_stats(stats[:, i, :], xt[:, i, :]).then_inc(stats_done, 1)
                        dve.wait_ge(stats_done, n * 4 + (2 * i + 1))
                        settle(dve, dve_begun)
                        nc.vector.bn_aggr(mv[:, i, :], stats[:, i, :]).then_inc(stats_done, 1)
                        dve.wait_ge(stats_done, n * 4 + (2 * i + 2))
                        nc.vector.tensor_scalar(mv[:, i, 1:2], mv[:, i, 1:2], EPS, None, ALU.add).then_inc(mv_done, 1)
                    for i in range(2):
                        dve.wait_ge(std_done, n * 2 + (i + 1))
                        nc.vector.reciprocal(rstd[:, i:i + 1], std[:, i:i + 1]).then_inc(rstd_done, 1)
                        dve.wait_ge(rstd_done, n * 2 + (i + 1))
                        nc.vector.tensor_scalar(xn[:, i, :], xt[:, i, :], mv[:, i, 0:1], rstd[:, i:i + 1], ALU.subtract, ALU.mult).then_inc(xn_done, 1)
                        dve.wait_ge(xn_done, n * 2 + (i + 1))
                        nc.vector.tensor_tensor(scaled[:, i, :], xn[:, i, :], mods[:, 1, :], ALU.mult).then_inc(scaled_done, 1)
                        dve.wait_ge(scaled_done, n * 2 + (i + 1))
                        nc.vector.tensor_tensor(h[:, i, :], scaled[:, i, :], mods[:, 0, :], ALU.add).then_inc(h_done, 1)
                    for i in range(2):
                        dve.wait_ge(hi_done, n * 2 + (i + 1))
                        cols = bass.ds((n * 2 + i) * P, P)
                        nc.vector.tensor_tensor(hT_lo[:, :, cols], ps_t[i][:, :].rearrange("p (c t) -> p c t", c=HC),
                                                f32(hT_hi[:, :, cols]), ALU.subtract).then_inc(lo_done, 1)


def stage_b(nc, wq, wk, wv, rope, masks, aT_dram, hT_hi, hT_lo):
    with ExitStack() as ctx:
        def sb(name, shape, dt=F32):
            return ctx.enter_context(nc.sbuf_tensor(name, shape, dt))

        def sem(name):
            return ctx.enter_context(nc.semaphore(name))

        def bank(name):
            return ctx.enter_context(nc.psum_tensor(name, [P, 512], F32))

        ident = sb("b_ident", [P, P])
        cs = sb("cs", [P, 2, TOK])
        mask = sb("mask_sb", [P, 512 + P])
        w_raw = sb("w_raw", [P, 3, HC, P])
        w_hi = sb("w_hi", [P, 3, HC, P], F32R)
        w_lo = sb("w_lo", [P, 3, HC, P], F32R)
        raw = sb("raw", [P, 3, UT])
        rot = sb("rot", [P, 2, UT])
        rsum = sb("rsum", [P, 2, UT])
        r_hi = sb("r_hi", [P, 2, UT], F32R)
        r_lo = sb("r_lo", [P, 2, UT], F32R)
        q_dup = sb("q_dup", [P, 2, 2, 2, UT], F32R)
        k_stack = sb("k_stack", [P, 2, TOK], F32R)
        v_tok = sb("v_tok", [P, NT, 2, 2 * D], F32R)
        prob = sb("prob", [P, 2, TOK])
        pt_hi = sb("pt_hi", [P, 3, 512], F32R)
        pt_lo = sb("pt_lo", [P, 3, 512], F32R)
        half = sb("half", [P, BLOCK])
        a_out = sb("a_out", [P, 2, UT])
        negmax = sb("negmax", [P, 8])
        den = sb("den", [P, 8])
        rden = sb("rden", [P, 8])
        ps_proj = [bank(f"ps_proj{i}") for i in range(2)]
        ps_s = [bank(f"ps_s{i}") for i in range(2)]
        ps_p = [bank(f"ps_p{i}") for i in range(2)]
        ps_o = bank("ps_o")
        ps_v = bank("ps_v")
        prob8 = prob[:, :, :].rearrange("p a n -> p (a n)")

        def job_prob(j):
            return prob8[:, j * 384:(j + 1) * 384]

        tables_loaded, ident_ready, zeros_ready = sem("tables_loaded"), sem("b_ident_ready"), sem("zeros_ready")
        w_loaded, w_hi_done, w_split = sem("w_loaded"), sem("w_hi_done"), sem("w_split")
        proj_done, raw_done = sem("proj_done"), sem("raw_done")
        rot_done = [sem("rot_q_done"), sem("rot_k_done")]
        mults_done, sum_done, rhi_done, rlo_done = sem("rope_mults_done"), sem("rope_sum_done"), sem("rope_hi_done"), sem("rope_lo_done")
        stacked = [sem("q_stacked"), sem("k_stacked")]
        vt_done, vhi_done, vlo_done = sem("vt_done"), sem("vhi_done"), sem("vlo_done")
        scores_done, max_done, exp_done = sem("scores_done"), sem("max_done"), sem("exp_done")
        rden_done, prob_done = sem("rden_done"), sem("prob_done")
        pt_done, pthi_done, ptlo_done = sem("pt_done"), sem("pthi_done"), sem("ptlo_done")
        pv_done, half_done, a_done, a_stored = sem("pv_done"), sem("half_done"), sem("a_done"), sem("a_stored")
        dve_begun, pool_begun, sp_begun = sem("b_dve_begun"), sem("b_pool_begun"), sem("b_sp_begun")
        g_scores_done, g_max_done, g_min_done, g_exp_done = sem("g_scores_done"), sem("g_max_done"), sem("g_min_done"), sem("g_exp_done")
        g_rden_done, g_prob_done = sem("g_rden_done"), sem("g_prob_done")
        g_pt_done, g_pthi_done, g_ptlo_done = sem("g_pt_done"), sem("g_pthi_done"), sem("g_ptlo_done")
        g_pv_done, g_half_done, g_a_done, g_a_stored = sem("g_pv_done"), sem("g_half_done"), sem("g_a_done"), sem("g_a_stored")

        def at(unit, per, count):
            p, t = unit
            return p * (UNITS * per) + (t * per + count)

        def following(unit):
            p, t = unit
            return (p, t + 1) if t + 1 < UNITS else (p + 1, 0)

        def job(j):
            return j // 4, j % 2, j % 4 // 2

        def first_tile(t, b):
            return 1 if (t == 0 and b == 0) else 0

        def job_cols(t, j):
            b, _, qt = job(j)
            return first_tile(t, b) * P, (2 + qt) * P

        G = [(m, hd) for m in range(TOK // BLOCK) for hd in range(2)]

        def g_chunks(m, qt):
            n = (2 * m + 1 + qt) * P
            return [(s, min(512, n - s), s + 512 >= n) for s in range(0, n, 512)]

        def g_counts(g):
            s = sum(len(g_chunks(m, 0)) + len(g_chunks(m, 1)) for m, _ in G[:g])
            f = sum(m + 1 for m, _ in G[:g])
            return s, f

        with nc.Block() as block:
            @block.sync
            def _(sp):
                def load_weights(p_ap, value=None):
                    if value is not None:
                        sp.wait_ge(w_split, value)
                        settle(sp, sp_begun)
                    for i, w in enumerate((wq, wk, wv)):
                        sp.dma_start(w_raw[:, i, :, :], w[p_ap].rearrange("a p c n -> p (a c) n")).then_inc(w_loaded, 16)

                def rotate(unit, i, first=False):
                    ready = sp.snap(at(unit, 3, i + 1)) if not first else i + 1
                    free = None if first else sp.snap(at(unit, 2, 0))
                    if not first:
                        sp.wait_ge(sum_done, free)
                        settle(sp, sp_begun)
                    sp.wait_ge(raw_done, ready)
                    for s in range(4):
                        d = s ^ 1
                        sp.dma_start(rot[32 * d:32 * d + 32, i, :], raw[32 * s:32 * s + 32, i, :]).then_inc(rot_done[i], 16)

                def stack(unit, i, first=False):
                    t = unit[1]
                    ready = sp.snap(at(unit, 2, i + 1)) if not first else i + 1
                    sp.wait_ge(rlo_done, ready)
                    for hd in range(2):
                        rows = slice(D * hd, D * hd + D)
                        for s, split in enumerate((r_hi, r_lo)):
                            if i == 1:
                                sp.dma_start(f32(k_stack[D * s:D * s + D, hd, t * UT:(t + 1) * UT]),
                                             f32(split[rows, 1, :])).then_inc(stacked[1], 16)
                            else:
                                for up in range(2):
                                    sp.dma_start(f32(q_dup[D * up:D * up + D, t % 2, hd, s, :]),
                                                 f32(split[rows, 0, :])).then_inc(stacked[0], 16)

                def store(unit, pair):
                    t = unit[1]
                    ready = sp.snap(at(unit, 4, 4 + 2))
                    sp.wait_ge(a_done, ready)
                    settle(sp, sp_begun)
                    sp.dma_start(aT_dram[t * 4:t * 4 + 4, :, pair, :].rearrange("k p a n -> p k (a n)"),
                                 a_out[:, t % 2, :].rearrange("p (k n) -> p k n", n=P)).then_inc(a_stored, 16)

                sp.sem_inc(a_stored, 32)
                sp.dma_start(w_raw[:, 0, :, :], wq[0]).then_inc(w_loaded, 16)
                sp.dma_start(w_raw[:, 1, :, :], wk[0]).then_inc(w_loaded, 16)
                sp.dma_start(w_raw[:, 2, :, :], wv[0]).then_inc(w_loaded, 16)
                sp.dma_start(cs[:, :, :], rope.rearrange("i p n -> p i n")).then_inc(tables_loaded, 16)
                sp.dma_start(mask[:, :], masks).then_inc(tables_loaded, 16)
                for i in range(2):
                    rotate((0, 0), i, first=True)
                for i in range(2):
                    stack((0, 0), i, first=True)
                with sp.Fori(0, LOCAL_PAIRS) as p:
                    for t in range(UNITS):
                        unit = (p, t)
                        nxt = following(unit)
                        pair = sp.snap(p)
                        if t == 0:
                            value = sp.snap(p * 3 + 3)
                            load_weights(bass.ds(sp.snap(p + 1), 1), value)
                        rotate(nxt, 0)
                        rotate(nxt, 1)
                        stack(nxt, 0)
                        stack(nxt, 1)
                        store(unit, bass.ds(pair, 1))
                for t in range(UNITS):
                    if t + 1 < UNITS:
                        nxt = (LOCAL_PAIRS, t + 1)
                        for i in range(2):
                            sp.wait_ge(sum_done, at(nxt, 2, 0))
                            sp.wait_ge(raw_done, at(nxt, 3, i + 1))
                            for s in range(4):
                                d = s ^ 1
                                sp.dma_start(rot[32 * d:32 * d + 32, i, :], raw[32 * s:32 * s + 32, i, :]).then_inc(rot_done[i], 16)
                        for i in range(2):
                            sp.wait_ge(rlo_done, at(nxt, 2, i + 1))
                            tn = t + 1
                            for hd in range(2):
                                rows = slice(D * hd, D * hd + D)
                                for s, split in enumerate((r_hi, r_lo)):
                                    if i == 1:
                                        sp.dma_start(f32(k_stack[D * s:D * s + D, hd, tn * UT:(tn + 1) * UT]),
                                                     f32(split[rows, 1, :])).then_inc(stacked[1], 16)
                                    else:
                                        for up in range(2):
                                            sp.dma_start(f32(q_dup[D * up:D * up + D, tn % 2, hd, s, :]),
                                                         f32(split[rows, 0, :])).then_inc(stacked[0], 16)
                    sp.wait_ge(g_a_done, 4 * (t + 1))
                    sp.dma_start(aT_dram[t * 4:t * 4 + 4, :, LOCAL_PAIRS, :].rearrange("k p n -> p k n"),
                                 a_out[:, t % 2, :].rearrange("p (k n) -> p k n", n=P)).then_inc(g_a_stored, 16)
                sp.wait_ge(a_stored, 16 * (LOCAL_PAIRS * UNITS) + 32)
                sp.wait_ge(g_a_stored, 16 * UNITS)

            @block.gpsimd
            def _(pool):
                def split_weights(p, m, first=False):
                    if not first:
                        pool.wait_ge(proj_done, (p - 1) * (3 * UNITS) + (3 * (UNITS - 1) + m + 1))
                    pool.wait_ge(w_loaded, p * 48 + 48)
                    settle(pool, pool_begun)
                    nc.gpsimd.tensor_copy(w_hi[:, m, :, :], w_raw[:, m, :, :]).then_inc(w_hi_done, 1)
                    pool.wait_ge(w_hi_done, p * 3 + (m + 1))
                    nc.gpsimd.tensor_tensor(w_lo[:, m, :, :], w_raw[:, m, :, :], f32(w_hi[:, m, :, :]), ALU.subtract).then_inc(w_split, 1)

                def rope_mults(unit, i, first=False):
                    cols = slice(unit[1] * UT, (unit[1] + 1) * UT)
                    if not first:
                        pool.wait_ge(rlo_done, at(unit, 2, 0))
                    pool.wait_ge(raw_done, at(unit, 3, i + 1))
                    nc.gpsimd.tensor_tensor(rsum[:, i, :], raw[:, i, :], cs[:, 0, cols], ALU.mult).then_inc(mults_done, 1)
                    pool.wait_ge(rot_done[i], at(unit, 64, 64))
                    nc.gpsimd.tensor_tensor(rot[:, i, :], rot[:, i, :], cs[:, 1, cols], ALU.mult).then_inc(mults_done, 1)

                def normalize(unit, b):
                    t = unit[1]
                    pool.wait_ge(rden_done, at(unit, 2, b + 1))
                    settle(pool, pool_begun)
                    for j in range(4 * b, 4 * b + 4):
                        lo, hi = job_cols(t, j)
                        row = job_prob(j)[:, lo:hi]
                        nc.gpsimd.tensor_scalar(row, row, rden[:, j:j + 1], 1.0, ALU.mult, ALU.mult).then_inc(prob_done, 1)

                make_identity(pool, ident, ident_ready)
                nc.gpsimd.memset(f32(pt_hi[:, 2, :]), 0.0).then_inc(zeros_ready, 1)
                nc.gpsimd.memset(f32(pt_lo[:, 2, :]), 0.0).then_inc(zeros_ready, 1)
                for m in range(3):
                    split_weights(0, m, first=True)
                pool.wait_ge(tables_loaded, 32)
                for i in range(2):
                    rope_mults((0, 0), i, first=True)
                with pool.Fori(0, LOCAL_PAIRS) as p:
                    for t in range(UNITS):
                        unit = (p, t)
                        nxt = following(unit)
                        if t == 2:
                            split_weights(p + 1, 0)
                        rope_mults(nxt, 0)
                        normalize(unit, 0)
                        if t == 2:
                            split_weights(p + 1, 1)
                        rope_mults(nxt, 1)
                        normalize(unit, 1)
                        if t == 2:
                            split_weights(p + 1, 2)
                for g, (m, hd) in enumerate(G):
                    t = m // 2
                    if m % 2 == 0 and t + 1 < UNITS:
                        rope_mults((LOCAL_PAIRS, t + 1), hd)
                    pool.wait_ge(g_rden_done, g + 1)
                    for qt in range(2):
                        row = prob[:, qt, 0:(2 * m + 1 + qt) * P]
                        nc.gpsimd.tensor_scalar(row, row, rden[:, qt:qt + 1], 1.0, ALU.mult, ALU.mult).then_inc(g_prob_done, 1)

            @block.scalar
            def _(act):
                def copy_raw(unit, m, first=False):
                    act.wait_ge(proj_done, at(unit, 3, m + 1))
                    if not first and m < 2:
                        act.wait_ge(rot_done[m], at(unit, 64, 0))
                        act.wait_ge(mults_done, at(unit, 4, 0))
                    if not first and m == 2:
                        act.wait_ge(vt_done, at(unit, 1, 0))
                    n = (3 * unit[1] + m) % 2
                    nc.scalar.activation(raw[:, m, :], ps_proj[n][:, :], ACT.Copy).then_inc(raw_done, 1)

                def v_hi(unit):
                    t = unit[1]
                    act.wait_ge(vt_done, at(unit, 1, 1))
                    nc.scalar.activation(v_tok[:, 4 * t:4 * t + 4, :, 0:D],
                                         ps_v[:, :].rearrange("p (k h d) -> p k h d", k=4, h=2), ACT.Copy).then_inc(vhi_done, 1)

                def exp(unit, j):
                    lo, hi = job_cols(unit[1], j)
                    row = job_prob(j)[:, lo:hi]
                    act.wait_ge(max_done, at(unit, 8, j + 1 + 2))
                    nc.scalar.activation(row, row, ACT.Exp, bias=negmax[:, j:j + 1], scale=-1.0,
                                         accum_out=den[:, j:j + 1]).then_inc(exp_done, 1)

                def p_hi(unit, b):
                    t = unit[1]
                    act.wait_ge(pv_done, at(unit, 2, b + 1))
                    for f in range(3):
                        act.wait_ge(pt_done, at(unit, 6, 3 * b + f + 1 + 6))
                        n = (3 * b + f) % 2
                        if f < 2:
                            lo = first_tile(t, b) * BLOCK
                            nc.scalar.activation(pt_hi[:, f, lo:512], ps_p[n][:, lo:512], ACT.Copy).then_inc(pthi_done, 1)
                        else:
                            nc.scalar.activation(pt_hi[:, 2, :].rearrange("p (h q) -> p h q", h=2)[:, :, P:BLOCK],
                                                 ps_p[n][:, 0:BLOCK].rearrange("p (h q) -> p h q", h=2), ACT.Copy).then_inc(pthi_done, 1)

                def halves(unit, b):
                    act.wait_ge(a_done, at(unit, 4, 2 * b + 2))
                    act.wait_ge(pv_done, at(unit, 2, b + 2))
                    nc.scalar.activation(half[0:D, :], ps_o[D:P, 0:BLOCK], ACT.Copy).then_inc(half_done, 1)
                    nc.scalar.activation(half[D:P, :], ps_o[0:D, BLOCK:2 * BLOCK], ACT.Copy).then_inc(half_done, 1)

                for m in range(3):
                    copy_raw((0, 0), m, first=True)
                v_hi((0, 0))
                with act.Fori(0, LOCAL_PAIRS) as p:
                    for t in range(UNITS):
                        unit = (p, t)
                        nxt = following(unit)
                        exp(unit, 0)
                        exp(unit, 1)
                        copy_raw(nxt, 0)
                        exp(unit, 2)
                        exp(unit, 3)
                        copy_raw(nxt, 1)
                        exp(unit, 4)
                        exp(unit, 5)
                        p_hi(unit, 0)
                        exp(unit, 6)
                        exp(unit, 7)
                        copy_raw(nxt, 2)
                        halves(unit, 0)
                        p_hi(unit, 1)
                        v_hi(nxt)
                        halves(unit, 1)
                for g, (m, hd) in enumerate(G):
                    t = m // 2
                    for qt in range(2):
                        row = prob[:, qt, 0:(2 * m + 1 + qt) * P]
                        act.wait_ge(g_min_done, 2 * g + qt + 1)
                        nc.scalar.activation(row, row, ACT.Exp, bias=negmax[:, qt:qt + 1], scale=-1.0,
                                             accum_out=den[:, qt:qt + 1]).then_inc(g_exp_done, 1)
                    if t + 1 < UNITS:
                        step = 2 * (m % 2) + hd
                        if step < 3:
                            copy_raw((LOCAL_PAIRS, t + 1), step)
                        else:
                            v_hi((LOCAL_PAIRS, t + 1))
                    f0 = g_counts(g)[1]
                    for f in range(m + 1):
                        act.wait_ge(g_pt_done, f0 + f + 1)
                        src = ps_p[(f0 + f) % 2]
                        if f < m:
                            if f >= 2:
                                act.wait_ge(g_pv_done, f0 + f - 1)
                            nc.scalar.activation(pt_hi[:, f % 2, :], src[:, :], ACT.Copy).then_inc(g_pthi_done, 1)
                        else:
                            if f >= 2:
                                act.wait_ge(g_pv_done, f0 + f - 1)
                            nc.scalar.activation(pt_hi[:, f % 2, 0:BLOCK], src[:, 0:BLOCK], ACT.Copy)
                            nc.scalar.activation(pt_hi[:, 2, P:BLOCK], src[:, BLOCK:BLOCK + P], ACT.Copy).then_inc(g_pthi_done, 1)
                    act.wait_ge(g_pv_done, f0 + m + 1)
                    if hd == 0:
                        nc.scalar.activation(half[0:D, :], ps_o[D:P, 0:BLOCK], ACT.Copy).then_inc(g_half_done, 1)
                    else:
                        nc.scalar.activation(half[D:P, :], ps_o[0:D, BLOCK:2 * BLOCK], ACT.Copy).then_inc(g_half_done, 1)

            @block.tensor
            def _(pe):
                def project(unit, m, first=False):
                    n = (3 * unit[1] + m) % 2
                    cols = slice(unit[1] * UT, (unit[1] + 1) * UT)
                    if not first:
                        pe.wait_ge(raw_done, at(unit, 3, m - 1))
                    elif m == 2:
                        pe.wait_ge(raw_done, 1)
                    pe.wait_ge(w_split, unit[0] * 3 + (m + 1))
                    k = 0
                    for w, h in ((w_hi, hT_hi), (w_hi, hT_lo), (w_lo, hT_hi)):
                        for c in range(HC):
                            last = nc.tensor.matmul(ps_proj[n][:, :], w[:, m, c, :], h[:, c, cols], start=(k == 0), stop=(k == 3 * HC - 1))
                            k += 1
                    last.then_inc(proj_done, 1)

                def transpose_v(unit, first=False):
                    if not first:
                        pe.wait_ge(vlo_done, at(unit, 1, 0))
                    pe.wait_ge(raw_done, at(unit, 3, 3))
                    for k in range(4):
                        last = nc.tensor.transpose(ps_v[:, k * P:(k + 1) * P], raw[:, 2, k * P:(k + 1) * P], ident[:, :])
                    last.then_inc(vt_done, 1)

                def scores(unit, j):
                    t = unit[1]
                    b, hd, qt = job(j)
                    lo, hi = job_cols(t, j)
                    if j == 0:
                        pe.wait_ge(stacked[0], at(unit, 128, 128))
                        pe.wait_ge(stacked[1], at(unit, 64, 64))
                    pe.wait_ge(max_done, at(unit, 8, j + 1))
                    q0 = b * BLOCK + qt * P
                    k0 = t * UT + b * BLOCK - LOOKBACK
                    for s in range(2):
                        last = nc.tensor.matmul(ps_s[j % 2][:, lo:hi], q_dup[:, t % 2, hd, s, q0:q0 + P],
                                                k_stack[:, hd, k0 + lo:k0 + hi], start=(s == 0), stop=(s == 1))
                    last.then_inc(scores_done, 1)

                def transpose_p(unit, b):
                    t = unit[1]
                    pe.wait_ge(prob_done, at(unit, 8, 4 * b + 4))
                    for f in range(3):
                        pe.wait_ge(ptlo_done, at(unit, 6, 3 * b + f + 1))
                        dst = ps_p[(3 * b + f) % 2]
                        if f < 2:
                            for c in range(first_tile(t, b), 2):
                                for qt in range(2):
                                    last = nc.tensor.transpose(dst[:, c * BLOCK + qt * P:c * BLOCK + (qt + 1) * P],
                                                               job_prob(4 * b + 2 * qt + f)[:, c * P:(c + 1) * P], ident[:, :])
                        else:
                            for hd in range(2):
                                last = nc.tensor.transpose(dst[:, hd * P:(hd + 1) * P], job_prob(4 * b + 2 + hd)[:, 2 * P:3 * P], ident[:, :])
                        last.then_inc(pt_done, 1)

                def weighted_values(unit, b):
                    t = unit[1]
                    pe.wait_ge(vlo_done, at(unit, 1, 1))
                    pe.wait_ge(a_done, at(unit, 4, 2 * b + 2))
                    pe.wait_ge(ptlo_done, at(unit, 6, 3 * b + 3 + 2))
                    for hd in range(2):
                        group = [(c, pt) for c in range(first_tile(t, b), 3) for pt in (pt_hi, pt_lo)]
                        for n, (c, pt) in enumerate(group):
                            moving = pt[:, hd, c * BLOCK:(c + 1) * BLOCK] if c < 2 else pt[:, 2, hd * BLOCK:(hd + 1) * BLOCK]
                            last = nc.tensor.matmul(ps_o[:, hd * BLOCK:(hd + 1) * BLOCK], v_tok[:, 4 * t + 2 * b - 1 + c, hd, :], moving,
                                                    start=(n == 0), stop=(n == len(group) - 1))
                    last.then_inc(pv_done, 1)

                pe.sem_inc(pt_done, 6)
                pe.sem_inc(pv_done, 1)
                pe.wait_ge(ident_ready, 2)
                for m in range(3):
                    project((0, 0), m, first=True)
                transpose_v((0, 0), first=True)
                with pe.Fori(0, LOCAL_PAIRS) as p:
                    for t in range(UNITS):
                        unit = (p, t)
                        nxt = following(unit)
                        scores(unit, 0)
                        scores(unit, 1)
                        project(nxt, 0)
                        scores(unit, 2)
                        scores(unit, 3)
                        project(nxt, 1)
                        scores(unit, 4)
                        scores(unit, 5)
                        transpose_p(unit, 0)
                        scores(unit, 6)
                        scores(unit, 7)
                        project(nxt, 2)
                        weighted_values(unit, 0)
                        transpose_p(unit, 1)
                        transpose_v(nxt)
                        weighted_values(unit, 1)
                for g, (m, hd) in enumerate(G):
                    t = m // 2
                    s0, f0 = g_counts(g)
                    if g % 4 == 0:
                        pe.wait_ge(stacked[0], at((LOCAL_PAIRS, t), 128, 128))
                        pe.wait_ge(stacked[1], at((LOCAL_PAIRS, t), 64, 64))
                        pe.wait_ge(vlo_done, at((LOCAL_PAIRS, t), 1, 1))
                    n = s0
                    for qt in range(2):
                        q0 = (m % 2) * BLOCK + qt * P
                        for start, width, _ in g_chunks(m, qt):
                            if n >= 2:
                                pe.wait_ge(g_max_done, n - 1)
                            for s in range(2):
                                last = nc.tensor.matmul(ps_s[n % 2][:, 0:width], q_dup[:, t % 2, hd, s, q0:q0 + P],
                                                        k_stack[:, hd, start:start + width], start=(s == 0), stop=(s == 1))
                            last.then_inc(g_scores_done, 1)
                            n += 1
                    if t + 1 < UNITS:
                        step = 2 * (m % 2) + hd
                        if step < 3:
                            project((LOCAL_PAIRS, t + 1), step)
                        else:
                            transpose_v((LOCAL_PAIRS, t + 1))
                    pe.wait_ge(g_prob_done, 2 * g + 2)

                    def transpose_bank(f):
                        if f0 + f >= 2:
                            pe.wait_ge(g_ptlo_done, f0 + f - 1)
                        dst = ps_p[(f0 + f) % 2]
                        cols = [(0, 0, 0), (0, 1, P), (1, 0, 2 * P), (1, 1, 3 * P)] if f < m else [(0, 0, 0), (0, 1, P), (1, 1, 2 * P)]
                        for c, qt, col in cols:
                            tr = nc.tensor.transpose(dst[:, col:col + P], prob[:, qt, (2 * f + c) * P:(2 * f + c + 1) * P], ident[:, :])
                        tr.then_inc(g_pt_done, 1)

                    transpose_bank(0)
                    for f in range(m + 1):
                        if f < m:
                            transpose_bank(f + 1)
                        if f == 0 and g >= 1:
                            pe.wait_ge(g_a_done, g)
                        pe.wait_ge(g_ptlo_done, f0 + f + 1)
                        for c in range(2):
                            for pt in (pt_hi, pt_lo):
                                moving = pt[:, 2, 0:BLOCK] if (f == m and c == 1) else pt[:, f % 2, c * BLOCK:(c + 1) * BLOCK]
                                last = nc.tensor.matmul(ps_o[:, hd * BLOCK:(hd + 1) * BLOCK], v_tok[:, 2 * f + c, hd, :], moving,
                                                        start=(f == 0 and c == 0 and pt is pt_hi), stop=(f == m and c == 1 and pt is pt_lo))
                        last.then_inc(g_pv_done, 1)

            @block.vector
            def _(dve):
                def row_max(unit, j):
                    lo, hi = job_cols(unit[1], j)
                    if j == 0:
                        dve.wait_ge(pt_done, at(unit, 6, 6))
                    dve.wait_ge(scores_done, at(unit, 8, j + 1))
                    settle(dve, dve_begun)
                    nc.vector.tensor_tensor_reduce(job_prob(j)[:, lo:hi], ps_s[j % 2][:, lo:hi], mask[:, 512 + P - (hi - lo):512 + P],
                                                   NEG_SCALE, 3e38, ALU.add, ALU.min, negmax[:, j:j + 1]).then_inc(max_done, 1)

                def reciprocals(unit, b):
                    dve.wait_ge(exp_done, at(unit, 8, 4 * b + 4))
                    nc.vector.reciprocal(rden[:, 4 * b:4 * b + 4], den[:, 4 * b:4 * b + 4]).then_inc(rden_done, 1)

                def rope_split(unit, i, first=False):
                    dve.wait_ge(mults_done, at(unit, 4, 2 * i + 2))
                    nc.vector.tensor_tensor(rsum[:, i, :], rsum[:, i, :], rot[:, i, :], ALU.add).then_inc(sum_done, 1)
                    if not first:
                        dve.wait_ge(stacked[i], at(unit, 128 if i == 0 else 64, 0))
                    dve.wait_ge(sum_done, at(unit, 2, i + 1))
                    nc.vector.tensor_copy(r_hi[:, i, :], rsum[:, i, :]).then_inc(rhi_done, 1)
                    dve.wait_ge(rhi_done, at(unit, 2, i + 1))
                    nc.vector.tensor_tensor(r_lo[:, i, :], rsum[:, i, :], f32(r_hi[:, i, :]), ALU.subtract).then_inc(rlo_done, 1)

                def v_lo(unit):
                    t = unit[1]
                    dve.wait_ge(vhi_done, at(unit, 1, 1))
                    v = v_tok[:, 4 * t:4 * t + 4, :, :]
                    nc.vector.tensor_tensor(v[:, :, :, D:2 * D], ps_v[:, :].rearrange("p (k h d) -> p k h d", k=4, h=2),
                                            f32(v[:, :, :, 0:D]), ALU.subtract).then_inc(vlo_done, 1)

                def p_lo(unit, b):
                    t = unit[1]
                    for f in range(3):
                        dve.wait_ge(pthi_done, at(unit, 6, 3 * b + f + 1))
                        src = ps_p[(3 * b + f) % 2]
                        if f < 2:
                            lo = first_tile(t, b) * BLOCK
                            nc.vector.tensor_tensor(pt_lo[:, f, lo:512], src[:, lo:512], f32(pt_hi[:, f, lo:512]), ALU.subtract).then_inc(ptlo_done, 1)
                        else:
                            hi = pt_hi[:, 2, :].rearrange("p (h q) -> p h q", h=2)[:, :, P:BLOCK]
                            out = pt_lo[:, 2, :].rearrange("p (h q) -> p h q", h=2)[:, :, P:BLOCK]
                            nc.vector.tensor_tensor(out, src[:, 0:BLOCK].rearrange("p (h q) -> p h q", h=2), f32(hi), ALU.subtract).then_inc(ptlo_done, 1)

                def join(unit, b):
                    t = unit[1]
                    cols = slice(b * BLOCK, (b + 1) * BLOCK)
                    if b == 0:
                        dve.wait_ge(a_stored, at(unit, 16, 16))
                    dve.wait_ge(half_done, at(unit, 4, 2 * b + 2))
                    nc.vector.tensor_tensor(a_out[0:D, t % 2, cols], ps_o[0:D, 0:BLOCK], half[0:D, :], ALU.add).then_inc(a_done, 1)
                    nc.vector.tensor_tensor(a_out[D:P, t % 2, cols], ps_o[D:P, BLOCK:2 * BLOCK], half[D:P, :], ALU.add).then_inc(a_done, 1)

                dve.sem_inc(max_done, 2)
                dve.sem_inc(ptlo_done, 2)
                dve.sem_inc(a_done, 2)
                dve.wait_ge(tables_loaded, 32)
                for i in range(2):
                    rope_split((0, 0), i, first=True)
                v_lo((0, 0))
                with dve.Fori(0, LOCAL_PAIRS) as p:
                    for t in range(UNITS):
                        unit = (p, t)
                        nxt = following(unit)
                        for j in range(4):
                            row_max(unit, j)
                        reciprocals(unit, 0)
                        row_max(unit, 4)
                        row_max(unit, 5)
                        rope_split(nxt, 0)
                        p_lo(unit, 0)
                        row_max(unit, 6)
                        row_max(unit, 7)
                        reciprocals(unit, 1)
                        rope_split(nxt, 1)
                        join(unit, 0)
                        p_lo(unit, 1)
                        v_lo(nxt)
                        join(unit, 1)
                dve.wait_ge(zeros_ready, 2)
                for g, (m, hd) in enumerate(G):
                    t = m // 2
                    s0, f0 = g_counts(g)
                    n = s0
                    if g == 0:
                        dve.wait_ge(pt_done, at((LOCAL_PAIRS, 0), 6, 6))
                    else:
                        dve.wait_ge(g_pt_done, f0)
                    for qt in range(2):
                        chunks = g_chunks(m, qt)
                        for i, (start, width, diagonal) in enumerate(chunks):
                            dve.wait_ge(g_scores_done, n + 1)
                            m0 = 512 + P - width if diagonal else 0
                            nc.vector.tensor_tensor_reduce(prob[:, qt, start:start + width], ps_s[n % 2][:, 0:width], mask[:, m0:m0 + width],
                                                           NEG_SCALE, 3e38, ALU.add, ALU.min, negmax[:, 4 + i:5 + i]).then_inc(g_max_done, 1)
                            n += 1
                        dve.wait_ge(g_max_done, n)
                        nc.vector.tensor_reduce(negmax[:, qt:qt + 1], negmax[:, 4:4 + len(chunks)], AX_X, ALU.min).then_inc(g_min_done, 1)
                        dve.wait_ge(g_min_done, 2 * g + qt + 1)
                    dve.wait_ge(g_exp_done, 2 * g + 2)
                    nc.vector.reciprocal(rden[:, 0:2], den[:, 0:2]).then_inc(g_rden_done, 1)
                    if t + 1 < UNITS:
                        step = 2 * (m % 2) + hd
                        if step in (1, 2):
                            rope_split((LOCAL_PAIRS, t + 1), step - 1)
                        elif step == 3:
                            v_lo((LOCAL_PAIRS, t + 1))
                    for f in range(m + 1):
                        dve.wait_ge(g_pthi_done, f0 + f + 1)
                        src = ps_p[(f0 + f) % 2]
                        if f < m:
                            nc.vector.tensor_tensor(pt_lo[:, f % 2, :], src[:, :], f32(pt_hi[:, f % 2, :]), ALU.subtract).then_inc(g_ptlo_done, 1)
                        else:
                            nc.vector.tensor_tensor(pt_lo[:, f % 2, 0:BLOCK], src[:, 0:BLOCK], f32(pt_hi[:, f % 2, 0:BLOCK]), ALU.subtract)
                            nc.vector.tensor_tensor(pt_lo[:, 2, P:BLOCK], src[:, BLOCK:BLOCK + P], f32(pt_hi[:, 2, P:BLOCK]), ALU.subtract).then_inc(g_ptlo_done, 1)
                    rows = slice(D * hd, D * hd + D)
                    if g % 4 == 0:
                        if t < 2:
                            dve.wait_ge(a_stored, 16 * (LOCAL_PAIRS * UNITS) + 32)
                        else:
                            dve.wait_ge(g_a_stored, 16 * (t - 1))
                    dve.wait_ge(g_half_done, g + 1)
                    nc.vector.tensor_tensor(a_out[rows, t % 2, (m % 2) * BLOCK:(m % 2 + 1) * BLOCK],
                                            ps_o[rows, hd * BLOCK:(hd + 1) * BLOCK], half[rows, :], ALU.add).then_inc(g_a_done, 1)


def stage_c(nc, x, wo, bo_rep, mods_dram, aT_dram, x1, hT_hi, hT_lo):
    with ExitStack() as ctx:
        def sb(name, shape, dt=F32):
            return ctx.enter_context(nc.sbuf_tensor(name, shape, dt))

        def sem(name):
            return ctx.enter_context(nc.semaphore(name))

        RC = 4
        PC = PAIRS // RC
        ident = sb("c_ident", [P, P])
        rows = sb("rows", [P, 3, HID])
        bias = sb("bias", [P, HID])
        WC = 8
        WP = PAIRS // WC
        wo_raw = sb("wo_raw", [P, 2, WP, HID])
        wo_hi = sb("wo_hi", [P, PAIRS, HID], F32R)
        wo_lo = sb("wo_lo", [P, PAIRS, HID], F32R)
        a_raw = sb("a_raw", [P, RC, PC, P])
        a_hi = sb("a_hi", [P, RC, PC, P], F32R)
        a_lo = sb("a_lo", [P, RC, PC, P], F32R)
        stats = sb("c_stats", [P, 2, 6])
        mv = sb("c_mv", [P, 2, 2])
        std = sb("c_std", [P, 2])
        rstd = sb("c_rstd", [P, 2])
        h = sb("c_h", [P, 2, HID])
        ps_y = [ctx.enter_context(nc.psum_tensor(f"ps_y{i}", [P, HID], F32)) for i in range(2)]
        ps_t = [ctx.enter_context(nc.psum_tensor(f"c_ps_t{i}", [P, HID], F32)) for i in range(2)]

        rows_loaded, ident_ready, bias_ready = sem("rows_loaded"), sem("c_ident_ready"), sem("bias_ready")
        wo_loaded = [sem("wo_loaded0"), sem("wo_loaded1")]
        wo_scaled, wo_hi_done, wo_split = sem("wo_scaled"), sem("wo_hi_done"), sem("wo_split")
        a_loaded = [sem(f"a_loaded{r}") for r in range(RC)]
        a_hi_done, a_split = sem("a_hi_done"), sem("a_split")
        x_loaded = sem("c_x_loaded")
        xb_done, y_done, x1_done = sem("xb_done"), sem("y_done"), sem("x1_done")
        stats_done, mv_done, std_done, rstd_done = sem("c_stats_done"), sem("c_mv_done"), sem("c_std_done"), sem("c_rstd_done")
        h_step, h_done = sem("c_h_step"), sem("c_h_done")
        t_done, hi_done, lo_done = sem("c_t_done"), sem("c_hi_done"), sem("c_lo_done")
        dve_begun, pool_begun, sp_begun, act_begun = sem("c_dve_begun"), sem("c_pool_begun"), sem("c_sp_begun"), sem("c_act_begun")

        def tile(n, i):
            return n * 2 + i

        with nc.Block() as block:
            @block.sync
            def _(sp):
                for k, j in enumerate((2, 3, 4)):
                    sp.dma_start(rows[:, k, :], mods_dram[j]).then_inc(rows_loaded, 16)
                sp.dma_start(bias[:, :], bo_rep).then_inc(rows_loaded, 16)
                def load_wo(r):
                    sp.dma_start(wo_raw[:, r % 2, :, :], wo[:, r * WP:(r + 1) * WP, :]).then_inc(wo_loaded[r % 2], 16)

                load_wo(0)
                load_wo(1)
                for r in range(RC):
                    sp.dma_start(a_raw[:, r, :, :], aT_dram[0, :, r * PC:(r + 1) * PC, :]).then_inc(a_loaded[r], 16)
                sp.dma_start(x1[:, :, :], x.rearrange("k p n -> p k n")).then_inc(x_loaded, 16)
                for r in range(2, WC):
                    sp.wait_ge(wo_split, r - 1)
                    load_wo(r)

                def load_next_a(n, i):
                    for r in range(RC):
                        sp.wait_ge(a_split, tile(n, i) * RC + (r + 1))
                        settle(sp, sp_begun)
                        sp.dma_start(a_raw[:, r, :, :], aT_dram[bass.ds(tile(n, i + 1), 1), :, r * PC:(r + 1) * PC, :]
                                     .rearrange("a p c n -> p (a c) n")).then_inc(a_loaded[r], 16)

                with sp.Fori(0, NT // 2 - 1) as n:
                    for i in range(2):
                        load_next_a(n, i)
                load_next_a(NT // 2 - 1, 0)

            @block.gpsimd
            def _(pool):
                make_identity(pool, ident, ident_ready)
                for r in range(WC):
                    pool.wait_ge(wo_hi_done, r + 1)
                    nc.gpsimd.tensor_tensor(wo_lo[:, r * WP:(r + 1) * WP, :], wo_raw[:, r % 2, :, :], f32(wo_hi[:, r * WP:(r + 1) * WP, :]),
                                            ALU.subtract).then_inc(wo_split, 1)
                pool.wait_ge(bias_ready, 1)
                pool.wait_ge(x_loaded, 16)

                def base(n, i):
                    for r in range(RC):
                        pool.wait_ge(a_hi_done, tile(n, i) * RC + (r + 1))
                        nc.gpsimd.tensor_tensor(a_lo[:, r, :, :], a_raw[:, r, :, :], f32(a_hi[:, r, :, :]), ALU.subtract).then_inc(a_split, 1)
                    row = x1[:, bass.ds(tile(n, i), 1), :].rearrange("p a n -> p (a n)")
                    nc.gpsimd.tensor_tensor(row, row, bias[:, :], ALU.add).then_inc(xb_done, 1)

                with pool.Fori(0, NT // 2) as n:
                    for i in range(2):
                        base(n, i)

            @block.scalar
            def _(act):
                for r in range(WC):
                    act.wait_ge(wo_scaled, r + 1)
                    nc.scalar.activation(wo_hi[:, r * WP:(r + 1) * WP, :], wo_raw[:, r % 2, :, :], ACT.Copy).then_inc(wo_hi_done, 1)

                def split(n, i, r):
                    act.wait_ge(y_done, tile(n, i) + 1)
                    act.wait_ge(a_loaded[r], tile(n, i) * 16 + 16)
                    nc.scalar.activation(a_hi[:, r, :, :], a_raw[:, r, :, :], ACT.Copy).then_inc(a_hi_done, 1)

                def norm(n, i):
                    act.wait_ge(mv_done, tile(n, i) + 1)
                    nc.scalar.activation(std[:, i:i + 1], mv[:, i, 1:2], ACT.Sqrt).then_inc(std_done, 1)
                    act.wait_ge(t_done, tile(n, i) + 1)
                    settle(act, act_begun)
                    nc.scalar.activation(hT_hi[:, :, bass.ds(tile(n, i) * P, P)],
                                         ps_t[i][:, :].rearrange("p (c t) -> p c t", c=HC), ACT.Copy).then_inc(hi_done, 1)

                for r in range(RC):
                    split(0, 0, r)
                with act.Fori(0, NT // 2 - 1) as n:
                    for i in range(2):
                        for r in range(RC):
                            split(n, i + 1, r)
                        norm(n, i)
                for r in range(RC):
                    split(NT // 2 - 1, 1, r)
                norm(NT // 2 - 1, 0)
                norm(NT // 2 - 1, 1)

            @block.tensor
            def _(pe):
                def product(n, i, first=False):
                    pe.wait_ge(x1_done, tile(n, i) + 1)
                    bank = ps_y[i % 2]
                    for r in range(RC):
                        if first:
                            pe.wait_ge(wo_split, (r + 1) * WC // RC)
                        pe.wait_ge(a_split, tile(n, i) * RC + (r + 1))
                        for a, w in ((a_hi, wo_hi), (a_hi, wo_lo), (a_lo, wo_hi)):
                            for c in range(PC):
                                k = (a is a_lo, w is wo_lo, r, c)
                                last = nc.tensor.matmul(bank[:, :], a[:, r, c, :], w[:, r * PC + c, :],
                                                        start=(k == (False, False, 0, 0)), stop=(k == (True, False, RC - 1, PC - 1)))
                    last.then_inc(y_done, 1)

                def transposes(n, i):
                    pe.wait_ge(h_done, tile(n, i) + 1)
                    pe.wait_ge(lo_done, tile(n, i) + 1)
                    for c in range(HC):
                        last = nc.tensor.transpose(ps_t[i][:, c * P:(c + 1) * P], h[:, i, c * P:(c + 1) * P], ident[:, :])
                    last.then_inc(t_done, 1)

                pe.sem_inc(y_done, 1)
                pe.wait_ge(ident_ready, 2)
                product(0, 0, first=True)
                with pe.Fori(0, NT // 2 - 1) as n:
                    for i in range(2):
                        product(n, i + 1)
                        transposes(n, i)
                product(NT // 2 - 1, 1)
                transposes(NT // 2 - 1, 0)
                transposes(NT // 2 - 1, 1)

            @block.vector
            def _(dve):
                dve.sem_inc(x1_done, 2)
                dve.sem_inc(lo_done, 2)
                dve.wait_ge(rows_loaded, 64)
                nc.vector.tensor_tensor(bias[:, :], bias[:, :], rows[:, 0, :], ALU.mult).then_inc(bias_ready, 1)
                for r in range(WC):
                    dve.wait_ge(wo_loaded[r % 2], 16 * (r // 2) + 16)
                    nc.vector.tensor_tensor(wo_raw[:, r % 2, :, :], wo_raw[:, r % 2, :, :], rows[:, 0:1, :].broadcast_to([P, WP, HID]),
                                            ALU.mult).then_inc(wo_scaled, 1)

                def residual_norm(n, i):
                    tok_tile = tile(n, i)
                    x1_tile = x1[:, bass.ds(tok_tile, 1), :].rearrange("p a n -> p (a n)")
                    dve.wait_ge(xb_done, tok_tile + 1)
                    dve.wait_ge(y_done, tok_tile + 2)
                    settle(dve, dve_begun)
                    nc.vector.tensor_tensor(x1_tile, ps_y[i][:, :], x1_tile, ALU.add).then_inc(x1_done, 1)
                    dve.wait_ge(x1_done, tok_tile + 3)
                    settle(dve, dve_begun)
                    nc.vector.bn_stats(stats[:, i, :], x1_tile).then_inc(stats_done, 1)
                    dve.wait_ge(stats_done, tok_tile * 2 + 1)
                    settle(dve, dve_begun)
                    nc.vector.bn_aggr(mv[:, i, :], stats[:, i, :]).then_inc(stats_done, 1)
                    dve.wait_ge(stats_done, tok_tile * 2 + 2)
                    nc.vector.tensor_scalar(mv[:, i, 1:2], mv[:, i, 1:2], EPS, None, ALU.add).then_inc(mv_done, 1)
                    dve.wait_ge(std_done, tok_tile + 1)
                    nc.vector.reciprocal(rstd[:, i:i + 1], std[:, i:i + 1]).then_inc(rstd_done, 1)
                    dve.wait_ge(rstd_done, tok_tile + 1)
                    settle(dve, dve_begun)
                    nc.vector.tensor_scalar(h[:, i, :], x1_tile, mv[:, i, 0:1], rstd[:, i:i + 1], ALU.subtract, ALU.mult).then_inc(h_step, 1)
                    dve.wait_ge(h_step, tok_tile * 2 + 1)
                    nc.vector.tensor_tensor(h[:, i, :], h[:, i, :], rows[:, 2, :], ALU.mult).then_inc(h_step, 1)
                    dve.wait_ge(h_step, tok_tile * 2 + 2)
                    nc.vector.tensor_tensor(h[:, i, :], h[:, i, :], rows[:, 1, :], ALU.add).then_inc(h_done, 1)

                def low_part(n, i):
                    cols = bass.ds(tile(n, i) * P, P)
                    dve.wait_ge(hi_done, tile(n, i) + 1)
                    settle(dve, dve_begun)
                    nc.vector.tensor_tensor(hT_lo[:, :, cols], ps_t[i][:, :].rearrange("p (c t) -> p c t", c=HC),
                                            f32(hT_hi[:, :, cols]), ALU.subtract).then_inc(lo_done, 1)

                with dve.Fori(0, NT // 2) as n:
                    for i in range(2):
                        residual_norm(n, i)
                        low_part(n, i)


def stage_d(nc, wg, wu, wd, mods_dram, out, x1, hT_hi, hT_lo):
    with ExitStack() as ctx:
        def sb(name, shape, dt=F32):
            return ctx.enter_context(nc.sbuf_tensor(name, shape, dt))

        def sem(name):
            return ctx.enter_context(nc.semaphore(name))

        def bank(name):
            return ctx.enter_context(nc.psum_tensor(name, [P, UT], F32))

        GC = INNER // (4 * P)
        J = 4
        gate_b = sb("gate_b", [P, HID])
        gu_raw = sb("gu_raw", [P, 2, 2, HC, P])
        gu_hi = sb("gu_hi", [P, J, 2, HC, P], F32R)
        gu_lo = sb("gu_lo", [P, J, 2, HC, P], F32R)
        wd_raw = sb("wd_raw", [P, 2, HID])
        wd_hi = sb("wd_hi", [P, J, HID], F32R)
        wd_lo = sb("wd_lo", [P, J, HID], F32R)
        silu = sb("silu", [P, 2, UT])
        h = sb("d_h", [P, J, UT])
        mag = sb("d_mag", [P, J, UT])
        ge = sb("ge", [P, 6, UT], BF16)
        rank = sb("rank", [P, J, UT], BF16)
        hs_hi = sb("hs_hi", [P, J, UT], F32R)
        hs_lo = sb("hs_lo", [P, J, UT], F32R)
        ps_g = [bank(f"ps_g{i}") for i in range(2)]
        ps_u = [bank(f"ps_u{i}") for i in range(2)]
        ps_d = [bank(f"ps_d{i}") for i in range(2)]

        gate_loaded = sem("gate_loaded")
        gu_loaded, gu_hi_done, gu_split = [sem("gu_loaded0"), sem("gu_loaded1")], sem("gu_hi_done"), sem("gu_split")
        wd_loaded, wd_scaled, wd_hi_done, wd_split = [sem("wd_loaded0"), sem("wd_loaded1")], sem("wd_scaled"), sem("wd_hi_done"), sem("wd_split")
        g_done, u_done, silu_done, h_done = sem("g_done"), sem("u_done"), sem("silu_done"), sem("d_h_done")
        mag_done, ge_done, rank_step, kept_done = sem("mag_done"), sem("ge_done"), sem("rank_step"), sem("kept_done")
        hs_hi_done, hs_lo_done = sem("hs_hi_done"), sem("hs_lo_done")
        down_done, added, stored = sem("down_done"), sem("added"), sem("stored")
        pool_begun, sp_begun, dve_begun = sem("d_pool_begun"), sem("d_sp_begun"), sem("d_dve_begun")

        def at(unit, per, count):
            g, t = unit
            return g * (UNITS * per) + (t * per + count)

        def following(unit):
            g, t = unit
            return (g, t + 1) if t + 1 < UNITS else (g + 1, 0)

        with nc.Block() as block:
            @block.sync
            def _(sp):
                def load_gu(g, j, first=False):
                    if isinstance(g, int):
                        chunk = slice(g, g + 1)
                    else:
                        chunk = bass.ds(sp.snap(g), 1)
                    if not first or j >= 2:
                        sp.wait_ge(gu_split, g * J + (j - 1))
                        settle(sp, sp_begun)
                    for i, w in enumerate((wg, wu)):
                        sp.dma_start(gu_raw[:, j % 2, i, :, :], w[chunk, :, j, :, :].rearrange("a p c n -> p (a c) n")).then_inc(gu_loaded[j % 2], 16)

                def load_wd(g, j, first=False):
                    if isinstance(g, int):
                        chunk = slice(g, g + 1)
                    else:
                        chunk = bass.ds(sp.snap(g), 1)
                    if not first or j >= 2:
                        sp.wait_ge(wd_split, g * J + (j - 1))
                        settle(sp, sp_begun)
                    sp.dma_start(wd_raw[:, j % 2, :], wd[chunk, :, j, :].rearrange("a p n -> p (a n)")).then_inc(wd_loaded[j % 2], 16)

                sp.dma_start(gate_b[:, :], mods_dram[5]).then_inc(gate_loaded, 16)
                for j in range(J):
                    load_gu(0, j, first=True)
                for j in range(J):
                    load_wd(0, j, first=True)
                with sp.Fori(0, GC - 1) as g:
                    for j in range(J):
                        load_gu(g + 1, j)
                    for j in range(J):
                        load_wd(g + 1, j)
                for t in range(UNITS):
                    for k in range(4):
                        sp.wait_ge(added, at((GC - 1, t), 4, k + 1) + 2)
                        sp.dma_start(out[4 * t + k], x1[:, 4 * t + k, :]).then_inc(stored, 16)
                sp.wait_ge(stored, 16 * NT)

            @block.gpsimd
            def _(pool):
                def gu_low(g, j):
                    pool.wait_ge(gu_hi_done, g * J + (j + 1))
                    nc.gpsimd.tensor_tensor(gu_lo[:, j], gu_raw[:, j % 2], f32(gu_hi[:, j]), ALU.subtract).then_inc(gu_split, 1)

                def wd_scale(g, j):
                    pool.wait_ge(wd_loaded[j % 2], g * 32 + (16 * (j // 2) + 16))
                    nc.gpsimd.tensor_tensor(wd_raw[:, j % 2, :], wd_raw[:, j % 2, :], gate_b[:, :], ALU.mult).then_inc(wd_scaled, 1)

                def wd_low(g, j):
                    pool.wait_ge(wd_hi_done, g * J + (j + 1))
                    nc.gpsimd.tensor_tensor(wd_lo[:, j, :], wd_raw[:, j % 2, :], f32(wd_hi[:, j, :]), ALU.subtract).then_inc(wd_split, 1)

                pool.wait_ge(gate_loaded, 16)
                for j in range(J):
                    gu_low(0, j)
                for j in range(J):
                    wd_scale(0, j)
                    wd_low(0, j)
                with pool.Fori(0, GC - 1) as g:
                    for j in range(J):
                        gu_low(g + 1, j)
                    for j in range(J):
                        wd_scale(g + 1, j)
                        wd_low(g + 1, j)

            @block.scalar
            def _(act):
                def gu_high(g, j, first=False):
                    if not first:
                        act.wait_ge(u_done, (g - 1) * (UNITS * J) + ((UNITS - 1) * J + j + 1))
                    act.wait_ge(gu_loaded[j % 2], g * 64 + (32 * (j // 2) + 32))
                    nc.scalar.activation(gu_hi[:, j], gu_raw[:, j % 2], ACT.Copy).then_inc(gu_hi_done, 1)

                def wd_high(g, j, first=False):
                    if not first:
                        act.wait_ge(down_done, g * (UNITS * 4) + 1)
                    act.wait_ge(wd_scaled, g * J + (j + 1))
                    nc.scalar.activation(wd_hi[:, j, :], wd_raw[:, j % 2, :], ACT.Copy).then_inc(wd_hi_done, 1)

                def silus(unit, j):
                    act.wait_ge(g_done, at(unit, 4, j + 1))
                    act.wait_ge(h_done, at(unit, 4, j + 1))
                    nc.scalar.activation(silu[:, j % 2, :], ps_g[j % 2][:, :], ACT.Silu).then_inc(silu_done, 1)

                def magnitudes(unit):
                    act.wait_ge(h_done, at(unit, 4, 4 + 2))
                    nc.scalar.activation(mag[:, :, :], h[:, :, :], ACT.Abs).then_inc(mag_done, 1)

                def kept_high(unit):
                    act.wait_ge(down_done, at(unit, 4, 1))
                    act.wait_ge(kept_done, at(unit, 4, 4))
                    nc.scalar.activation(hs_hi[:, :, :], mag[:, :, :], ACT.Copy).then_inc(hs_hi_done, 1)

                for j in range(J):
                    gu_high(0, j, first=True)
                for j in range(J):
                    silus((0, 0), j)
                for j in range(J):
                    wd_high(0, j, first=True)

                def slot(unit, last=False):
                    g, t = unit
                    nxt = following(unit)
                    magnitudes(unit)
                    kept_high(unit)
                    if t == 0 and not (isinstance(g, int) and g == 0):
                        pass
                    if not last:
                        for j in range(J):
                            silus(nxt, j)
                            if t == UNITS - 2 and not (isinstance(g, int) and g == GC - 1):
                                gu_high(g + 1, j)
                    if t == UNITS - 1 and not (isinstance(g, int) and g == GC - 1):
                        for j in range(J):
                            wd_high(g + 1, j)

                with act.Fori(0, GC - 1) as g:
                    for t in range(UNITS):
                        slot((g, t))
                for t in range(UNITS):
                    slot((GC - 1, t), last=(t == UNITS - 1))

            @block.tensor
            def _(pe):
                def gate_up(unit):
                    g, t = unit
                    cols = slice(t * UT, (t + 1) * UT)
                    for j in range(J):
                        if t == 0:
                            pe.wait_ge(gu_split, g * J + (j + 1))
                        pe.wait_ge(h_done, at(unit, 4, j + 1))
                        for i, (bank, done) in enumerate(((ps_g, g_done), (ps_u, u_done))):
                            k = 0
                            for w, hT in ((gu_hi, hT_hi), (gu_hi, hT_lo), (gu_lo, hT_hi)):
                                for c in range(HC):
                                    last = nc.tensor.matmul(bank[j % 2][:, :], w[:, j, i, c, :], hT[:, c, cols], start=(k == 0), stop=(k == 3 * HC - 1))
                                    k += 1
                            last.then_inc(done, 1)

                def down(unit):
                    g, t = unit
                    pe.wait_ge(hs_lo_done, at(unit, 1, 1))
                    if t == 0:
                        pe.wait_ge(wd_split, g * J + J)
                    for n in range(4):
                        pe.wait_ge(added, at(unit, 4, n + 1))
                        k = 0
                        for a, w in ((hs_hi, wd_hi), (hs_hi, wd_lo), (hs_lo, wd_hi)):
                            for j in range(J):
                                last = nc.tensor.matmul(ps_d[n % 2][:, :], a[:, j, n * P:(n + 1) * P], w[:, j, :], start=(k == 0), stop=(k == 3 * J - 1))
                                k += 1
                        last.then_inc(down_done, 1)

                pe.sem_inc(down_done, 1)
                gate_up((0, 0))
                with pe.Fori(0, GC - 1) as g:
                    for t in range(UNITS):
                        gate_up(following((g, t)))
                        down((g, t))
                for t in range(UNITS):
                    if t + 1 < UNITS:
                        gate_up((GC - 1, t + 1))
                    down((GC - 1, t))

            @block.vector
            def _(dve):
                def members(unit, j):
                    dve.wait_ge(u_done, at(unit, 4, j + 1))
                    dve.wait_ge(silu_done, at(unit, 4, j + 1))
                    nc.vector.tensor_tensor(h[:, j, :], ps_u[j % 2][:, :], silu[:, j % 2, :], ALU.mult).then_inc(h_done, 1)

                def select(unit):
                    dve.wait_ge(mag_done, at(unit, 1, 1))
                    g0 = 0
                    for i, n in ((0, 3), (1, 2), (2, 1)):
                        nc.vector.tensor_tensor(ge[:, g0:g0 + n, :], mag[:, i:i + 1, :].broadcast_to([P, n, UT]), mag[:, i + 1:i + 1 + n, :], ALU.is_ge).then_inc(ge_done, 1)
                        g0 += n
                    dve.wait_ge(ge_done, at(unit, 3, 3))
                    steps = [(0, 0, 1, ALU.add), (1, 3, 4, ALU.add), (2, 5, 1, ALU.subtract), (3, 2, 4, ALU.add)]
                    for j, a, b, op in steps:
                        nc.vector.tensor_tensor(rank[:, j, :], ge[:, a, :], ge[:, b, :], op).then_inc(rank_step, 1)
                    for n, (j, b, op) in enumerate(((0, 2, ALU.add), (1, 0, ALU.subtract), (2, 3, ALU.subtract), (3, 5, ALU.add))):
                        dve.wait_ge(rank_step, at(unit, 8, 4 + n))
                        nc.vector.tensor_tensor(rank[:, j, :], rank[:, j, :], ge[:, b, :], op).then_inc(rank_step, 1)
                    for n, (j, bound, op) in enumerate(((0, 1.5, ALU.is_ge), (1, 0.5, ALU.is_ge), (2, -0.5, ALU.is_ge), (3, 1.5, ALU.is_le))):
                        if n == 0:
                            dve.wait_ge(rank_step, at(unit, 8, 8))
                        nc.vector.scalar_tensor_tensor(mag[:, j, :], rank[:, j, :], bound, h[:, j, :], op, ALU.mult).then_inc(kept_done, 1)

                def kept_low(unit):
                    dve.wait_ge(hs_hi_done, at(unit, 1, 1))
                    nc.vector.tensor_tensor(hs_lo[:, :, :], mag[:, :, :], f32(hs_hi[:, :, :]), ALU.subtract).then_inc(hs_lo_done, 1)

                def accumulate(unit, n):
                    dve.wait_ge(down_done, at(unit, 4, n + 1 + 1))
                    tile = x1[:, 4 * unit[1] + n, :]
                    nc.vector.tensor_tensor(tile, ps_d[n % 2][:, :], tile, ALU.add).then_inc(added, 1)

                dve.sem_inc(h_done, 2)
                dve.sem_inc(added, 2)
                for j in range(J):
                    members((0, 0), j)

                def slot(unit, last=False):
                    select(unit)
                    kept_low(unit)
                    if not last:
                        for j in range(J):
                            members(following(unit), j)
                    for n in range(4):
                        accumulate(unit, n)

                with dve.Fori(0, GC - 1) as g:
                    for t in range(UNITS):
                        slot((g, t))
                for t in range(UNITS):
                    slot((GC - 1, t), last=(t == UNITS - 1))


def block_program(nc, x, c_cols, wmod, wq, wk, wv, wo, bo_rep, wg, wu, wd, rope, masks, out):
    mods_dram = nc.dram_tensor("mods_scratch", [6, P, HID], F32, kind="Internal").ap()
    aT_dram = nc.dram_tensor("aT_scratch", [NT, P, PAIRS, P], F32, kind="Internal").ap()
    with ExitStack() as ctx:
        hT_hi = ctx.enter_context(nc.sbuf_tensor("hT_hi", [P, HC, TOK], F32R))
        hT_lo = ctx.enter_context(nc.sbuf_tensor("hT_lo", [P, HC, TOK], F32R))
        stage_a(nc, x, c_cols, wmod, mods_dram, hT_hi, hT_lo)
        stage_b(nc, wq, wk, wv, rope, masks, aT_dram, hT_hi, hT_lo)
        x1 = ctx.enter_context(nc.sbuf_tensor("x1", [P, NT, HID], F32))
        stage_c(nc, x, wo, bo_rep, mods_dram, aT_dram, x1, hT_hi, hT_lo)
        stage_d(nc, wg, wu, wd, mods_dram, out, x1, hT_hi, hT_lo)


def rope_tables():
    inv_freq = (1.0 / 10000.0 ** (np.arange(0, D, 2, dtype=np.float32) / np.float32(D))).astype(np.float32)
    freqs = np.arange(TOK, dtype=np.float32)[None, :] * inv_freq[:, None]
    cos, sin = np.cos(freqs), np.sin(freqs)
    return np.stack([np.tile(cos, (4, 1)), np.tile(np.concatenate([-sin, sin]), (2, 1))]).astype(np.float32)


def mask_table():
    m = np.zeros((P, 512 + P), np.float32)
    m[:, 512:] = np.where(np.arange(P)[:, None] >= np.arange(P)[None, :], 0.0, MASKED)
    return m


def laid_out(x, Wq, Wk, Wv, Wo, bo, w_gate, w_up, w_down, c, wmod):
    def pairs(w):
        return w.reshape(PAIRS, P, HC, P).transpose(0, 3, 2, 1)

    def members(w):
        return w.reshape(HC, P, INNER // (4 * P), P, 4).transpose(2, 1, 4, 0, 3)

    return {
        "x": x.reshape(NT, P, HID),
        "c_cols": c.reshape(HC, P).T,
        "wmod": wmod,
        "wq": pairs(Wq), "wk": pairs(Wk), "wv": pairs(Wv),
        "wo": Wo.T.reshape(PAIRS, P, HID).transpose(1, 0, 2),
        "bo_rep": np.broadcast_to(bo, (P, HID)),
        "wg": members(w_gate), "wu": members(w_up),
        "wd": w_down.reshape(INNER // (4 * P), P, 4, HID),
        "rope": rope_tables(), "masks": mask_table(),
    }


def kernel(L0_attn_hidden_states, L0_attn_Wq, L0_attn_Wk, L0_attn_Wv, L0_attn_Wo, L0_attn_bo,
           L0_ffn_w_gate, L0_ffn_w_up, L0_ffn_w_down, L0_c, L0_wmod):
    import concourse.bacc as bacc
    from concourse.bass_utils import run_bass_kernel_spmd

    nc = bacc.Bacc("TRN2", target_bir_lowering=False, num_devices=1)
    arrays = {n: np.ascontiguousarray(a) for n, a in laid_out(
        np.asarray(L0_attn_hidden_states), np.asarray(L0_attn_Wq), np.asarray(L0_attn_Wk), np.asarray(L0_attn_Wv),
        np.asarray(L0_attn_Wo), np.asarray(L0_attn_bo), np.asarray(L0_ffn_w_gate), np.asarray(L0_ffn_w_up),
        np.asarray(L0_ffn_w_down), np.asarray(L0_c), np.asarray(L0_wmod)).items()}
    args = {n: nc.dram_tensor(n, a.shape, F32, kind="ExternalInput").ap() for n, a in arrays.items()}
    out = nc.dram_tensor("out", (NT, P, HID), F32, kind="ExternalOutput").ap()
    block_program(nc, out=out, **args)
    r = run_bass_kernel_spmd(nc, [arrays], core_ids=[0])
    return r.results[0]["out"].reshape(1, TOK, HID)
```

```python
from contextlib import ExitStack

import numpy as np

import concourse.bass as bass
from concourse import mybir

F32 = mybir.dt.float32
F32R = mybir.dt.float32r
BF16 = mybir.dt.bfloat16
ALU = mybir.AluOpType
ACT = mybir.ActivationFunctionType
AX_X = mybir.AxisListType.X

P = 128
TOK = 2048
HID = 512
HC = HID // P
NT = TOK // P
UT = 512
UNITS = TOK // UT
HEADS = 32
D = 64
PAIRS = HEADS // 2
LOCAL_PAIRS = PAIRS - 1
INNER = 2048
BLOCK = 256
LOOKBACK = 128
EPS = 1e-5
GATE_MIN = 0.25
MASKED = -1e30
SCALE = 1.0 / D ** 0.5
NEG_SCALE = -SCALE


def f32(ap):
    return ap.bitcast(F32)


def settle(eng, begun):
    eng.sem_inc(begun, 1)


def make_identity(pool, ident, done):
    pool.memset(ident[:, :], 0.0).then_inc(done, 1)
    pool.wait_ge(done, 1)
    pool.affine_select(out=ident[:, :], in_=ident[:, :], compare_op=ALU.not_equal, fill=1.0,
                       base=0, pattern=[[-1, P]], channel_multiplier=1).then_inc(done, 1)


def stage_a(nc, x, c_cols, wmod, mods_dram, hT_hi, hT_lo):
    with ExitStack() as ctx:
        def sb(name, shape, dt=F32):
            return ctx.enter_context(nc.sbuf_tensor(name, shape, dt))

        def sem(name):
            return ctx.enter_context(nc.semaphore(name))

        ident = sb("a_ident", [P, P])
        c_sb = sb("c_sb", [P, HC])
        silu_c = sb("silu_c", [P, HC])
        ones = sb("ones", [P, P])
        silu_rep = sb("silu_rep", [P, HC, P])
        wm = sb("wm", [P, HC, 6 * HID])
        mods = sb("mods_sb", [P, 6, HID])
        sign = sb("sign", [P, 2, HID])
        mag = sb("mag", [P, 2, HID])
        xt = sb("xt", [P, 2, HID])
        stats = sb("stats", [P, 2, 6])
        mv = sb("mv", [P, 2, 2])
        std = sb("std", [P, 2])
        rstd = sb("rstd", [P, 2])
        xn = sb("xn", [P, 2, HID])
        scaled = sb("scaled", [P, 2, HID])
        h = sb("h", [P, 2, HID])
        ps_mod = [ctx.enter_context(nc.psum_tensor(f"ps_mod{i}", [P, HID], F32)) for i in range(2)]
        ps_t = [ctx.enter_context(nc.psum_tensor(f"ps_t{i}", [P, HID], F32)) for i in range(2)]

        c_loaded, wm_loaded, ident_ready = sem("c_loaded"), sem("wm_loaded"), sem("a_ident_ready")
        silu_ready, ones_ready, rep_ready = sem("silu_ready"), sem("ones_ready"), sem("rep_ready")
        mod_done, mod_copied, gate_step, gates_ready = sem("mod_done"), sem("mod_copied"), sem("gate_step"), sem("gates_ready")
        mods_stored, dve_begun, sp_begun = sem("mods_stored"), sem("a_dve_begun"), sem("a_sp_begun")
        x_loaded = [sem(f"x_loaded{i}") for i in range(2)]
        stats_done, mv_done, std_done, rstd_done = sem("stats_done"), sem("mv_done"), sem("std_done"), sem("rstd_done")
        xn_done, scaled_done, h_done = sem("xn_done"), sem("scaled_done"), sem("h_done")
        t_done, hi_done, lo_done = sem("t_done"), sem("hi_done"), sem("lo_done")

        with nc.Block() as block:
            @block.sync
            def _(sp):
                sp.dma_start(c_sb[:, :], c_cols).then_inc(c_loaded, 16)
                for i in range(2):
                    sp.dma_start(xt[:, i, :], x[i]).then_inc(x_loaded[i], 16)
                sp.dma_start(wm[:, :, :], wmod.rearrange("(c p) n -> p c n", p=P)).then_inc(wm_loaded, 16)
                with sp.Fori(1, NT // 2) as n:
                    for i in range(2):
                        used = sp.snap(n * 2 + (i - 1))
                        tile = sp.snap(n * 2 + i)
                        sp.wait_ge(xn_done, used)
                        settle(sp, sp_begun)
                        sp.dma_start(xt[:, i, :], x[bass.ds(tile, 1)].rearrange("a p n -> p (a n)")).then_inc(x_loaded[i], 16)
                sp.wait_ge(gates_ready, 4)
                sp.dma_start(mods_dram.rearrange("i p n -> p i n"), mods[:, :, :]).then_inc(mods_stored, 16)
                sp.wait_ge(mods_stored, 16)

            @block.gpsimd
            def _(pool):
                make_identity(pool, ident, ident_ready)

            @block.scalar
            def _(act):
                act.wait_ge(c_loaded, 16)
                nc.scalar.activation(silu_c[:, :], c_sb[:, :], ACT.Silu).then_inc(silu_ready, 1)
                for j in range(6):
                    act.wait_ge(mod_done, j + 1)
                    nc.scalar.activation(mods[:, j, :], ps_mod[j % 2][:, :], ACT.Copy).then_inc(mod_copied, 1)
                with act.Fori(0, NT // 2) as n:
                    for i in range(2):
                        act.wait_ge(mv_done, n * 2 + (i + 1))
                        nc.scalar.activation(std[:, i:i + 1], mv[:, i, 1:2], ACT.Sqrt).then_inc(std_done, 1)
                    for i in range(2):
                        act.wait_ge(t_done, n * 2 + (i + 1))
                        act.wait_ge(ident_ready, 2)
                        nc.scalar.activation(hT_hi[:, :, bass.ds((n * 2 + i) * P, P)],
                                             ps_t[i][:, :].rearrange("p (c t) -> p c t", c=HC), ACT.Copy).then_inc(hi_done, 1)

            @block.tensor
            def _(pe):
                pe.wait_ge(rep_ready, HC)
                pe.wait_ge(wm_loaded, 16)
                for j in range(6):
                    if j >= 2:
                        pe.wait_ge(mod_copied, j - 1)
                    for c in range(HC):
                        last = nc.tensor.matmul(ps_mod[j % 2][:, :], silu_rep[:, c, :], wm[:, c, j * HID:(j + 1) * HID],
                                                start=(c == 0), stop=(c == HC - 1))
                    last.then_inc(mod_done, 1)
                pe.wait_ge(ident_ready, 2)
                with pe.Fori(0, NT // 2) as n:
                    for i in range(2):
                        pe.wait_ge(h_done, n * 2 + (i + 1))
                        pe.wait_ge(lo_done, n * 2 + (i + 1))
                        for c in range(HC):
                            last = nc.tensor.transpose(ps_t[i][:, c * P:(c + 1) * P], h[:, i, c * P:(c + 1) * P], ident[:, :])
                        last.then_inc(t_done, 1)

            @block.vector
            def _(dve):
                dve.sem_inc(lo_done, 2)
                nc.vector.memset(ones[:, :], 1.0).then_inc(ones_ready, 1)
                dve.wait_ge(ones_ready, 1)
                dve.wait_ge(silu_ready, 1)
                for c in range(HC):
                    nc.vector.tensor_scalar(silu_rep[:, c, :], ones[:, :], silu_c[:, c:c + 1], None, ALU.mult).then_inc(rep_ready, 1)
                dve.wait_ge(mod_copied, 6)
                for k, j in enumerate((1, 4)):
                    nc.vector.tensor_scalar(mods[:, j, :], mods[:, j, :], 1.0, None, ALU.add).then_inc(gates_ready, 1)
                for k, j in enumerate((2, 5)):
                    nc.vector.tensor_scalar(sign[:, k, :], mods[:, j, :], 0.0, 2.0, ALU.is_ge, ALU.mult).then_inc(gate_step, 1)
                    nc.vector.scalar_tensor_tensor(mag[:, k, :], mods[:, j, :], -1.0, mods[:, j, :], ALU.mult, ALU.max).then_inc(gate_step, 1)
                    dve.wait_ge(gate_step, 3 * k + 2)
                    nc.vector.tensor_scalar(mag[:, k, :], mag[:, k, :], GATE_MIN, None, ALU.max).then_inc(gate_step, 1)
                    dve.wait_ge(gate_step, 3 * k + 3)
                    nc.vector.scalar_tensor_tensor(mods[:, j, :], sign[:, k, :], -1.0, mag[:, k, :], ALU.add, ALU.mult).then_inc(gates_ready, 1)
                dve.wait_ge(gates_ready, 4)
                with dve.Fori(0, NT // 2) as n:
                    for i in range(2):
                        dve.wait_ge(x_loaded[i], n * 16 + 16)
                        nc.vector.bn_stats(stats[:, i, :], xt[:, i, :]).then_inc(stats_done, 1)
                        dve.wait_ge(stats_done, n * 4 + (2 * i + 1))
                        settle(dve, dve_begun)
                        nc.vector.bn_aggr(mv[:, i, :], stats[:, i, :]).then_inc(stats_done, 1)
                        dve.wait_ge(stats_done, n * 4 + (2 * i + 2))
                        nc.vector.tensor_scalar(mv[:, i, 1:2], mv[:, i, 1:2], EPS, None, ALU.add).then_inc(mv_done, 1)
                    for i in range(2):
                        dve.wait_ge(std_done, n * 2 + (i + 1))
                        nc.vector.reciprocal(rstd[:, i:i + 1], std[:, i:i + 1]).then_inc(rstd_done, 1)
                        dve.wait_ge(rstd_done, n * 2 + (i + 1))
                        nc.vector.tensor_scalar(xn[:, i, :], xt[:, i, :], mv[:, i, 0:1], rstd[:, i:i + 1], ALU.subtract, ALU.mult).then_inc(xn_done, 1)
                        dve.wait_ge(xn_done, n * 2 + (i + 1))
                        nc.vector.tensor_tensor(scaled[:, i, :], xn[:, i, :], mods[:, 1, :], ALU.mult).then_inc(scaled_done, 1)
                        dve.wait_ge(scaled_done, n * 2 + (i + 1))
                        nc.vector.tensor_tensor(h[:, i, :], scaled[:, i, :], mods[:, 0, :], ALU.add).then_inc(h_done, 1)
                    for i in range(2):
                        dve.wait_ge(hi_done, n * 2 + (i + 1))
                        cols = bass.ds((n * 2 + i) * P, P)
                        nc.vector.tensor_tensor(hT_lo[:, :, cols], ps_t[i][:, :].rearrange("p (c t) -> p c t", c=HC),
                                                f32(hT_hi[:, :, cols]), ALU.subtract).then_inc(lo_done, 1)


def stage_b(nc, wq, wk, wv, rope, masks, aT_dram, hT_hi, hT_lo):
    with ExitStack() as ctx:
        def sb(name, shape, dt=F32):
            return ctx.enter_context(nc.sbuf_tensor(name, shape, dt))

        def sem(name):
            return ctx.enter_context(nc.semaphore(name))

        def bank(name):
            return ctx.enter_context(nc.psum_tensor(name, [P, 512], F32))

        ident = sb("b_ident", [P, P])
        cs = sb("cs", [P, 2, TOK])
        mask = sb("mask_sb", [P, 512 + P])
        before_split = sb("before_split", [P, 10, UT])
        w_raw = before_split[:, 0:3, :].rearrange("p i (c n) -> p i c n", c=HC)
        raw = before_split[:, 3:6, :]
        rot = before_split[:, 6:8, :]
        rsum = before_split[:, 8:10, :]
        w_hi = sb("w_hi", [P, 3, HC, P], F32R)
        w_lo = sb("w_lo", [P, 3, HC, P], F32R)
        split = sb("split", [P, 2, 2, UT], F32R)
        q_dup = sb("q_dup", [P, 2, 2, 2, UT], F32R)
        k_stack = sb("k_stack", [P, 2, TOK], F32R)
        v_tok = sb("v_tok", [P, NT, 2, 2 * D], F32R)
        prob = sb("prob", [P, 2 * TOK])
        pt_hi = sb("pt_hi", [P, 3, 512], F32R)
        pt_lo = sb("pt_lo", [P, 3, 512], F32R)
        half = sb("half", [P, BLOCK])
        a_out = sb("a_out", [P, 2, UT])
        negmax = sb("negmax", [P, 8])
        den = sb("den", [P, 8])
        rden = sb("rden", [P, 8])
        ps_proj = [bank(f"ps_proj{i}") for i in range(2)]
        ps_s = [bank(f"ps_s{i}") for i in range(2)]
        ps_p = [bank(f"ps_p{i}") for i in range(2)]
        ps_o = bank("ps_o")
        ps_v = bank("ps_v")

        def job_prob(j):
            return prob[:, j * 384:(j + 1) * 384]

        tables_loaded, ident_ready, zeros_ready = sem("tables_loaded"), sem("b_ident_ready"), sem("zeros_ready")
        w_loaded, w_hi_done, w_split = sem("w_loaded"), sem("w_hi_done"), sem("w_split")
        proj_done, raw_done, rot_done = sem("proj_done"), sem("raw_done"), sem("rot_done")
        mults_done, sum_done, rhi_done, rlo_done = sem("rope_mults_done"), sem("rope_sum_done"), sem("rope_hi_done"), sem("rope_lo_done")
        stacked = sem("stacked")
        vt_done, vhi_done, vlo_done = sem("vt_done"), sem("vhi_done"), sem("vlo_done")
        scores_done, max_done, exp_done = sem("scores_done"), sem("max_done"), sem("exp_done")
        rden_done, prob_done = sem("rden_done"), sem("prob_done")
        pt_done, pthi_done, ptlo_done = sem("pt_done"), sem("pthi_done"), sem("ptlo_done")
        pv_done, half_done, a_done, a_stored = sem("pv_done"), sem("half_done"), sem("a_done"), sem("a_stored")
        dve_begun, pool_begun, sp_begun = sem("b_dve_begun"), sem("b_pool_begun"), sem("b_sp_begun")
        g_scores_done, g_max_done, g_min_done, g_exp_done = sem("g_scores_done"), sem("g_max_done"), sem("g_min_done"), sem("g_exp_done")
        g_rden_done, g_prob_done = sem("g_rden_done"), sem("g_prob_done")
        g_pt_done, g_pthi_done, g_ptlo_done = sem("g_pt_done"), sem("g_pthi_done"), sem("g_ptlo_done")
        g_pv_done, g_half_done, g_a_done = sem("g_pv_done"), sem("g_half_done"), sem("g_a_done")
        g_a_stored = [sem("g_a_stored0"), sem("g_a_stored1")]

        def at(unit, per, count):
            p, t = unit
            return p * (UNITS * per) + (t * per + count)

        def following(unit, n=1):
            p, t = unit
            return (p, t + n) if t + n < UNITS else (p + 1, t + n - UNITS)

        def before(unit):
            p, t = unit
            return (p, t - 1) if t > 0 else (p - 1, UNITS - 1)

        def job(j):
            return j // 4, j % 2, j % 4 // 2

        def first_tile(t, b):
            return 1 if (t == 0 and b == 0) else 0

        def job_cols(t, j):
            b, _, qt = job(j)
            return first_tile(t, b) * P, (2 + qt) * P

        GLOBAL = LOCAL_PAIRS
        END = (GLOBAL, 0)
        G = [(m, hd) for m in range(TOK // BLOCK) for hd in range(2)]
        SIDE = {-1 + 4 * (t - 2) + k: ((GLOBAL, t), k) for t in (2, 3) for k in range(4)}

        def g_chunks(m, qt):
            n = (2 * m + 1 + qt) * P
            return [(s, min(512, n - s), s + 512 >= n) for s in range(0, n, 512)]

        def g_banks(g):
            if g >= len(G):
                return []
            m = G[g][0]
            return [(qt, i, ch, i + 1 == len(g_chunks(m, qt))) for qt in range(2) for i, ch in enumerate(g_chunks(m, qt))]

        def g_counts(g):
            s = sum(len(g_banks(i)) for i in range(g))
            f = sum(m + 1 for m, _ in G[:g])
            return s, f

        def g_row(g, qt):
            m = G[g][0]
            if m < 4:
                return prob[:, (2 * (g % 2) + qt) * (TOK // 2):(2 * (g % 2) + qt + 1) * (TOK // 2)]
            if g % 2 == 1:
                return prob[:, qt * TOK:(qt + 1) * TOK]
            return before_split[:, :, :].rearrange("p a n -> p (a n)")[:, qt * TOK:(qt + 1) * TOK]

        with nc.Block() as block:
            @block.sync
            def _(sp):
                def load_weights(p):
                    pair = slice(0, 1) if isinstance(p, int) and p == 0 else bass.ds(sp.snap(p) if not isinstance(p, int) else p, 1)
                    for i, w in enumerate((wq, wk, wv)):
                        sp.dma_start(w_raw[:, i, :, :], w[pair].rearrange("a p c n -> p (a c) n")).then_inc(w_loaded, 16)

                def rotate(unit, first=False):
                    if not first:
                        sp.wait_ge(sum_done, at(unit, 1, 0))
                        settle(sp, sp_begun)
                    sp.wait_ge(raw_done, at(unit, 3, 2))
                    settle(sp, sp_begun)
                    for s in range(4):
                        d = s ^ 1
                        sp.dma_start(rot[32 * d:32 * d + 32, :, :], raw[32 * s:32 * s + 32, 0:2, :]).then_inc(rot_done, 16)

                def stack(unit, free=None, count=None):
                    t = unit[1]
                    if free is not None:
                        sp.wait_ge(free, count)
                        settle(sp, sp_begun)
                    sp.wait_ge(rlo_done, at(unit, 1, 1))
                    settle(sp, sp_begun)
                    for hd in range(2):
                        rows = slice(D * hd, D * hd + D)
                        for up in range(2):
                            sp.dma_start(f32(q_dup[D * up:D * up + D, t % 2, hd, :, :]), f32(split[rows, 0, :, :])).then_inc(stacked, 16)
                        for s in range(2):
                            sp.dma_start(f32(k_stack[D * s:D * s + D, hd, t * UT:(t + 1) * UT]), f32(split[rows, 1, s, :])).then_inc(stacked, 16)

                def store(unit):
                    p, t = unit
                    sp.wait_ge(a_done, at(unit, 4, 4 + 2))
                    settle(sp, sp_begun)
                    pair = bass.ds(p if isinstance(p, int) else sp.snap(p), 1)
                    sp.dma_start(aT_dram[t * 4:t * 4 + 4, :, pair, :].rearrange("k p a n -> p k (a n)"),
                                 a_out[:, t % 2, :].rearrange("p (k n) -> p k n", n=P)).then_inc(a_stored, 16)

                def slot(unit, first=False):
                    p, t = unit
                    if t == 0:
                        sp.wait_ge(w_split, p * 3 + 3)
                        settle(sp, sp_begun)
                        load_weights(p + 1)
                    if not first:
                        store(before(unit))
                    rotate(following(unit, 2))
                    if first:
                        stack(following(unit))
                    else:
                        stack(following(unit), scores_done, at(unit, 8, 0))

                sp.sem_inc(a_stored, 32)
                load_weights(0)
                sp.dma_start(cs[:, :, :], rope.rearrange("i p n -> p i n")).then_inc(tables_loaded, 16)
                sp.dma_start(mask[:, :], masks).then_inc(tables_loaded, 16)
                rotate((0, 0), first=True)
                stack((0, 0))
                rotate((0, 1))
                for t in range(UNITS):
                    slot((0, t), first=(t == 0))
                with sp.Fori(1, LOCAL_PAIRS) as p:
                    for t in range(UNITS):
                        slot((p, t))
                store(before(END))
                stack((GLOBAL, 1), scores_done, at(END, 8, 0))
                for t in range(UNITS):
                    if t < 2:
                        rotate((GLOBAL, t + 2))
                        stack((GLOBAL, t + 2), g_scores_done, g_counts(4 * (t + 1))[0])
                    sp.wait_ge(g_a_done, 4 * (t + 1))
                    sp.dma_start(aT_dram[t * 4:t * 4 + 4, :, GLOBAL, :].rearrange("k p n -> p k n"),
                                 a_out[:, t % 2, :].rearrange("p (k n) -> p k n", n=P)).then_inc(g_a_stored[t % 2], 16)
                sp.wait_ge(a_stored, 16 * (LOCAL_PAIRS * UNITS) + 32)
                for i in range(2):
                    sp.wait_ge(g_a_stored[i], 16 * UNITS // 2)

            @block.gpsimd
            def _(pool):
                def weights_low(p, m):
                    pool.wait_ge(w_hi_done, p * 3 + (m + 1))
                    settle(pool, pool_begun)
                    nc.gpsimd.tensor_tensor(w_lo[:, m, :, :], w_raw[:, m, :, :], f32(w_hi[:, m, :, :]), ALU.subtract).then_inc(w_split, 1)

                def rope_mults(unit, first=False):
                    cols = slice(unit[1] * UT, (unit[1] + 1) * UT)
                    if not first:
                        pool.wait_ge(rlo_done, at(unit, 1, 0))
                    pool.wait_ge(raw_done, at(unit, 3, 2))
                    nc.gpsimd.tensor_tensor(rsum[:, :, :], raw[:, 0:2, :], cs[:, 0:1, cols].broadcast_to([P, 2, UT]), ALU.mult).then_inc(mults_done, 1)
                    pool.wait_ge(rot_done, at(unit, 64, 64))
                    nc.gpsimd.tensor_tensor(rot[:, :, :], rot[:, :, :], cs[:, 1:2, cols].broadcast_to([P, 2, UT]), ALU.mult).then_inc(mults_done, 1)

                def normalize(unit, r):
                    pool.wait_ge(rden_done, at(unit, 4, r + 1))
                    settle(pool, pool_begun)
                    for j in (2 * r, 2 * r + 1):
                        lo, hi = job_cols(unit[1], j)
                        row = job_prob(j)[:, lo:hi]
                        nc.gpsimd.tensor_scalar(row, row, rden[:, j:j + 1], 1.0, ALU.mult, ALU.mult).then_inc(prob_done, 1)

                def slot(unit):
                    p, t = unit
                    for r in range(4):
                        normalize(unit, r)
                        if t == 1 and r >= 2:
                            weights_low(p + 1, r - 2)
                    if t == 1:
                        weights_low(p + 1, 2)
                    rope_mults(following(unit, 2))

                def g_normalize(g):
                    m = G[g][0]
                    for qt in range(2):
                        row = g_row(g, qt)[:, 0:(2 * m + 1 + qt) * P]
                        c = 2 * (g % 2) + qt
                        pool.wait_ge(g_rden_done, 2 * g + qt + 1)
                        nc.gpsimd.tensor_scalar(row, row, rden[:, c:c + 1], 1.0, ALU.mult, ALU.mult).then_inc(g_prob_done, 1)

                make_identity(pool, ident, ident_ready)
                nc.gpsimd.memset(f32(pt_hi[:, 2, :]), 0.0).then_inc(zeros_ready, 1)
                nc.gpsimd.memset(f32(pt_lo[:, 2, :]), 0.0).then_inc(zeros_ready, 1)
                for m in range(3):
                    weights_low(0, m)
                pool.wait_ge(tables_loaded, 32)
                rope_mults((0, 0), first=True)
                rope_mults((0, 1))
                for t in range(UNITS):
                    slot((0, t))
                with pool.Fori(1, LOCAL_PAIRS) as p:
                    for t in range(UNITS):
                        slot((p, t))
                g_normalize(0)
                for g in range(len(G)):
                    if g + 1 < len(G):
                        g_normalize(g + 1)
                    if g in (1, 5):
                        rope_mults((GLOBAL, 2 + g // 4))

            @block.scalar
            def _(act):
                def copy_raw(unit, m, first=False):
                    act.wait_ge(proj_done, at(unit, 3, m + 1))
                    if not first and m < 2:
                        act.wait_ge(rot_done, at(unit, 64, 0))
                        act.wait_ge(mults_done, at(unit, 2, 0))
                    if not first and m == 2:
                        act.wait_ge(vt_done, at(unit, 1, 0))
                    n = (3 * unit[1] + m) % 2
                    nc.scalar.activation(raw[:, m, :], ps_proj[n][:, :], ACT.Copy).then_inc(raw_done, 1)

                def v_hi(unit):
                    t = unit[1]
                    act.wait_ge(vt_done, at(unit, 1, 1))
                    nc.scalar.activation(v_tok[:, 4 * t:4 * t + 4, :, 0:D],
                                         ps_v[:, :].rearrange("p (k h d) -> p k h d", k=4, h=2), ACT.Copy).then_inc(vhi_done, 1)

                def exp(unit, j):
                    lo, hi = job_cols(unit[1], j)
                    row = job_prob(j)[:, lo:hi]
                    act.wait_ge(max_done, at(unit, 8, j + 1 + 2))
                    nc.scalar.activation(row, row, ACT.Exp, bias=negmax[:, j:j + 1], scale=-1.0,
                                         accum_out=den[:, j:j + 1]).then_inc(exp_done, 1)

                def p_hi(unit, b, f):
                    t = unit[1]
                    if f == 0:
                        act.wait_ge(pv_done, at(unit, 2, b + 1))
                    act.wait_ge(pt_done, at(unit, 6, 3 * b + f + 1))
                    n = (3 * b + f) % 2
                    if f < 2:
                        lo = first_tile(t, b) * BLOCK
                        nc.scalar.activation(pt_hi[:, f, lo:512], ps_p[n][:, lo:512], ACT.Copy).then_inc(pthi_done, 1)
                    else:
                        nc.scalar.activation(pt_hi[:, 2, :].rearrange("p (h q) -> p h q", h=2)[:, :, P:BLOCK],
                                             ps_p[n][:, 0:BLOCK].rearrange("p (h q) -> p h q", h=2), ACT.Copy).then_inc(pthi_done, 1)

                def halves(unit, b):
                    act.wait_ge(a_done, at(unit, 4, 2 * b + 2))
                    act.wait_ge(pv_done, at(unit, 2, b + 2))
                    nc.scalar.activation(half[0:D, :], ps_o[D:P, 0:BLOCK], ACT.Copy).then_inc(half_done, 1)
                    nc.scalar.activation(half[D:P, :], ps_o[0:D, BLOCK:2 * BLOCK], ACT.Copy).then_inc(half_done, 1)

                def slot(unit, first=False):
                    last, ahead = before(unit), following(unit, 2)
                    exp(unit, 0)
                    exp(unit, 1)
                    if not first:
                        p_hi(last, 1, 0)
                        p_hi(last, 1, 1)
                    exp(unit, 2)
                    exp(unit, 3)
                    if not first:
                        p_hi(last, 1, 2)
                    copy_raw(ahead, 0)
                    if not first:
                        halves(last, 1)
                    copy_raw(ahead, 1)
                    exp(unit, 4)
                    exp(unit, 5)
                    p_hi(unit, 0, 0)
                    p_hi(unit, 0, 1)
                    exp(unit, 6)
                    exp(unit, 7)
                    p_hi(unit, 0, 2)
                    copy_raw(ahead, 2)
                    halves(unit, 0)
                    v_hi(ahead)

                def g_exp(g, qt):
                    m = G[g][0]
                    row = g_row(g, qt)[:, 0:(2 * m + 1 + qt) * P]
                    c = 2 * (g % 2) + qt
                    act.wait_ge(g_min_done, 2 * g + qt + 1)
                    nc.scalar.activation(row, row, ACT.Exp, bias=negmax[:, c:c + 1], scale=-1.0,
                                         accum_out=den[:, c:c + 1]).then_inc(g_exp_done, 1)

                def side(g):
                    if g in SIDE:
                        unit, k = SIDE[g]
                        if k < 3:
                            copy_raw(unit, k)
                        else:
                            v_hi(unit)

                def g_p_hi(g, f):
                    m = G[g][0]
                    n = g_counts(g)[1] + f
                    src, dst = ps_p[n % 2], pt_hi[:, n % 2, :]
                    act.wait_ge(g_pt_done, n + 1)
                    if n >= 2:
                        act.wait_ge(g_pv_done, n - 1)
                    if f < m:
                        nc.scalar.activation(dst, src[:, :], ACT.Copy).then_inc(g_pthi_done, 1)
                    else:
                        if n == 1:
                            act.wait_ge(g_pv_done, 1)
                        nc.scalar.activation(dst[:, 0:BLOCK], src[:, 0:BLOCK], ACT.Copy)
                        nc.scalar.activation(pt_hi[:, 2, P:BLOCK], src[:, BLOCK:BLOCK + P], ACT.Copy).then_inc(g_pthi_done, 1)

                for t in range(2):
                    for m in range(3):
                        copy_raw((0, t), m, first=(t == 0))
                    v_hi((0, t))
                for t in range(UNITS):
                    slot((0, t), first=(t == 0))
                with act.Fori(1, LOCAL_PAIRS) as p:
                    for t in range(UNITS):
                        slot((p, t))
                p_hi(before(END), 1, 0)
                p_hi(before(END), 1, 1)
                for qt in range(2):
                    g_exp(0, qt)
                p_hi(before(END), 1, 2)
                side(-1)
                halves(before(END), 1)
                for g, (m, hd) in enumerate(G):
                    nb = len(g_banks(g + 1))
                    for f in range(m + 1):
                        g_p_hi(g, f)
                        for b in (2 * f, 2 * f + 1):
                            if b < nb and g_banks(g + 1)[b][3]:
                                g_exp(g + 1, g_banks(g + 1)[b][0])
                    side(g)
                    if g >= 2:
                        act.wait_ge(g_a_done, g - 1)
                    act.wait_ge(g_pv_done, g_counts(g + 1)[1])
                    if hd == 0:
                        nc.scalar.activation(half[0:D, :], ps_o[D:P, 0:BLOCK], ACT.Copy).then_inc(g_half_done, 1)
                    else:
                        nc.scalar.activation(half[D:P, :], ps_o[0:D, BLOCK:2 * BLOCK], ACT.Copy).then_inc(g_half_done, 1)

            @block.tensor
            def _(pe):
                def project(unit, m, first=False):
                    n = (3 * unit[1] + m) % 2
                    cols = slice(unit[1] * UT, (unit[1] + 1) * UT)
                    if not first:
                        pe.wait_ge(raw_done, at(unit, 3, m - 1))
                    elif m == 2:
                        pe.wait_ge(raw_done, 1)
                    pe.wait_ge(w_split, unit[0] * 3 + (m + 1))
                    k = 0
                    for w, h in ((w_hi, hT_hi), (w_hi, hT_lo), (w_lo, hT_hi)):
                        for c in range(HC):
                            last = nc.tensor.matmul(ps_proj[n][:, :], w[:, m, c, :], h[:, c, cols], start=(k == 0), stop=(k == 3 * HC - 1))
                            k += 1
                    last.then_inc(proj_done, 1)

                def transpose_v(unit, first=False):
                    if not first:
                        pe.wait_ge(vlo_done, at(unit, 1, 0))
                    pe.wait_ge(raw_done, at(unit, 3, 3))
                    for k in range(4):
                        last = nc.tensor.transpose(ps_v[:, k * P:(k + 1) * P], raw[:, 2, k * P:(k + 1) * P], ident[:, :])
                    last.then_inc(vt_done, 1)

                def scores(unit, j):
                    t = unit[1]
                    b, hd, qt = job(j)
                    lo, hi = job_cols(t, j)
                    if j == 0:
                        pe.wait_ge(stacked, at(unit, 128, 128))
                    pe.wait_ge(max_done, at(unit, 8, j + 1))
                    q0 = b * BLOCK + qt * P
                    k0 = t * UT + b * BLOCK - LOOKBACK
                    for s in range(2):
                        last = nc.tensor.matmul(ps_s[j % 2][:, lo:hi], q_dup[:, t % 2, hd, s, q0:q0 + P],
                                                k_stack[:, hd, k0 + lo:k0 + hi], start=(s == 0), stop=(s == 1))
                    last.then_inc(scores_done, 1)

                def transpose_p(unit, b, f):
                    t = unit[1]
                    if f == 0:
                        pe.wait_ge(prob_done, at(unit, 8, 4 * b + 4))
                    pe.wait_ge(ptlo_done, at(unit, 6, 3 * b + f + 1))
                    dst = ps_p[(3 * b + f) % 2]
                    if f < 2:
                        for c in range(first_tile(t, b), 2):
                            for qt in range(2):
                                last = nc.tensor.transpose(dst[:, c * BLOCK + qt * P:c * BLOCK + (qt + 1) * P],
                                                           job_prob(4 * b + 2 * qt + f)[:, c * P:(c + 1) * P], ident[:, :])
                    else:
                        for hd in range(2):
                            last = nc.tensor.transpose(dst[:, hd * P:(hd + 1) * P], job_prob(4 * b + 2 + hd)[:, 2 * P:3 * P], ident[:, :])
                    last.then_inc(pt_done, 1)

                def weighted_values(unit, b):
                    t = unit[1]
                    pe.wait_ge(vlo_done, at(unit, 1, 1))
                    pe.wait_ge(a_done, at(unit, 4, 2 * b + 2))
                    pe.wait_ge(ptlo_done, at(unit, 6, 3 * b + 3 + 2))
                    for hd in range(2):
                        group = [(c, pt) for c in range(first_tile(t, b), 3) for pt in (pt_hi, pt_lo)]
                        for n, (c, pt) in enumerate(group):
                            moving = pt[:, hd, c * BLOCK:(c + 1) * BLOCK] if c < 2 else pt[:, 2, hd * BLOCK:(hd + 1) * BLOCK]
                            last = nc.tensor.matmul(ps_o[:, hd * BLOCK:(hd + 1) * BLOCK], v_tok[:, 4 * t + 2 * b - 1 + c, hd, :], moving,
                                                    start=(n == 0), stop=(n == len(group) - 1))
                    last.then_inc(pv_done, 1)

                def slot(unit, first=False):
                    last, ahead = before(unit), following(unit, 2)
                    scores(unit, 0)
                    scores(unit, 1)
                    if not first:
                        transpose_p(last, 1, 0)
                        transpose_p(last, 1, 1)
                    scores(unit, 2)
                    scores(unit, 3)
                    if not first:
                        transpose_p(last, 1, 2)
                    project(ahead, 0)
                    if not first:
                        weighted_values(last, 1)
                    project(ahead, 1)
                    scores(unit, 4)
                    scores(unit, 5)
                    transpose_p(unit, 0, 0)
                    transpose_p(unit, 0, 1)
                    scores(unit, 6)
                    scores(unit, 7)
                    transpose_p(unit, 0, 2)
                    project(ahead, 2)
                    weighted_values(unit, 0)
                    transpose_v(ahead)

                def g_scores(g, b):
                    m, hd = G[g]
                    t = m // 2
                    qt, _, (start, width, _), _ = g_banks(g)[b]
                    n = g_counts(g)[0] + b
                    if b == 0 and g % 4 == 0:
                        pe.wait_ge(stacked, at((GLOBAL, t), 128, 128))
                    if n >= 2:
                        pe.wait_ge(g_max_done, n - 1)
                    else:
                        pe.wait_ge(max_done, at(END, 8, n + 1))
                    q0 = (m % 2) * BLOCK + qt * P
                    for s in range(2):
                        last = nc.tensor.matmul(ps_s[n % 2][:, 0:width], q_dup[:, t % 2, hd, s, q0:q0 + P],
                                                k_stack[:, hd, start:start + width], start=(s == 0), stop=(s == 1))
                    last.then_inc(g_scores_done, 1)

                def side(g):
                    if g in SIDE:
                        unit, k = SIDE[g]
                        if k < 3:
                            project(unit, k)
                        else:
                            transpose_v(unit)

                def g_transpose(g, f):
                    m = G[g][0]
                    n = g_counts(g)[1] + f
                    if f == 0:
                        pe.wait_ge(g_prob_done, 2 * g + 2)
                    if n >= 2:
                        pe.wait_ge(g_ptlo_done, n - 1)
                    cols = [(0, 0, 0), (0, 1, P), (1, 0, 2 * P), (1, 1, 3 * P)] if f < m else [(0, 0, 0), (0, 1, P), (1, 1, 2 * P)]
                    for c, qt, col in cols:
                        last = nc.tensor.transpose(ps_p[n % 2][:, col:col + P], g_row(g, qt)[:, (2 * f + c) * P:(2 * f + c + 1) * P], ident[:, :])
                    last.then_inc(g_pt_done, 1)

                def g_values(g, f):
                    m, hd = G[g]
                    n = g_counts(g)[1] + f
                    if f == 0 and g >= 2:
                        pe.wait_ge(g_a_done, g - 1)
                    if f == 0 and g < 2:
                        pe.wait_ge(a_done, at(END, 4, 2))
                    if f == 0 and g % 4 == 0:
                        pe.wait_ge(vlo_done, at((GLOBAL, m // 2), 1, 1))
                    pe.wait_ge(g_ptlo_done, n + 1)
                    for c in range(2):
                        for pt in (pt_hi, pt_lo):
                            moving = pt[:, 2, 0:BLOCK] if (f == m and c == 1) else pt[:, n % 2, c * BLOCK:(c + 1) * BLOCK]
                            last = nc.tensor.matmul(ps_o[:, hd * BLOCK:(hd + 1) * BLOCK], v_tok[:, 2 * f + c, hd, :], moving,
                                                    start=(f == 0 and c == 0 and pt is pt_hi), stop=(f == m and c == 1 and pt is pt_lo))
                    last.then_inc(g_pv_done, 1)

                pe.sem_inc(pv_done, 1)
                pe.wait_ge(ident_ready, 2)
                for t in range(2):
                    for m in range(3):
                        project((0, t), m, first=(t == 0))
                    transpose_v((0, t), first=(t == 0))
                for t in range(UNITS):
                    slot((0, t), first=(t == 0))
                with pe.Fori(1, LOCAL_PAIRS) as p:
                    for t in range(UNITS):
                        slot((p, t))
                for b in range(2):
                    g_scores(0, b)
                for f in range(3):
                    transpose_p(before(END), 1, f)
                side(-1)
                weighted_values(before(END), 1)
                for g, (m, hd) in enumerate(G):
                    nb = len(g_banks(g + 1))
                    for f in range(m + 1):
                        g_transpose(g, f)
                        for b in (2 * f, 2 * f + 1):
                            if b < nb:
                                g_scores(g + 1, b)
                        if f >= 1:
                            g_values(g, f - 1)
                    side(g)
                    g_values(g, m)

            @block.vector
            def _(dve):
                def weights_high(p, m, first=False):
                    if not first:
                        dve.wait_ge(proj_done, at((p - 1, UNITS - 1), 3, m + 1))
                    dve.wait_ge(w_loaded, p * 48 + 48)
                    nc.vector.tensor_copy(w_hi[:, m, :, :], w_raw[:, m, :, :]).then_inc(w_hi_done, 1)

                def row_max(unit, j, first=False):
                    lo, hi = job_cols(unit[1], j)
                    if j in (0, 4) and not first:
                        dve.wait_ge(pt_done, at(unit, 6, 3 * (j // 4) - 3))
                    dve.wait_ge(scores_done, at(unit, 8, j + 1))
                    settle(dve, dve_begun)
                    nc.vector.tensor_tensor_reduce(job_prob(j)[:, lo:hi], ps_s[j % 2][:, lo:hi], mask[:, 512 + P - (hi - lo):512 + P],
                                                   NEG_SCALE, 3e38, ALU.add, ALU.min, negmax[:, j:j + 1]).then_inc(max_done, 1)

                def reciprocals(unit, r):
                    dve.wait_ge(exp_done, at(unit, 8, 2 * r + 2))
                    nc.vector.reciprocal(rden[:, 2 * r:2 * r + 2], den[:, 2 * r:2 * r + 2]).then_inc(rden_done, 1)

                def rope_split(unit, first=False):
                    dve.wait_ge(mults_done, at(unit, 2, 2))
                    nc.vector.tensor_tensor(rsum[:, :, :], rsum[:, :, :], rot[:, :, :], ALU.add).then_inc(sum_done, 1)
                    if not first:
                        dve.wait_ge(stacked, at(unit, 128, 0))
                    dve.wait_ge(sum_done, at(unit, 1, 1))
                    nc.vector.tensor_copy(split[:, :, 0, :], rsum[:, :, :]).then_inc(rhi_done, 1)
                    dve.wait_ge(rhi_done, at(unit, 1, 1))
                    nc.vector.tensor_tensor(split[:, :, 1, :], rsum[:, :, :], f32(split[:, :, 0, :]), ALU.subtract).then_inc(rlo_done, 1)

                def v_lo(unit):
                    t = unit[1]
                    dve.wait_ge(vhi_done, at(unit, 1, 1))
                    v = v_tok[:, 4 * t:4 * t + 4, :, :]
                    nc.vector.tensor_tensor(v[:, :, :, D:2 * D], ps_v[:, :].rearrange("p (k h d) -> p k h d", k=4, h=2),
                                            f32(v[:, :, :, 0:D]), ALU.subtract).then_inc(vlo_done, 1)

                def p_lo(unit, b, f):
                    t = unit[1]
                    dve.wait_ge(pthi_done, at(unit, 6, 3 * b + f + 1))
                    src = ps_p[(3 * b + f) % 2]
                    if f < 2:
                        lo = first_tile(t, b) * BLOCK
                        nc.vector.tensor_tensor(pt_lo[:, f, lo:512], src[:, lo:512], f32(pt_hi[:, f, lo:512]), ALU.subtract).then_inc(ptlo_done, 1)
                    else:
                        hi = pt_hi[:, 2, :].rearrange("p (h q) -> p h q", h=2)[:, :, P:BLOCK]
                        out = pt_lo[:, 2, :].rearrange("p (h q) -> p h q", h=2)[:, :, P:BLOCK]
                        nc.vector.tensor_tensor(out, src[:, 0:BLOCK].rearrange("p (h q) -> p h q", h=2), f32(hi), ALU.subtract).then_inc(ptlo_done, 1)

                def join(unit, b):
                    t = unit[1]
                    cols = slice(b * BLOCK, (b + 1) * BLOCK)
                    if b == 0:
                        dve.wait_ge(a_stored, at(unit, 16, 16))
                    dve.wait_ge(half_done, at(unit, 4, 2 * b + 2))
                    nc.vector.tensor_tensor(a_out[0:D, t % 2, cols], ps_o[0:D, 0:BLOCK], half[0:D, :], ALU.add).then_inc(a_done, 1)
                    nc.vector.tensor_tensor(a_out[D:P, t % 2, cols], ps_o[D:P, BLOCK:2 * BLOCK], half[D:P, :], ALU.add).then_inc(a_done, 1)

                def slot(unit, first=False):
                    p, t = unit
                    last = before(unit)
                    row_max(unit, 0, first)
                    row_max(unit, 1)
                    if not first:
                        p_lo(last, 1, 0)
                        p_lo(last, 1, 1)
                    row_max(unit, 2)
                    row_max(unit, 3)
                    reciprocals(unit, 0)
                    if not first:
                        p_lo(last, 1, 2)
                    reciprocals(unit, 1)
                    rope_split(following(unit))
                    if not first:
                        join(last, 1)
                    row_max(unit, 4, first)
                    row_max(unit, 5)
                    p_lo(unit, 0, 0)
                    p_lo(unit, 0, 1)
                    row_max(unit, 6)
                    row_max(unit, 7)
                    reciprocals(unit, 2)
                    p_lo(unit, 0, 2)
                    reciprocals(unit, 3)
                    if t == 1:
                        for m in range(3):
                            weights_high(p + 1, m)
                    join(unit, 0)
                    v_lo(following(unit, 2))

                def g_row_max(g, b):
                    qt, i, (start, width, diagonal), row_done = g_banks(g)[b]
                    n = g_counts(g)[0] + b
                    c = 2 * (g % 2) + qt
                    if b == 0 and g < 2:
                        dve.wait_ge(pt_done, at(END, 6, -3 + 3 * g))
                    if b == 0 and g >= 2:
                        dve.wait_ge(g_pt_done, g_counts(g - 1)[1])
                    if b == 0 and g == 8:
                        dve.wait_ge(rlo_done, at((GLOBAL, UNITS), 1, 0))
                        dve.wait_ge(vlo_done, at((GLOBAL, UNITS), 1, 0))
                    if i == 0 and 2 * g + qt > 0:
                        dve.wait_ge(g_min_done, 2 * g + qt)
                    dve.wait_ge(g_scores_done, n + 1)
                    m0 = 512 + P - width if diagonal else 0
                    nc.vector.tensor_tensor_reduce(g_row(g, qt)[:, start:start + width], ps_s[n % 2][:, 0:width], mask[:, m0:m0 + width],
                                                   NEG_SCALE, 3e38, ALU.add, ALU.min, negmax[:, 4 + i:5 + i]).then_inc(g_max_done, 1)
                    if row_done:
                        dve.wait_ge(g_max_done, n + 1)
                        nc.vector.tensor_reduce(negmax[:, c:c + 1], negmax[:, 4:5 + i], AX_X, ALU.min).then_inc(g_min_done, 1)

                def g_reciprocal(g, qt):
                    c = 2 * (g % 2) + qt
                    dve.wait_ge(g_exp_done, 2 * g + qt + 1)
                    nc.vector.reciprocal(rden[:, c:c + 1], den[:, c:c + 1]).then_inc(g_rden_done, 1)

                def g_p_lo(g, f):
                    m = G[g][0]
                    n = g_counts(g)[1] + f
                    src = ps_p[n % 2]
                    dve.wait_ge(g_pthi_done, n + 1)
                    if f < m:
                        nc.vector.tensor_tensor(pt_lo[:, n % 2, :], src[:, :], f32(pt_hi[:, n % 2, :]), ALU.subtract).then_inc(g_ptlo_done, 1)
                    else:
                        nc.vector.tensor_tensor(pt_lo[:, n % 2, 0:BLOCK], src[:, 0:BLOCK], f32(pt_hi[:, n % 2, 0:BLOCK]), ALU.subtract)
                        nc.vector.tensor_tensor(pt_lo[:, 2, P:BLOCK], src[:, BLOCK:BLOCK + P], f32(pt_hi[:, 2, P:BLOCK]), ALU.subtract).then_inc(g_ptlo_done, 1)

                def g_join(g):
                    m, hd = G[g]
                    t = m // 2
                    rows = slice(D * hd, D * hd + D)
                    if g % 4 == 0:
                        if t < 2:
                            dve.wait_ge(a_stored, at(END, 16, 32))
                        else:
                            dve.wait_ge(g_a_stored[t % 2], 16 * (t // 2))
                    dve.wait_ge(g_half_done, g + 1)
                    nc.vector.tensor_tensor(a_out[rows, t % 2, (m % 2) * BLOCK:(m % 2 + 1) * BLOCK],
                                            ps_o[rows, hd * BLOCK:(hd + 1) * BLOCK], half[rows, :], ALU.add).then_inc(g_a_done, 1)

                dve.sem_inc(max_done, 2)
                dve.sem_inc(ptlo_done, 2)
                dve.sem_inc(a_done, 2)
                for m in range(3):
                    weights_high(0, m, first=True)
                rope_split((0, 0), first=True)
                v_lo((0, 0))
                v_lo((0, 1))
                dve.wait_ge(tables_loaded, 32)
                for t in range(UNITS):
                    slot((0, t), first=(t == 0))
                with dve.Fori(1, LOCAL_PAIRS) as p:
                    for t in range(UNITS):
                        slot((p, t))
                dve.wait_ge(zeros_ready, 2)
                for b in range(2):
                    g_row_max(0, b)
                for f in range(2):
                    p_lo(before(END), 1, f)
                for qt in range(2):
                    g_reciprocal(0, qt)
                p_lo(before(END), 1, 2)
                rope_split((GLOBAL, 1))
                join(before(END), 1)
                for g, (m, hd) in enumerate(G):
                    banks = g_banks(g + 1)
                    waiting = []
                    for f in range(m + 1):
                        issued = []
                        for b in (2 * f, 2 * f + 1):
                            if b < len(banks):
                                g_row_max(g + 1, b)
                                if banks[b][3]:
                                    issued.append(banks[b][0])
                        g_p_lo(g, f)
                        for qt in waiting:
                            g_reciprocal(g + 1, qt)
                        waiting = issued
                    for qt in waiting:
                        g_reciprocal(g + 1, qt)
                    if g in SIDE and SIDE[g][1] == 3:
                        rope_split(SIDE[g][0])
                        v_lo(SIDE[g][0])
                    g_join(g)


def stage_c(nc, x, wo, bo_rep, mods_dram, aT_dram, x1, hT_hi, hT_lo):
    with ExitStack() as ctx:
        def sb(name, shape, dt=F32):
            return ctx.enter_context(nc.sbuf_tensor(name, shape, dt))

        def sem(name):
            return ctx.enter_context(nc.semaphore(name))

        RC = 4
        PC = PAIRS // RC
        ident = sb("c_ident", [P, P])
        rows = sb("rows", [P, 3, HID])
        bias = sb("bias", [P, HID])
        WC = 8
        WP = PAIRS // WC
        wo_raw = sb("wo_raw", [P, 2, WP, HID])
        wo_hi = sb("wo_hi", [P, PAIRS, HID], F32R)
        wo_lo = sb("wo_lo", [P, PAIRS, HID], F32R)
        a_raw = sb("a_raw", [P, RC, PC, P])
        a_hi = sb("a_hi", [P, RC, PC, P], F32R)
        a_lo = sb("a_lo", [P, RC, PC, P], F32R)
        stats = sb("c_stats", [P, 2, 6])
        mv = sb("c_mv", [P, 2, 2])
        std = sb("c_std", [P, 2])
        rstd = sb("c_rstd", [P, 2])
        h = sb("c_h", [P, 2, HID])
        ps_y = [ctx.enter_context(nc.psum_tensor(f"ps_y{i}", [P, HID], F32)) for i in range(2)]
        ps_t = [ctx.enter_context(nc.psum_tensor(f"c_ps_t{i}", [P, HID], F32)) for i in range(2)]

        rows_loaded, ident_ready, bias_ready = sem("rows_loaded"), sem("c_ident_ready"), sem("bias_ready")
        wo_loaded = [sem("wo_loaded0"), sem("wo_loaded1")]
        wo_scaled, wo_hi_done, wo_split = sem("wo_scaled"), sem("wo_hi_done"), sem("wo_split")
        a_loaded = [sem(f"a_loaded{r}") for r in range(RC)]
        a_hi_done, a_split = sem("a_hi_done"), sem("a_split")
        x_loaded = sem("c_x_loaded")
        xb_done, y_done, x1_done = sem("xb_done"), sem("y_done"), sem("x1_done")
        stats_done, mv_done, std_done, rstd_done = sem("c_stats_done"), sem("c_mv_done"), sem("c_std_done"), sem("c_rstd_done")
        h_step, h_done = sem("c_h_step"), sem("c_h_done")
        t_done, hi_done, lo_done = sem("c_t_done"), sem("c_hi_done"), sem("c_lo_done")
        dve_begun, pool_begun, sp_begun, act_begun = sem("c_dve_begun"), sem("c_pool_begun"), sem("c_sp_begun"), sem("c_act_begun")

        def tile(n, i):
            return n * 2 + i

        with nc.Block() as block:
            @block.sync
            def _(sp):
                for k, j in enumerate((2, 3, 4)):
                    sp.dma_start(rows[:, k, :], mods_dram[j]).then_inc(rows_loaded, 16)
                sp.dma_start(bias[:, :], bo_rep).then_inc(rows_loaded, 16)
                def load_wo(r):
                    sp.dma_start(wo_raw[:, r % 2, :, :], wo[:, r * WP:(r + 1) * WP, :]).then_inc(wo_loaded[r % 2], 16)

                load_wo(0)
                load_wo(1)
                for r in range(RC):
                    sp.dma_start(a_raw[:, r, :, :], aT_dram[0, :, r * PC:(r + 1) * PC, :]).then_inc(a_loaded[r], 16)
                sp.dma_start(x1[:, :, :], x.rearrange("k p n -> p k n")).then_inc(x_loaded, 16)
                for r in range(2, WC):
                    sp.wait_ge(wo_split, r - 1)
                    load_wo(r)

                def load_next_a(n, i):
                    for r in range(RC):
                        sp.wait_ge(a_split, tile(n, i) * RC + (r + 1))
                        settle(sp, sp_begun)
                        sp.dma_start(a_raw[:, r, :, :], aT_dram[bass.ds(tile(n, i + 1), 1), :, r * PC:(r + 1) * PC, :]
                                     .rearrange("a p c n -> p (a c) n")).then_inc(a_loaded[r], 16)

                with sp.Fori(0, NT // 2 - 1) as n:
                    for i in range(2):
                        load_next_a(n, i)
                load_next_a(NT // 2 - 1, 0)

            @block.gpsimd
            def _(pool):
                make_identity(pool, ident, ident_ready)
                for r in range(WC):
                    pool.wait_ge(wo_hi_done, r + 1)
                    nc.gpsimd.tensor_tensor(wo_lo[:, r * WP:(r + 1) * WP, :], wo_raw[:, r % 2, :, :], f32(wo_hi[:, r * WP:(r + 1) * WP, :]),
                                            ALU.subtract).then_inc(wo_split, 1)
                pool.wait_ge(bias_ready, 1)
                pool.wait_ge(x_loaded, 16)

                def base(n, i):
                    for r in range(RC):
                        pool.wait_ge(a_hi_done, tile(n, i) * RC + (r + 1))
                        nc.gpsimd.tensor_tensor(a_lo[:, r, :, :], a_raw[:, r, :, :], f32(a_hi[:, r, :, :]), ALU.subtract).then_inc(a_split, 1)
                    row = x1[:, bass.ds(tile(n, i), 1), :].rearrange("p a n -> p (a n)")
                    nc.gpsimd.tensor_tensor(row, row, bias[:, :], ALU.add).then_inc(xb_done, 1)

                with pool.Fori(0, NT // 2) as n:
                    for i in range(2):
                        base(n, i)

            @block.scalar
            def _(act):
                for r in range(WC):
                    act.wait_ge(wo_scaled, r + 1)
                    nc.scalar.activation(wo_hi[:, r * WP:(r + 1) * WP, :], wo_raw[:, r % 2, :, :], ACT.Copy).then_inc(wo_hi_done, 1)

                def split(n, i, r):
                    act.wait_ge(y_done, tile(n, i) + 1)
                    act.wait_ge(a_loaded[r], tile(n, i) * 16 + 16)
                    nc.scalar.activation(a_hi[:, r, :, :], a_raw[:, r, :, :], ACT.Copy).then_inc(a_hi_done, 1)

                def norm(n, i):
                    act.wait_ge(mv_done, tile(n, i) + 1)
                    nc.scalar.activation(std[:, i:i + 1], mv[:, i, 1:2], ACT.Sqrt).then_inc(std_done, 1)
                    act.wait_ge(t_done, tile(n, i) + 1)
                    settle(act, act_begun)
                    nc.scalar.activation(hT_hi[:, :, bass.ds(tile(n, i) * P, P)],
                                         ps_t[i][:, :].rearrange("p (c t) -> p c t", c=HC), ACT.Copy).then_inc(hi_done, 1)

                for r in range(RC):
                    split(0, 0, r)
                with act.Fori(0, NT // 2 - 1) as n:
                    for i in range(2):
                        for r in range(RC):
                            split(n, i + 1, r)
                        norm(n, i)
                for r in range(RC):
                    split(NT // 2 - 1, 1, r)
                norm(NT // 2 - 1, 0)
                norm(NT // 2 - 1, 1)

            @block.tensor
            def _(pe):
                def product(n, i, first=False):
                    pe.wait_ge(x1_done, tile(n, i) + 1)
                    bank = ps_y[i % 2]
                    for r in range(RC):
                        if first:
                            pe.wait_ge(wo_split, (r + 1) * WC // RC)
                        pe.wait_ge(a_split, tile(n, i) * RC + (r + 1))
                        for a, w in ((a_hi, wo_hi), (a_hi, wo_lo), (a_lo, wo_hi)):
                            for c in range(PC):
                                k = (a is a_lo, w is wo_lo, r, c)
                                last = nc.tensor.matmul(bank[:, :], a[:, r, c, :], w[:, r * PC + c, :],
                                                        start=(k == (False, False, 0, 0)), stop=(k == (True, False, RC - 1, PC - 1)))
                    last.then_inc(y_done, 1)

                def transposes(n, i):
                    pe.wait_ge(h_done, tile(n, i) + 1)
                    pe.wait_ge(lo_done, tile(n, i) + 1)
                    for c in range(HC):
                        last = nc.tensor.transpose(ps_t[i][:, c * P:(c + 1) * P], h[:, i, c * P:(c + 1) * P], ident[:, :])
                    last.then_inc(t_done, 1)

                pe.sem_inc(y_done, 1)
                pe.wait_ge(ident_ready, 2)
                product(0, 0, first=True)
                with pe.Fori(0, NT // 2 - 1) as n:
                    for i in range(2):
                        product(n, i + 1)
                        transposes(n, i)
                product(NT // 2 - 1, 1)
                transposes(NT // 2 - 1, 0)
                transposes(NT // 2 - 1, 1)

            @block.vector
            def _(dve):
                dve.sem_inc(x1_done, 2)
                dve.sem_inc(lo_done, 2)
                dve.wait_ge(rows_loaded, 64)
                nc.vector.tensor_tensor(bias[:, :], bias[:, :], rows[:, 0, :], ALU.mult).then_inc(bias_ready, 1)
                for r in range(WC):
                    dve.wait_ge(wo_loaded[r % 2], 16 * (r // 2) + 16)
                    nc.vector.tensor_tensor(wo_raw[:, r % 2, :, :], wo_raw[:, r % 2, :, :], rows[:, 0:1, :].broadcast_to([P, WP, HID]),
                                            ALU.mult).then_inc(wo_scaled, 1)

                def residual_norm(n, i):
                    tok_tile = tile(n, i)
                    x1_tile = x1[:, bass.ds(tok_tile, 1), :].rearrange("p a n -> p (a n)")
                    dve.wait_ge(xb_done, tok_tile + 1)
                    dve.wait_ge(y_done, tok_tile + 2)
                    settle(dve, dve_begun)
                    nc.vector.tensor_tensor(x1_tile, ps_y[i][:, :], x1_tile, ALU.add).then_inc(x1_done, 1)
                    dve.wait_ge(x1_done, tok_tile + 3)
                    settle(dve, dve_begun)
                    nc.vector.bn_stats(stats[:, i, :], x1_tile).then_inc(stats_done, 1)
                    dve.wait_ge(stats_done, tok_tile * 2 + 1)
                    settle(dve, dve_begun)
                    nc.vector.bn_aggr(mv[:, i, :], stats[:, i, :]).then_inc(stats_done, 1)
                    dve.wait_ge(stats_done, tok_tile * 2 + 2)
                    nc.vector.tensor_scalar(mv[:, i, 1:2], mv[:, i, 1:2], EPS, None, ALU.add).then_inc(mv_done, 1)
                    dve.wait_ge(std_done, tok_tile + 1)
                    nc.vector.reciprocal(rstd[:, i:i + 1], std[:, i:i + 1]).then_inc(rstd_done, 1)
                    dve.wait_ge(rstd_done, tok_tile + 1)
                    settle(dve, dve_begun)
                    nc.vector.tensor_scalar(h[:, i, :], x1_tile, mv[:, i, 0:1], rstd[:, i:i + 1], ALU.subtract, ALU.mult).then_inc(h_step, 1)
                    dve.wait_ge(h_step, tok_tile * 2 + 1)
                    nc.vector.tensor_tensor(h[:, i, :], h[:, i, :], rows[:, 2, :], ALU.mult).then_inc(h_step, 1)
                    dve.wait_ge(h_step, tok_tile * 2 + 2)
                    nc.vector.tensor_tensor(h[:, i, :], h[:, i, :], rows[:, 1, :], ALU.add).then_inc(h_done, 1)

                def low_part(n, i):
                    cols = bass.ds(tile(n, i) * P, P)
                    dve.wait_ge(hi_done, tile(n, i) + 1)
                    settle(dve, dve_begun)
                    nc.vector.tensor_tensor(hT_lo[:, :, cols], ps_t[i][:, :].rearrange("p (c t) -> p c t", c=HC),
                                            f32(hT_hi[:, :, cols]), ALU.subtract).then_inc(lo_done, 1)

                with dve.Fori(0, NT // 2) as n:
                    for i in range(2):
                        residual_norm(n, i)
                        low_part(n, i)


def stage_d(nc, wg, wu, wd, mods_dram, out, x1, hT_hi, hT_lo):
    with ExitStack() as ctx:
        def sb(name, shape, dt=F32):
            return ctx.enter_context(nc.sbuf_tensor(name, shape, dt))

        def sem(name):
            return ctx.enter_context(nc.semaphore(name))

        def bank(name):
            return ctx.enter_context(nc.psum_tensor(name, [P, UT], F32))

        GC = INNER // (4 * P)
        J = 4
        gate_b = sb("gate_b", [P, HID])
        gu_raw = sb("gu_raw", [P, 2, 2, HC, P])
        gu_hi = sb("gu_hi", [P, J, 2, HC, P], F32R)
        gu_lo = sb("gu_lo", [P, J, 2, HC, P], F32R)
        wd_raw = sb("wd_raw", [P, 2, HID])
        wd_hi = sb("wd_hi", [P, J, HID], F32R)
        wd_lo = sb("wd_lo", [P, J, HID], F32R)
        silu = sb("silu", [P, 2, UT])
        h = sb("d_h", [P, J, UT])
        mag = sb("d_mag", [P, J, UT])
        ge = sb("ge", [P, 6, UT], BF16)
        rank = sb("rank", [P, J, UT], BF16)
        hs_hi = sb("hs_hi", [P, J, UT], F32R)
        hs_lo = sb("hs_lo", [P, J, UT], F32R)
        ps_g = [bank(f"ps_g{i}") for i in range(2)]
        ps_u = [bank(f"ps_u{i}") for i in range(2)]
        ps_d = [bank(f"ps_d{i}") for i in range(2)]

        gate_loaded = sem("gate_loaded")
        gu_loaded, gu_hi_done, gu_split = [sem("gu_loaded0"), sem("gu_loaded1")], sem("gu_hi_done"), sem("gu_split")
        wd_loaded, wd_scaled, wd_hi_done, wd_split = [sem("wd_loaded0"), sem("wd_loaded1")], sem("wd_scaled"), sem("wd_hi_done"), sem("wd_split")
        g_done, u_done, silu_done, h_done = sem("g_done"), sem("u_done"), sem("silu_done"), sem("d_h_done")
        mag_done, ge_done, rank_step, kept_done = sem("mag_done"), sem("ge_done"), sem("rank_step"), sem("kept_done")
        hs_hi_done, hs_lo_done = sem("hs_hi_done"), sem("hs_lo_done")
        down_done, added, stored = sem("down_done"), sem("added"), sem("stored")
        pool_begun, sp_begun, dve_begun = sem("d_pool_begun"), sem("d_sp_begun"), sem("d_dve_begun")

        def at(unit, per, count):
            g, t = unit
            return g * (UNITS * per) + (t * per + count)

        def following(unit):
            g, t = unit
            return (g, t + 1) if t + 1 < UNITS else (g + 1, 0)

        with nc.Block() as block:
            @block.sync
            def _(sp):
                def load_gu(g, j, first=False):
                    if isinstance(g, int):
                        chunk = slice(g, g + 1)
                    else:
                        chunk = bass.ds(sp.snap(g), 1)
                    if not first or j >= 2:
                        sp.wait_ge(gu_split, g * J + (j - 1))
                        settle(sp, sp_begun)
                    for i, w in enumerate((wg, wu)):
                        sp.dma_start(gu_raw[:, j % 2, i, :, :], w[chunk, :, j, :, :].rearrange("a p c n -> p (a c) n")).then_inc(gu_loaded[j % 2], 16)

                def load_wd(g, j, first=False):
                    if isinstance(g, int):
                        chunk = slice(g, g + 1)
                    else:
                        chunk = bass.ds(sp.snap(g), 1)
                    if not first or j >= 2:
                        sp.wait_ge(wd_split, g * J + (j - 1))
                        settle(sp, sp_begun)
                    sp.dma_start(wd_raw[:, j % 2, :], wd[chunk, :, j, :].rearrange("a p n -> p (a n)")).then_inc(wd_loaded[j % 2], 16)

                sp.dma_start(gate_b[:, :], mods_dram[5]).then_inc(gate_loaded, 16)
                for j in range(J):
                    load_gu(0, j, first=True)
                for j in range(J):
                    load_wd(0, j, first=True)
                with sp.Fori(0, GC - 1) as g:
                    for j in range(J):
                        load_gu(g + 1, j)
                    for j in range(J):
                        load_wd(g + 1, j)
                for t in range(UNITS):
                    for k in range(4):
                        sp.wait_ge(added, at((GC - 1, t), 4, k + 1) + 2)
                        sp.dma_start(out[4 * t + k], x1[:, 4 * t + k, :]).then_inc(stored, 16)
                sp.wait_ge(stored, 16 * NT)

            @block.gpsimd
            def _(pool):
                def gu_low(g, j):
                    pool.wait_ge(gu_hi_done, g * J + (j + 1))
                    nc.gpsimd.tensor_tensor(gu_lo[:, j], gu_raw[:, j % 2], f32(gu_hi[:, j]), ALU.subtract).then_inc(gu_split, 1)

                def wd_scale(g, j):
                    pool.wait_ge(wd_loaded[j % 2], g * 32 + (16 * (j // 2) + 16))
                    nc.gpsimd.tensor_tensor(wd_raw[:, j % 2, :], wd_raw[:, j % 2, :], gate_b[:, :], ALU.mult).then_inc(wd_scaled, 1)

                def wd_low(g, j):
                    pool.wait_ge(wd_hi_done, g * J + (j + 1))
                    nc.gpsimd.tensor_tensor(wd_lo[:, j, :], wd_raw[:, j % 2, :], f32(wd_hi[:, j, :]), ALU.subtract).then_inc(wd_split, 1)

                pool.wait_ge(gate_loaded, 16)
                for j in range(J):
                    gu_low(0, j)
                for j in range(J):
                    wd_scale(0, j)
                    wd_low(0, j)
                with pool.Fori(0, GC - 1) as g:
                    for j in range(J):
                        gu_low(g + 1, j)
                    for j in range(J):
                        wd_scale(g + 1, j)
                        wd_low(g + 1, j)

            @block.scalar
            def _(act):
                def gu_high(g, j, first=False):
                    if not first:
                        act.wait_ge(u_done, (g - 1) * (UNITS * J) + ((UNITS - 1) * J + j + 1))
                    act.wait_ge(gu_loaded[j % 2], g * 64 + (32 * (j // 2) + 32))
                    nc.scalar.activation(gu_hi[:, j], gu_raw[:, j % 2], ACT.Copy).then_inc(gu_hi_done, 1)

                def wd_high(g, j, first=False):
                    if not first:
                        act.wait_ge(down_done, g * (UNITS * 4) + 1)
                    act.wait_ge(wd_scaled, g * J + (j + 1))
                    nc.scalar.activation(wd_hi[:, j, :], wd_raw[:, j % 2, :], ACT.Copy).then_inc(wd_hi_done, 1)

                def silus(unit, j):
                    act.wait_ge(g_done, at(unit, 4, j + 1))
                    act.wait_ge(h_done, at(unit, 4, j + 1))
                    nc.scalar.activation(silu[:, j % 2, :], ps_g[j % 2][:, :], ACT.Silu).then_inc(silu_done, 1)

                def magnitudes(unit):
                    act.wait_ge(h_done, at(unit, 4, 4 + 2))
                    nc.scalar.activation(mag[:, :, :], h[:, :, :], ACT.Abs).then_inc(mag_done, 1)

                def kept_high(unit):
                    act.wait_ge(down_done, at(unit, 4, 1))
                    act.wait_ge(kept_done, at(unit, 4, 4))
                    nc.scalar.activation(hs_hi[:, :, :], mag[:, :, :], ACT.Copy).then_inc(hs_hi_done, 1)

                for j in range(J):
                    gu_high(0, j, first=True)
                for j in range(J):
                    silus((0, 0), j)
                for j in range(J):
                    wd_high(0, j, first=True)

                def slot(unit, last=False):
                    g, t = unit
                    nxt = following(unit)
                    magnitudes(unit)
                    kept_high(unit)
                    if t == 0 and not (isinstance(g, int) and g == 0):
                        pass
                    if not last:
                        for j in range(J):
                            silus(nxt, j)
                            if t == UNITS - 2 and not (isinstance(g, int) and g == GC - 1):
                                gu_high(g + 1, j)
                    if t == UNITS - 1 and not (isinstance(g, int) and g == GC - 1):
                        for j in range(J):
                            wd_high(g + 1, j)

                with act.Fori(0, GC - 1) as g:
                    for t in range(UNITS):
                        slot((g, t))
                for t in range(UNITS):
                    slot((GC - 1, t), last=(t == UNITS - 1))

            @block.tensor
            def _(pe):
                def gate_up(unit):
                    g, t = unit
                    cols = slice(t * UT, (t + 1) * UT)
                    for j in range(J):
                        if t == 0:
                            pe.wait_ge(gu_split, g * J + (j + 1))
                        pe.wait_ge(h_done, at(unit, 4, j + 1))
                        for i, (bank, done) in enumerate(((ps_g, g_done), (ps_u, u_done))):
                            k = 0
                            for w, hT in ((gu_hi, hT_hi), (gu_hi, hT_lo), (gu_lo, hT_hi)):
                                for c in range(HC):
                                    last = nc.tensor.matmul(bank[j % 2][:, :], w[:, j, i, c, :], hT[:, c, cols], start=(k == 0), stop=(k == 3 * HC - 1))
                                    k += 1
                            last.then_inc(done, 1)

                def down(unit):
                    g, t = unit
                    pe.wait_ge(hs_lo_done, at(unit, 1, 1))
                    if t == 0:
                        pe.wait_ge(wd_split, g * J + J)
                    for n in range(4):
                        pe.wait_ge(added, at(unit, 4, n + 1))
                        k = 0
                        for a, w in ((hs_hi, wd_hi), (hs_hi, wd_lo), (hs_lo, wd_hi)):
                            for j in range(J):
                                last = nc.tensor.matmul(ps_d[n % 2][:, :], a[:, j, n * P:(n + 1) * P], w[:, j, :], start=(k == 0), stop=(k == 3 * J - 1))
                                k += 1
                        last.then_inc(down_done, 1)

                pe.sem_inc(down_done, 1)
                gate_up((0, 0))
                with pe.Fori(0, GC - 1) as g:
                    for t in range(UNITS):
                        gate_up(following((g, t)))
                        down((g, t))
                for t in range(UNITS):
                    if t + 1 < UNITS:
                        gate_up((GC - 1, t + 1))
                    down((GC - 1, t))

            @block.vector
            def _(dve):
                def members(unit, j):
                    dve.wait_ge(u_done, at(unit, 4, j + 1))
                    dve.wait_ge(silu_done, at(unit, 4, j + 1))
                    nc.vector.tensor_tensor(h[:, j, :], ps_u[j % 2][:, :], silu[:, j % 2, :], ALU.mult).then_inc(h_done, 1)

                def select(unit):
                    dve.wait_ge(mag_done, at(unit, 1, 1))
                    g0 = 0
                    for i, n in ((0, 3), (1, 2), (2, 1)):
                        nc.vector.tensor_tensor(ge[:, g0:g0 + n, :], mag[:, i:i + 1, :].broadcast_to([P, n, UT]), mag[:, i + 1:i + 1 + n, :], ALU.is_ge).then_inc(ge_done, 1)
                        g0 += n
                    dve.wait_ge(ge_done, at(unit, 3, 3))
                    steps = [(0, 0, 1, ALU.add), (1, 3, 4, ALU.add), (2, 5, 1, ALU.subtract), (3, 2, 4, ALU.add)]
                    for j, a, b, op in steps:
                        nc.vector.tensor_tensor(rank[:, j, :], ge[:, a, :], ge[:, b, :], op).then_inc(rank_step, 1)
                    for n, (j, b, op) in enumerate(((0, 2, ALU.add), (1, 0, ALU.subtract), (2, 3, ALU.subtract), (3, 5, ALU.add))):
                        dve.wait_ge(rank_step, at(unit, 8, 4 + n))
                        nc.vector.tensor_tensor(rank[:, j, :], rank[:, j, :], ge[:, b, :], op).then_inc(rank_step, 1)
                    for n, (j, bound, op) in enumerate(((0, 1.5, ALU.is_ge), (1, 0.5, ALU.is_ge), (2, -0.5, ALU.is_ge), (3, 1.5, ALU.is_le))):
                        if n == 0:
                            dve.wait_ge(rank_step, at(unit, 8, 8))
                        nc.vector.scalar_tensor_tensor(mag[:, j, :], rank[:, j, :], bound, h[:, j, :], op, ALU.mult).then_inc(kept_done, 1)

                def kept_low(unit):
                    dve.wait_ge(hs_hi_done, at(unit, 1, 1))
                    nc.vector.tensor_tensor(hs_lo[:, :, :], mag[:, :, :], f32(hs_hi[:, :, :]), ALU.subtract).then_inc(hs_lo_done, 1)

                def accumulate(unit, n):
                    dve.wait_ge(down_done, at(unit, 4, n + 1 + 1))
                    tile = x1[:, 4 * unit[1] + n, :]
                    nc.vector.tensor_tensor(tile, ps_d[n % 2][:, :], tile, ALU.add).then_inc(added, 1)

                dve.sem_inc(h_done, 2)
                dve.sem_inc(added, 2)
                for j in range(J):
                    members((0, 0), j)

                def slot(unit, last=False):
                    select(unit)
                    kept_low(unit)
                    if not last:
                        for j in range(J):
                            members(following(unit), j)
                    for n in range(4):
                        accumulate(unit, n)

                with dve.Fori(0, GC - 1) as g:
                    for t in range(UNITS):
                        slot((g, t))
                for t in range(UNITS):
                    slot((GC - 1, t), last=(t == UNITS - 1))


def block_program(nc, x, c_cols, wmod, wq, wk, wv, wo, bo_rep, wg, wu, wd, rope, masks, out):
    mods_dram = nc.dram_tensor("mods_scratch", [6, P, HID], F32, kind="Internal").ap()
    aT_dram = nc.dram_tensor("aT_scratch", [NT, P, PAIRS, P], F32, kind="Internal").ap()
    with ExitStack() as ctx:
        hT_hi = ctx.enter_context(nc.sbuf_tensor("hT_hi", [P, HC, TOK], F32R))
        hT_lo = ctx.enter_context(nc.sbuf_tensor("hT_lo", [P, HC, TOK], F32R))
        stage_a(nc, x, c_cols, wmod, mods_dram, hT_hi, hT_lo)
        stage_b(nc, wq, wk, wv, rope, masks, aT_dram, hT_hi, hT_lo)
        x1 = ctx.enter_context(nc.sbuf_tensor("x1", [P, NT, HID], F32))
        stage_c(nc, x, wo, bo_rep, mods_dram, aT_dram, x1, hT_hi, hT_lo)
        stage_d(nc, wg, wu, wd, mods_dram, out, x1, hT_hi, hT_lo)


def rope_tables():
    inv_freq = (1.0 / 10000.0 ** (np.arange(0, D, 2, dtype=np.float32) / np.float32(D))).astype(np.float32)
    freqs = np.arange(TOK, dtype=np.float32)[None, :] * inv_freq[:, None]
    cos, sin = np.cos(freqs), np.sin(freqs)
    return np.stack([np.tile(cos, (4, 1)), np.tile(np.concatenate([-sin, sin]), (2, 1))]).astype(np.float32)


def mask_table():
    m = np.zeros((P, 512 + P), np.float32)
    m[:, 512:] = np.where(np.arange(P)[:, None] >= np.arange(P)[None, :], 0.0, MASKED)
    return m


def laid_out(x, Wq, Wk, Wv, Wo, bo, w_gate, w_up, w_down, c, wmod):
    def pairs(w):
        return w.reshape(PAIRS, P, HC, P).transpose(0, 3, 2, 1)

    def members(w):
        return w.reshape(HC, P, INNER // (4 * P), P, 4).transpose(2, 1, 4, 0, 3)

    return {
        "x": x.reshape(NT, P, HID),
        "c_cols": c.reshape(HC, P).T,
        "wmod": wmod,
        "wq": pairs(Wq), "wk": pairs(Wk), "wv": pairs(Wv),
        "wo": Wo.T.reshape(PAIRS, P, HID).transpose(1, 0, 2),
        "bo_rep": np.broadcast_to(bo, (P, HID)),
        "wg": members(w_gate), "wu": members(w_up),
        "wd": w_down.reshape(INNER // (4 * P), P, 4, HID),
        "rope": rope_tables(), "masks": mask_table(),
    }


def kernel(L0_attn_hidden_states, L0_attn_Wq, L0_attn_Wk, L0_attn_Wv, L0_attn_Wo, L0_attn_bo,
           L0_ffn_w_gate, L0_ffn_w_up, L0_ffn_w_down, L0_c, L0_wmod):
    import concourse.bacc as bacc
    from concourse.bass_utils import run_bass_kernel_spmd

    nc = bacc.Bacc("TRN2", target_bir_lowering=False, num_devices=1)
    arrays = {n: np.ascontiguousarray(a) for n, a in laid_out(
        np.asarray(L0_attn_hidden_states), np.asarray(L0_attn_Wq), np.asarray(L0_attn_Wk), np.asarray(L0_attn_Wv),
        np.asarray(L0_attn_Wo), np.asarray(L0_attn_bo), np.asarray(L0_ffn_w_gate), np.asarray(L0_ffn_w_up),
        np.asarray(L0_ffn_w_down), np.asarray(L0_c), np.asarray(L0_wmod)).items()}
    args = {n: nc.dram_tensor(n, a.shape, F32, kind="ExternalInput").ap() for n, a in arrays.items()}
    out = nc.dram_tensor("out", (NT, P, HID), F32, kind="ExternalOutput").ap()
    block_program(nc, out=out, **args)
    r = run_bass_kernel_spmd(nc, [arrays], core_ids=[0])
    return r.results[0]["out"].reshape(1, TOK, HID)
```

```python
from contextlib import ExitStack

import numpy as np

import concourse.bass as bass
from concourse import mybir

F32 = mybir.dt.float32
F32R = mybir.dt.float32r
BF16 = mybir.dt.bfloat16
ALU = mybir.AluOpType
ACT = mybir.ActivationFunctionType
AX_X = mybir.AxisListType.X

P = 128
TOK = 2048
HID = 512
HC = HID // P
NT = TOK // P
UT = 512
UNITS = TOK // UT
HEADS = 32
D = 64
PAIRS = HEADS // 2
LOCAL_PAIRS = PAIRS - 1
INNER = 2048
BLOCK = 256
LOOKBACK = 128
EPS = 1e-5
GATE_MIN = 0.25
MASKED = -1e30
SCALE = 1.0 / D ** 0.5
NEG_SCALE = -SCALE


def f32(ap):
    return ap.bitcast(F32)


def settle(eng, begun):
    eng.sem_inc(begun, 1)


def make_identity(pool, ident, done):
    pool.memset(ident[:, :], 0.0).then_inc(done, 1)
    pool.wait_ge(done, 1)
    pool.affine_select(out=ident[:, :], in_=ident[:, :], compare_op=ALU.not_equal, fill=1.0,
                       base=0, pattern=[[-1, P]], channel_multiplier=1).then_inc(done, 1)


def stage_a(nc, x, c_cols, wmod, mods_dram, hT_hi, hT_lo):
    with ExitStack() as ctx:
        def sb(name, shape, dt=F32):
            return ctx.enter_context(nc.sbuf_tensor(name, shape, dt))

        def sem(name):
            return ctx.enter_context(nc.semaphore(name))

        GT = 4
        GROUPS = NT // GT
        ROWS = 6
        ident = sb("a_ident", [P, P])
        c_sb = sb("c_sb", [P, HC])
        silu_c = sb("silu_c", [P, HC])
        ones = sb("ones", [P, P])
        silu_rep = sb("silu_rep", [P, HC, P])
        wm = sb("wm", [P, HC, ROWS * HID])
        mods = sb("mods_sb", [P, ROWS, HID])
        sign = sb("sign", [P, 2, HID])
        mag = sb("mag", [P, 2, HID])
        xt = sb("xt", [P, NT, HID])
        stats = sb("stats", [P, GT, 6])
        mv = sb("mv", [P, GT, 2])
        std = sb("std", [P, GT])
        rstd = sb("rstd", [P, GT])
        ps_mod = [ctx.enter_context(nc.psum_tensor(f"ps_mod{j}", [P, HID], F32)) for j in range(ROWS)]
        ps_t = [ctx.enter_context(nc.psum_tensor(f"ps_t{i}", [P, HID], F32)) for i in range(2)]

        c_loaded, ident_ready = sem("c_loaded"), sem("a_ident_ready")
        wm_loaded = [sem(f"wm_loaded{j}") for j in range(ROWS)]
        silu_ready, ones_ready, rep_ready = sem("silu_ready"), sem("ones_ready"), sem("rep_ready")
        mod_done, shift_ready, scale_ready = sem("mod_done"), sem("shift_ready"), sem("scale_ready")
        gate_step, row_final = sem("gate_step"), [sem(f"row_final{j}") for j in range(ROWS)]
        mods_stored, dve_begun, sp_begun, pool_begun = sem("mods_stored"), sem("a_dve_begun"), sem("a_sp_begun"), sem("a_pool_begun")
        x_loaded = [sem(f"x_loaded{i}") for i in range(GT)]
        stats_done, mv_done, std_done, rstd_done = sem("stats_done"), sem("mv_done"), sem("std_done"), sem("rstd_done")
        xn_done, scaled_done, h_done = sem("xn_done"), sem("scaled_done"), sem("h_done")
        t_done, hi_done, lo_done = sem("t_done"), sem("hi_done"), sem("lo_done")

        def tile(n, i):
            return n * GT + i

        def x_tile(n, i):
            return xt[:, bass.ds(tile(n, i), 1), :].rearrange("p a n -> p (a n)")

        with nc.Block() as block:
            @block.sync
            def _(sp):
                def load_row(j):
                    sp.dma_start(wm[:, :, j * HID:(j + 1) * HID], wmod[:, j * HID:(j + 1) * HID].rearrange("(c p) n -> p c n", p=P)).then_inc(wm_loaded[j], 16)

                sp.dma_start(c_sb[:, :], c_cols).then_inc(c_loaded, 16)
                for i in range(GT):
                    sp.dma_start(xt[:, i, :], x[i]).then_inc(x_loaded[i], 16)
                load_row(0)
                load_row(1)

                def load_group(n):
                    for i in range(GT):
                        t = tile(n, i) if isinstance(n, int) else sp.snap(tile(n, i))
                        sp.wait_ge(stats_done, (t - i) * 2 - 2 * GT + (i + 1))
                        settle(sp, sp_begun)
                        sp.dma_start(xt[:, bass.ds(t, 1), :].rearrange("p a n -> p (a n)"),
                                     x[bass.ds(t, 1)].rearrange("a p n -> p (a n)")).then_inc(x_loaded[i], 16)
                load_group(1)
                load_row(2)
                load_row(3)
                with sp.Fori(2, GROUPS) as n:
                    load_group(n)
                for j in range(4, ROWS):
                    load_row(j)
                for j in (2, 4, 3, 5):
                    sp.wait_ge(row_final[j], 1)
                    sp.dma_start(mods_dram[j], mods[:, j, :]).then_inc(mods_stored, 16)
                sp.wait_ge(mods_stored, 16 * (ROWS - 2))

            @block.gpsimd
            def _(pool):
                make_identity(pool, ident, ident_ready)
                pool.wait_ge(shift_ready, 1)
                with pool.Fori(0, GROUPS) as n:
                    for i in range(GT):
                        pool.wait_ge(scaled_done, tile(n, i) + 1)
                        settle(pool, pool_begun)
                        nc.gpsimd.tensor_tensor(x_tile(n, i), x_tile(n, i), mods[:, 0, :], ALU.add).then_inc(h_done, 1)

            @block.scalar
            def _(act):
                def deviations(n):
                    for i in range(GT):
                        act.wait_ge(mv_done, tile(n, i) + 1)
                        nc.scalar.activation(std[:, i:i + 1], mv[:, i, 1:2], ACT.Sqrt).then_inc(std_done, 1)

                def high_parts(n):
                    for i in range(GT):
                        act.wait_ge(t_done, tile(n, i) + 1)
                        act.wait_ge(ident_ready, 2)
                        nc.scalar.activation(hT_hi[:, :, bass.ds(tile(n, i) * P, P)],
                                             ps_t[i % 2][:, :].rearrange("p (c t) -> p c t", c=HC), ACT.Copy).then_inc(hi_done, 1)

                act.wait_ge(c_loaded, 16)
                nc.scalar.activation(silu_c[:, :], c_sb[:, :], ACT.Silu).then_inc(silu_ready, 1)
                deviations(0)
                deviations(1)
                act.wait_ge(mod_done, 1)
                nc.scalar.activation(mods[:, 0, :], ps_mod[0][:, :], ACT.Copy).then_inc(shift_ready, 1)
                with act.Fori(0, GROUPS - 2) as n:
                    deviations(n + 2)
                    high_parts(n)
                for n in (GROUPS - 2, GROUPS - 1):
                    high_parts(n)
                act.wait_ge(mod_done, 4)
                nc.scalar.activation(mods[:, 3, :], ps_mod[3][:, :], ACT.Copy).then_inc(row_final[3], 1)

            @block.tensor
            def _(pe):
                def mod_row(j):
                    pe.wait_ge(wm_loaded[j], 16)
                    for c in range(HC):
                        last = nc.tensor.matmul(ps_mod[j][:, :], silu_rep[:, c, :], wm[:, c, j * HID:(j + 1) * HID],
                                                start=(c == 0), stop=(c == HC - 1))
                    last.then_inc(mod_done, 1)

                pe.wait_ge(rep_ready, HC)
                mod_row(0)
                mod_row(1)
                pe.wait_ge(ident_ready, 2)
                for t in range(NT):
                    pe.wait_ge(h_done, t + 1)
                    pe.wait_ge(lo_done, t + 1)
                    for c in range(HC):
                        last = nc.tensor.transpose(ps_t[t % 2][:, c * P:(c + 1) * P], xt[:, t, c * P:(c + 1) * P], ident[:, :])
                    last.then_inc(t_done, 1)
                    if t in (GT - 1, 2 * GT - 1):
                        for j in range(2):
                            mod_row(2 + 2 * (t // GT) + j)

            @block.vector
            def _(dve):
                def normalize(n):
                    for i in range(GT):
                        dve.wait_ge(x_loaded[i], n * 16 + 16)
                        settle(dve, dve_begun)
                        nc.vector.bn_stats(stats[:, i, :], x_tile(n, i)).then_inc(stats_done, 1)
                    for i in range(GT):
                        dve.wait_ge(stats_done, n * (2 * GT) + (i + 1))
                        settle(dve, dve_begun)
                        nc.vector.bn_aggr(mv[:, i, :], stats[:, i, :]).then_inc(stats_done, 1)
                    for i in range(GT):
                        dve.wait_ge(stats_done, n * (2 * GT) + (GT + i + 1))
                        nc.vector.tensor_scalar(mv[:, i, 1:2], mv[:, i, 1:2], EPS, None, ALU.add).then_inc(mv_done, 1)
                    for i in range(GT):
                        dve.wait_ge(std_done, tile(n, i) + 1)
                        nc.vector.reciprocal(rstd[:, i:i + 1], std[:, i:i + 1]).then_inc(rstd_done, 1)
                    for i in range(GT):
                        dve.wait_ge(rstd_done, tile(n, i) + 1)
                        settle(dve, dve_begun)
                        nc.vector.tensor_scalar(x_tile(n, i), x_tile(n, i), mv[:, i, 0:1], rstd[:, i:i + 1], ALU.subtract, ALU.mult).then_inc(xn_done, 1)

                def scale(n):
                    for i in range(GT):
                        dve.wait_ge(xn_done, tile(n, i) + 1)
                        settle(dve, dve_begun)
                        nc.vector.tensor_tensor(x_tile(n, i), x_tile(n, i), mods[:, 1, :], ALU.mult).then_inc(scaled_done, 1)

                def low_parts(n):
                    for i in range(GT):
                        dve.wait_ge(hi_done, tile(n, i) + 1)
                        settle(dve, dve_begun)
                        cols = bass.ds(tile(n, i) * P, P)
                        nc.vector.tensor_tensor(hT_lo[:, :, cols], ps_t[i % 2][:, :].rearrange("p (c t) -> p c t", c=HC),
                                                f32(hT_hi[:, :, cols]), ALU.subtract).then_inc(lo_done, 1)

                def add_one(j, done):
                    dve.wait_ge(mod_done, j + 1)
                    nc.vector.tensor_scalar(mods[:, j, :], ps_mod[j][:, :], 1.0, None, ALU.add).then_inc(done, 1)

                def gate(k, j):
                    dve.wait_ge(mod_done, j + 1)
                    nc.vector.tensor_scalar(sign[:, k, :], ps_mod[j][:, :], 0.0, 2.0, ALU.is_ge, ALU.mult).then_inc(gate_step, 1)
                    nc.vector.tensor_scalar(mag[:, k, :], ps_mod[j][:, :], -1.0, GATE_MIN, ALU.mult, ALU.max).then_inc(gate_step, 1)
                    dve.wait_ge(gate_step, 3 * k + 2)
                    nc.vector.tensor_tensor(mag[:, k, :], mag[:, k, :], ps_mod[j][:, :], ALU.max).then_inc(gate_step, 1)
                    dve.wait_ge(gate_step, 3 * k + 3)
                    nc.vector.scalar_tensor_tensor(mods[:, j, :], sign[:, k, :], -1.0, mag[:, k, :], ALU.add, ALU.mult).then_inc(row_final[j], 1)

                dve.sem_inc(lo_done, 2)
                nc.vector.memset(ones[:, :], 1.0).then_inc(ones_ready, 1)
                dve.wait_ge(ones_ready, 1)
                dve.wait_ge(silu_ready, 1)
                for c in range(HC):
                    nc.vector.tensor_scalar(silu_rep[:, c, :], ones[:, :], silu_c[:, c:c + 1], None, ALU.mult).then_inc(rep_ready, 1)
                normalize(0)
                normalize(1)
                add_one(1, scale_ready)
                dve.wait_ge(scale_ready, 1)
                with dve.Fori(0, GROUPS - 2) as n:
                    scale(n)
                    normalize(n + 2)
                    low_parts(n)
                scale(GROUPS - 2)
                gate(0, 2)
                low_parts(GROUPS - 2)
                scale(GROUPS - 1)
                add_one(4, row_final[4])
                gate(1, 5)
                low_parts(GROUPS - 1)


def stage_b(nc, wq, wk, wv, rope, masks, aT_dram, hT_hi, hT_lo):
    with ExitStack() as ctx:
        def sb(name, shape, dt=F32):
            return ctx.enter_context(nc.sbuf_tensor(name, shape, dt))

        def sem(name):
            return ctx.enter_context(nc.semaphore(name))

        def bank(name):
            return ctx.enter_context(nc.psum_tensor(name, [P, 512], F32))

        ident = sb("b_ident", [P, P])
        cs = sb("cs", [P, 2, TOK])
        mask = sb("mask_sb", [P, 512 + P])
        before_split = sb("before_split", [P, 10, UT])
        w_raw = before_split[:, 0:3, :].rearrange("p i (c n) -> p i c n", c=HC)
        raw = before_split[:, 3:6, :]
        rot = before_split[:, 6:8, :]
        rsum = before_split[:, 8:10, :]
        w_hi = sb("w_hi", [P, 3, HC, P], F32R)
        w_lo = sb("w_lo", [P, 3, HC, P], F32R)
        split = sb("split", [P, 2, 2, UT], F32R)
        q_dup = sb("q_dup", [P, 2, 2, 2, UT], F32R)
        k_stack = sb("k_stack", [P, 2, TOK], F32R)
        v_tok = sb("v_tok", [P, NT, 2, 2 * D], F32R)
        prob = sb("prob", [P, 2 * TOK])
        pt_hi = sb("pt_hi", [P, 3, 512], F32R)
        pt_lo = sb("pt_lo", [P, 3, 512], F32R)
        half = sb("half", [P, BLOCK])
        a_out = sb("a_out", [P, 2, UT])
        negmax = sb("negmax", [P, 8])
        den = sb("den", [P, 8])
        rden = sb("rden", [P, 8])
        ps_proj = [bank(f"ps_proj{i}") for i in range(2)]
        ps_s = [bank(f"ps_s{i}") for i in range(2)]
        ps_p = [bank(f"ps_p{i}") for i in range(2)]
        ps_o = bank("ps_o")
        ps_v = bank("ps_v")

        def p_bank(f):
            return ps_p[f] if f < 2 else ps_v

        def job_prob(j):
            return prob[:, j * 384:(j + 1) * 384]

        tables_loaded, ident_ready, zeros_ready = sem("tables_loaded"), sem("b_ident_ready"), sem("zeros_ready")
        w_first = [sem(f"w_first{m}") for m in range(3)]
        w_loaded, w_hi_done, w_split = sem("w_loaded"), sem("w_hi_done"), sem("w_split")
        proj_done, raw_done, rot_done = sem("proj_done"), sem("raw_done"), sem("rot_done")
        mults_done, sum_done, rhi_done, rlo_done = sem("rope_mults_done"), sem("rope_sum_done"), sem("rope_hi_done"), sem("rope_lo_done")
        stacked = sem("stacked")
        vt_done, vhi_done, vlo_done = sem("vt_done"), sem("vhi_done"), sem("vlo_done")
        scores_done, max_done, exp_done = sem("scores_done"), sem("max_done"), sem("exp_done")
        rden_done, prob_done = sem("rden_done"), sem("prob_done")
        pt_done, pthi_done, ptlo_done = sem("pt_done"), sem("pthi_done"), sem("ptlo_done")
        pv_done, half_done, a_done, a_stored = sem("pv_done"), sem("half_done"), sem("a_done"), sem("a_stored")
        dve_begun, pool_begun, sp_begun = sem("b_dve_begun"), sem("b_pool_begun"), sem("b_sp_begun")
        g_scores_done, g_max_done, g_min_done, g_exp_done = sem("g_scores_done"), sem("g_max_done"), sem("g_min_done"), sem("g_exp_done")
        g_rden_done, g_prob_done = sem("g_rden_done"), sem("g_prob_done")
        g_pt_done, g_pthi_done, g_ptlo_done = sem("g_pt_done"), sem("g_pthi_done"), sem("g_ptlo_done")
        g_pv_done, g_half_done, g_a_done = sem("g_pv_done"), sem("g_half_done"), sem("g_a_done")
        g_a_stored = [sem("g_a_stored0"), sem("g_a_stored1")]

        def at(unit, per, count):
            p, t = unit
            return p * (UNITS * per) + (t * per + count)

        def following(unit, n=1):
            p, t = unit
            return (p, t + n) if t + n < UNITS else (p + 1, t + n - UNITS)

        def before(unit):
            p, t = unit
            return (p, t - 1) if t > 0 else (p - 1, UNITS - 1)

        def job(j):
            return j // 4, j % 2, j % 4 // 2

        def first_tile(t, b):
            return 1 if (t == 0 and b == 0) else 0

        def job_cols(t, j):
            b, _, qt = job(j)
            return first_tile(t, b) * P, (2 + qt) * P

        GLOBAL = LOCAL_PAIRS
        END = (GLOBAL, 0)
        G = [(m, hd) for m in range(TOK // BLOCK) for hd in range(2)]
        SIDE = {-1 + 4 * (t - 2) + k: ((GLOBAL, t), k) for t in (2, 3) for k in range(4)}

        def g_chunks(m, qt):
            n = (2 * m + 1 + qt) * P
            return [(s, min(512, n - s), s + 512 >= n) for s in range(0, n, 512)]

        def g_banks(g):
            if g >= len(G):
                return []
            m = G[g][0]
            return [(qt, i, ch, i + 1 == len(g_chunks(m, qt))) for qt in range(2) for i, ch in enumerate(g_chunks(m, qt))]

        def g_counts(g):
            s = sum(len(g_banks(i)) for i in range(g))
            f = sum(m + 1 for m, _ in G[:g])
            return s, f

        def g_row(g, qt):
            m = G[g][0]
            if m < 4:
                return prob[:, (2 * (g % 2) + qt) * (TOK // 2):(2 * (g % 2) + qt + 1) * (TOK // 2)]
            if g % 2 == 1:
                return prob[:, qt * TOK:(qt + 1) * TOK]
            return before_split[:, :, :].rearrange("p a n -> p (a n)")[:, qt * TOK:(qt + 1) * TOK]

        DEEP = 8

        def g_share(g, f):
            nb = len(g_banks(g + 1))
            return [b for b in range(nb) if min(b // 2, G[g][0]) == f]

        def g_ways(g):
            return 4 if g >= DEEP else 2

        def g_bank(g, n):
            return (ps_p + ps_proj)[n % g_ways(g)]

        def g_place(pt, g, n):
            k = n % g_ways(g)
            w = w_hi if pt is pt_hi else w_lo
            return pt[:, k, :] if k < 2 else w[:, k - 2, :, :].rearrange("p c n -> p (c n)")

        def g_last_use(g, n):
            if g >= DEEP and n % 4 >= 2:
                return max(n - 3, 0) if n - 4 >= g_counts(DEEP)[1] else 0
            return n - 3 if g >= DEEP and n - 4 >= g_counts(DEEP)[1] else max(n - 1, 0)

        with nc.Block() as block:
            @block.sync
            def _(sp):
                def load_weights(p):
                    pair = slice(0, 1) if isinstance(p, int) and p == 0 else bass.ds(sp.snap(p) if not isinstance(p, int) else p, 1)
                    for i, w in enumerate((wq, wk, wv)):
                        loaded = w_first[i] if isinstance(p, int) and p == 0 else w_loaded
                        sp.dma_start(w_raw[:, i, :, :], w[pair].rearrange("a p c n -> p (a c) n")).then_inc(loaded, 16)

                def rotate(unit, first=False):
                    if not first:
                        sp.wait_ge(sum_done, at(unit, 1, 0))
                        settle(sp, sp_begun)
                    sp.wait_ge(raw_done, at(unit, 3, 2))
                    settle(sp, sp_begun)
                    for s in range(4):
                        d = s ^ 1
                        sp.dma_start(rot[32 * d:32 * d + 32, :, :], raw[32 * s:32 * s + 32, 0:2, :]).then_inc(rot_done, 16)

                def stack(unit, free=None, count=None):
                    t = unit[1]
                    if free is not None:
                        sp.wait_ge(free, count)
                        settle(sp, sp_begun)
                    sp.wait_ge(rlo_done, at(unit, 1, 1))
                    settle(sp, sp_begun)
                    for hd in range(2):
                        rows = slice(D * hd, D * hd + D)
                        for up in range(2):
                            sp.dma_start(f32(q_dup[D * up:D * up + D, t % 2, hd, :, :]), f32(split[rows, 0, :, :])).then_inc(stacked, 16)
                        for s in range(2):
                            sp.dma_start(f32(k_stack[D * s:D * s + D, hd, t * UT:(t + 1) * UT]), f32(split[rows, 1, s, :])).then_inc(stacked, 16)

                def store(unit):
                    p, t = unit
                    sp.wait_ge(a_done, at(unit, 4, 4 + 2))
                    settle(sp, sp_begun)
                    pair = bass.ds(p if isinstance(p, int) else sp.snap(p), 1)
                    sp.dma_start(aT_dram[t * 4:t * 4 + 4, :, pair, :].rearrange("k p a n -> p k (a n)"),
                                 a_out[:, t % 2, :].rearrange("p (k n) -> p k n", n=P)).then_inc(a_stored, 16)

                def slot(unit, first=False):
                    p, t = unit
                    if t == 0:
                        sp.wait_ge(w_split, p * 3 + 3)
                        settle(sp, sp_begun)
                        load_weights(p + 1)
                    if first:
                        stack(following(unit))
                    else:
                        stack(following(unit), scores_done, at(unit, 8, 0))
                    rotate(following(unit, 2))
                    if not first:
                        store(before(unit))

                sp.sem_inc(a_stored, 32)
                load_weights(0)
                sp.dma_start(cs[:, :, :], rope.rearrange("i p n -> p i n")).then_inc(tables_loaded, 16)
                sp.dma_start(mask[:, :], masks).then_inc(tables_loaded, 16)
                rotate((0, 0), first=True)
                stack((0, 0))
                rotate((0, 1))
                for t in range(UNITS):
                    slot((0, t), first=(t == 0))
                with sp.Fori(1, LOCAL_PAIRS) as p:
                    for t in range(UNITS):
                        slot((p, t))
                store(before(END))
                stack((GLOBAL, 1), scores_done, at(END, 8, 0))
                for t in range(UNITS):
                    if t < 2:
                        rotate((GLOBAL, t + 2))
                        stack((GLOBAL, t + 2), g_scores_done, g_counts(4 * (t + 1))[0])
                    sp.wait_ge(g_a_done, 4 * (t + 1))
                    sp.dma_start(aT_dram[t * 4:t * 4 + 4, :, GLOBAL, :].rearrange("k p n -> p k n"),
                                 a_out[:, t % 2, :].rearrange("p (k n) -> p k n", n=P)).then_inc(g_a_stored[t % 2], 16)
                sp.wait_ge(a_stored, 16 * (LOCAL_PAIRS * UNITS) + 32)
                for i in range(2):
                    sp.wait_ge(g_a_stored[i], 16 * UNITS // 2)

            @block.gpsimd
            def _(pool):
                def weights_low(p, m):
                    pool.wait_ge(w_hi_done, p * 3 + (m + 1))
                    settle(pool, pool_begun)
                    nc.gpsimd.tensor_tensor(w_lo[:, m, :, :], w_raw[:, m, :, :], f32(w_hi[:, m, :, :]), ALU.subtract).then_inc(w_split, 1)

                def rope_cos(unit, first=False):
                    cols = slice(unit[1] * UT, (unit[1] + 1) * UT)
                    if not first:
                        pool.wait_ge(rlo_done, at(unit, 1, 0))
                    pool.wait_ge(raw_done, at(unit, 3, 2))
                    nc.gpsimd.tensor_tensor(rsum[:, :, :], raw[:, 0:2, :], cs[:, 0:1, cols].broadcast_to([P, 2, UT]), ALU.mult).then_inc(mults_done, 1)

                def rope_sin(unit):
                    cols = slice(unit[1] * UT, (unit[1] + 1) * UT)
                    pool.wait_ge(rot_done, at(unit, 64, 64))
                    nc.gpsimd.tensor_tensor(rot[:, :, :], rot[:, :, :], cs[:, 1:2, cols].broadcast_to([P, 2, UT]), ALU.mult).then_inc(mults_done, 1)

                def normalize(unit, r):
                    pool.wait_ge(rden_done, at(unit, 4, r + 1))
                    settle(pool, pool_begun)
                    for j in (2 * r, 2 * r + 1):
                        lo, hi = job_cols(unit[1], j)
                        row = job_prob(j)[:, lo:hi]
                        nc.gpsimd.tensor_scalar(row, row, rden[:, j:j + 1], 1.0, ALU.mult, ALU.mult).then_inc(prob_done, 1)

                def slot(unit):
                    p, t = unit
                    normalize(unit, 0)
                    normalize(unit, 1)
                    if t == 2:
                        weights_low(p + 1, 2)
                    if t == 1:
                        weights_low(p + 1, 0)
                        weights_low(p + 1, 1)
                    normalize(unit, 2)
                    rope_cos(following(unit, 2))
                    normalize(unit, 3)
                    rope_sin(following(unit, 2))

                def g_normalize(g):
                    m = G[g][0]
                    for qt in range(2):
                        row = g_row(g, qt)[:, 0:(2 * m + 1 + qt) * P]
                        c = 2 * (g % 2) + qt
                        pool.wait_ge(g_rden_done, 2 * g + qt + 1)
                        nc.gpsimd.tensor_scalar(row, row, rden[:, c:c + 1], 1.0, ALU.mult, ALU.mult).then_inc(g_prob_done, 1)

                make_identity(pool, ident, ident_ready)
                nc.gpsimd.memset(f32(pt_hi[:, 2, :]), 0.0).then_inc(zeros_ready, 1)
                nc.gpsimd.memset(f32(pt_lo[:, 2, :]), 0.0).then_inc(zeros_ready, 1)
                for m in range(3):
                    weights_low(0, m)
                pool.wait_ge(tables_loaded, 32)
                for t in range(2):
                    rope_cos((0, t), first=(t == 0))
                    rope_sin((0, t))
                for t in range(UNITS):
                    slot((0, t))
                with pool.Fori(1, LOCAL_PAIRS) as p:
                    for t in range(UNITS):
                        slot((p, t))
                g_normalize(0)
                for g in range(len(G)):
                    if g + 1 < len(G):
                        g_normalize(g + 1)
                    if g in (1, 5):
                        rope_cos((GLOBAL, 2 + g // 4))
                        rope_sin((GLOBAL, 2 + g // 4))

            @block.scalar
            def _(act):
                def copy_raw(unit, m, first=False):
                    act.wait_ge(proj_done, at(unit, 3, m + 1))
                    if not first and m < 2:
                        act.wait_ge(rot_done, at(unit, 64, 0))
                        act.wait_ge(mults_done, at(unit, 2, 0))
                    if not first and m == 2:
                        act.wait_ge(vt_done, at(unit, 1, 0))
                    n = (3 * unit[1] + m) % 2
                    nc.scalar.activation(raw[:, m, :], ps_proj[n][:, :], ACT.Copy).then_inc(raw_done, 1)

                def v_hi(unit):
                    t = unit[1]
                    act.wait_ge(vt_done, at(unit, 1, 1))
                    nc.scalar.activation(v_tok[:, 4 * t:4 * t + 4, :, 0:D],
                                         ps_v[:, :].rearrange("p (k h d) -> p k h d", k=4, h=2), ACT.Copy).then_inc(vhi_done, 1)

                def exp(unit, j):
                    lo, hi = job_cols(unit[1], j)
                    row = job_prob(j)[:, lo:hi]
                    act.wait_ge(max_done, at(unit, 8, j + 1 + 2))
                    nc.scalar.activation(row, row, ACT.Exp, bias=negmax[:, j:j + 1], scale=-1.0,
                                         accum_out=den[:, j:j + 1]).then_inc(exp_done, 1)

                def p_hi(unit, b, f):
                    t = unit[1]
                    if f == 0:
                        act.wait_ge(pv_done, at(unit, 2, b + 1))
                    act.wait_ge(pt_done, at(unit, 6, 3 * b + f + 1))
                    if f < 2:
                        lo = first_tile(t, b) * BLOCK
                        nc.scalar.activation(pt_hi[:, f, lo:512], ps_p[f][:, lo:512], ACT.Copy).then_inc(pthi_done, 1)
                    else:
                        nc.scalar.activation(pt_hi[:, 2, :].rearrange("p (h q) -> p h q", h=2)[:, :, P:BLOCK],
                                             ps_v[:, 0:BLOCK].rearrange("p (h q) -> p h q", h=2), ACT.Copy).then_inc(pthi_done, 1)

                def halves(unit, b):
                    act.wait_ge(a_done, at(unit, 4, 2 * b + 2))
                    act.wait_ge(pv_done, at(unit, 2, b + 2))
                    nc.scalar.activation(half[0:D, :], ps_o[D:P, 0:BLOCK], ACT.Copy).then_inc(half_done, 1)
                    nc.scalar.activation(half[D:P, :], ps_o[0:D, BLOCK:2 * BLOCK], ACT.Copy).then_inc(half_done, 1)

                def slot(unit, first=False):
                    last, ahead = before(unit), following(unit, 2)
                    exp(unit, 0)
                    if not first:
                        p_hi(last, 1, 0)
                        p_hi(last, 1, 1)
                    exp(unit, 1)
                    if not first:
                        p_hi(last, 1, 2)
                    exp(unit, 2)
                    copy_raw(ahead, 0)
                    exp(unit, 3)
                    if not first:
                        halves(last, 1)
                    copy_raw(ahead, 1)
                    exp(unit, 4)
                    exp(unit, 5)
                    p_hi(unit, 0, 0)
                    exp(unit, 6)
                    p_hi(unit, 0, 1)
                    p_hi(unit, 0, 2)
                    exp(unit, 7)
                    v_hi(following(unit))
                    copy_raw(ahead, 2)
                    halves(unit, 0)

                def g_exp(g, qt):
                    m = G[g][0]
                    row = g_row(g, qt)[:, 0:(2 * m + 1 + qt) * P]
                    c = 2 * (g % 2) + qt
                    act.wait_ge(g_min_done, 2 * g + qt + 1)
                    nc.scalar.activation(row, row, ACT.Exp, bias=negmax[:, c:c + 1], scale=-1.0,
                                         accum_out=den[:, c:c + 1]).then_inc(g_exp_done, 1)

                def side(g):
                    if g in SIDE:
                        unit, k = SIDE[g]
                        if k < 3:
                            copy_raw(unit, k)
                        else:
                            v_hi(unit)

                def g_p_hi(g, f):
                    m = G[g][0]
                    n = g_counts(g)[1] + f
                    src, dst = g_bank(g, n), g_place(pt_hi, g, n)
                    act.wait_ge(g_pt_done, n + 1)
                    if g_last_use(g, n):
                        act.wait_ge(g_pv_done, g_last_use(g, n))
                    if f < m:
                        nc.scalar.activation(dst, src[:, :], ACT.Copy).then_inc(g_pthi_done, 1)
                    else:
                        if n == 1:
                            act.wait_ge(g_pv_done, 1)
                        nc.scalar.activation(dst[:, 0:BLOCK], src[:, 0:BLOCK], ACT.Copy)
                        nc.scalar.activation(pt_hi[:, 2, P:BLOCK], src[:, BLOCK:BLOCK + P], ACT.Copy).then_inc(g_pthi_done, 1)

                for t in range(2):
                    for m in range(3):
                        copy_raw((0, t), m, first=(t == 0))
                    if t == 0:
                        v_hi((0, t))
                for t in range(UNITS):
                    slot((0, t), first=(t == 0))
                with act.Fori(1, LOCAL_PAIRS) as p:
                    for t in range(UNITS):
                        slot((p, t))
                p_hi(before(END), 1, 0)
                p_hi(before(END), 1, 1)
                for qt in range(2):
                    g_exp(0, qt)
                p_hi(before(END), 1, 2)
                v_hi((GLOBAL, 1))
                side(-1)
                halves(before(END), 1)
                for g, (m, hd) in enumerate(G):
                    ahead = g_ways(g) // 2 - 1
                    for f in range(ahead):
                        g_p_hi(g, f)
                    rows = []
                    for f in range(m + 1):
                        if f + ahead <= m:
                            g_p_hi(g, f + ahead)
                        for qt in rows:
                            g_exp(g + 1, qt)
                        rows = [g_banks(g + 1)[b][0] for b in g_share(g, f) if g_banks(g + 1)[b][3]]
                    for qt in rows:
                        g_exp(g + 1, qt)
                    side(g)
                    if g >= 2:
                        act.wait_ge(g_a_done, g - 1)
                    act.wait_ge(g_pv_done, g_counts(g + 1)[1])
                    if hd == 0:
                        nc.scalar.activation(half[0:D, :], ps_o[D:P, 0:BLOCK], ACT.Copy).then_inc(g_half_done, 1)
                    else:
                        nc.scalar.activation(half[D:P, :], ps_o[0:D, BLOCK:2 * BLOCK], ACT.Copy).then_inc(g_half_done, 1)

            @block.tensor
            def _(pe):
                def project(unit, m, first=False, part=slice(0, 3 * HC)):
                    n = (3 * unit[1] + m) % 2
                    cols = slice(unit[1] * UT, (unit[1] + 1) * UT)
                    if part.start == 0:
                        if not first:
                            pe.wait_ge(raw_done, at(unit, 3, m - 1))
                        elif m == 2:
                            pe.wait_ge(raw_done, 1)
                        pe.wait_ge(w_split, unit[0] * 3 + (m + 1))
                    passes = [(w, h, c) for w, h in ((w_hi, hT_hi), (w_hi, hT_lo), (w_lo, hT_hi)) for c in range(HC)]
                    for w, h, c in passes[part]:
                        last = nc.tensor.matmul(ps_proj[n][:, :], w[:, m, c, :], h[:, c, cols],
                                                start=(w is w_hi and h is hT_hi and c == 0), stop=(w is w_lo and c == HC - 1))
                    if part.stop == len(passes):
                        last.then_inc(proj_done, 1)

                def transpose_v(unit, read_out=None, count=None):
                    if read_out is not None:
                        pe.wait_ge(read_out, count)
                    pe.wait_ge(raw_done, at(unit, 3, 3))
                    for k in range(4):
                        last = nc.tensor.transpose(ps_v[:, k * P:(k + 1) * P], raw[:, 2, k * P:(k + 1) * P], ident[:, :])
                    last.then_inc(vt_done, 1)

                def scores(unit, j):
                    t = unit[1]
                    b, hd, qt = job(j)
                    lo, hi = job_cols(t, j)
                    if j == 0:
                        pe.wait_ge(stacked, at(unit, 128, 128))
                    pe.wait_ge(max_done, at(unit, 8, j + 1))
                    q0 = b * BLOCK + qt * P
                    k0 = t * UT + b * BLOCK - LOOKBACK
                    for s in range(2):
                        last = nc.tensor.matmul(ps_s[j % 2][:, lo:hi], q_dup[:, t % 2, hd, s, q0:q0 + P],
                                                k_stack[:, hd, k0 + lo:k0 + hi], start=(s == 0), stop=(s == 1))
                    last.then_inc(scores_done, 1)

                def transpose_p(unit, b, f):
                    t = unit[1]
                    if f == 0:
                        pe.wait_ge(prob_done, at(unit, 8, 4 * b + 4))
                    pe.wait_ge(ptlo_done, at(unit, 6, 3 * b + f + 1))
                    if f == 2 and b == 1:
                        pe.wait_ge(vlo_done, at(following(unit), 1, 1))
                    if f == 2 and b == 0 and isinstance(unit[0], int) and unit == (0, 0):
                        pe.wait_ge(vlo_done, 1)
                    dst = p_bank(f)
                    if f < 2:
                        for c in range(first_tile(t, b), 2):
                            for qt in range(2):
                                last = nc.tensor.transpose(dst[:, c * BLOCK + qt * P:c * BLOCK + (qt + 1) * P],
                                                           job_prob(4 * b + 2 * qt + f)[:, c * P:(c + 1) * P], ident[:, :])
                    else:
                        for hd in range(2):
                            last = nc.tensor.transpose(dst[:, hd * P:(hd + 1) * P], job_prob(4 * b + 2 + hd)[:, 2 * P:3 * P], ident[:, :])
                    last.then_inc(pt_done, 1)

                def weighted_values(unit, b, f):
                    t = unit[1]
                    first = first_tile(t, b)
                    if f == 0:
                        pe.wait_ge(vlo_done, at(unit, 1, 1))
                        pe.wait_ge(a_done, at(unit, 4, 2 * b + 2))
                    pe.wait_ge(ptlo_done, at(unit, 6, 3 * b + f + 1 + 3))
                    for hd, c in ([(f, c) for c in range(first, 2)] if f < 2 else [(0, 2), (1, 2)]):
                        for pt in (pt_hi, pt_lo):
                            moving = pt[:, hd, c * BLOCK:(c + 1) * BLOCK] if c < 2 else pt[:, 2, hd * BLOCK:(hd + 1) * BLOCK]
                            last = nc.tensor.matmul(ps_o[:, hd * BLOCK:(hd + 1) * BLOCK], v_tok[:, 4 * t + 2 * b - 1 + c, hd, :], moving,
                                                    start=(hd == 0 and c == first and pt is pt_hi), stop=(hd == 1 and c == 2 and pt is pt_lo))
                    if f == 2:
                        last.then_inc(pv_done, 1)

                def slot(unit, first=False):
                    last, ahead = before(unit), following(unit, 2)
                    thirds = [slice(k * HC, (k + 1) * HC) for k in range(3)]
                    scores(unit, 0)
                    scores(unit, 1)
                    if not first:
                        transpose_p(last, 1, 0)
                    project(ahead, 0, part=thirds[0])
                    if not first:
                        transpose_p(last, 1, 1)
                    scores(unit, 2)
                    project(ahead, 0, part=thirds[1])
                    scores(unit, 3)
                    project(ahead, 0, part=thirds[2])
                    if not first:
                        transpose_p(last, 1, 2)
                        weighted_values(last, 1, 0)
                        weighted_values(last, 1, 1)
                    project(ahead, 1, part=thirds[0])
                    project(ahead, 1, part=thirds[1])
                    scores(unit, 4)
                    scores(unit, 5)
                    if not first:
                        weighted_values(last, 1, 2)
                    project(ahead, 1, part=thirds[2])
                    scores(unit, 6)
                    transpose_p(unit, 0, 0)
                    transpose_p(unit, 0, 1)
                    project(ahead, 2, part=thirds[0])
                    scores(unit, 7)
                    project(ahead, 2, part=thirds[1])
                    transpose_p(unit, 0, 2)
                    weighted_values(unit, 0, 0)
                    project(ahead, 2, part=thirds[2])
                    transpose_v(following(unit), ptlo_done, at(unit, 6, 3) + 3)
                    weighted_values(unit, 0, 1)
                    weighted_values(unit, 0, 2)

                def g_scores(g, b):
                    m, hd = G[g]
                    t = m // 2
                    qt, _, (start, width, _), _ = g_banks(g)[b]
                    n = g_counts(g)[0] + b
                    if b == 0 and g % 4 == 0:
                        pe.wait_ge(stacked, at((GLOBAL, t), 128, 128))
                    if n >= 2:
                        pe.wait_ge(g_max_done, n - 1)
                    else:
                        pe.wait_ge(max_done, at(END, 8, n + 1))
                    q0 = (m % 2) * BLOCK + qt * P
                    for s in range(2):
                        last = nc.tensor.matmul(ps_s[n % 2][:, 0:width], q_dup[:, t % 2, hd, s, q0:q0 + P],
                                                k_stack[:, hd, start:start + width], start=(s == 0), stop=(s == 1))
                    last.then_inc(g_scores_done, 1)

                def side(g):
                    if g in SIDE:
                        unit, k = SIDE[g]
                        if k < 3:
                            project(unit, k)
                        else:
                            transpose_v(unit, vlo_done, at(unit, 1, 0))

                def g_transpose(g, f):
                    m = G[g][0]
                    n = g_counts(g)[1] + f
                    if f == 0:
                        pe.wait_ge(g_prob_done, 2 * g + 2)
                    if g_last_use(g, n):
                        pe.wait_ge(g_ptlo_done, g_last_use(g, n))
                    elif g >= DEEP:
                        pe.wait_ge(raw_done, at((GLOBAL, UNITS), 3, 0))
                    cols = [(0, 0, 0), (0, 1, P), (1, 0, 2 * P), (1, 1, 3 * P)] if f < m else [(0, 0, 0), (0, 1, P), (1, 1, 2 * P)]
                    for c, qt, col in cols:
                        last = nc.tensor.transpose(g_bank(g, n)[:, col:col + P], g_row(g, qt)[:, (2 * f + c) * P:(2 * f + c + 1) * P], ident[:, :])
                    last.then_inc(g_pt_done, 1)

                def g_values(g, f):
                    m, hd = G[g]
                    n = g_counts(g)[1] + f
                    if f == 0 and g >= 2:
                        pe.wait_ge(g_a_done, g - 1)
                    if f == 0 and g < 2:
                        pe.wait_ge(a_done, at(END, 4, 2))
                    if f == 0 and g % 4 == 0:
                        pe.wait_ge(vlo_done, at((GLOBAL, m // 2), 1, 1))
                    pe.wait_ge(g_ptlo_done, n + 1)
                    for c in range(2):
                        for pt in (pt_hi, pt_lo):
                            moving = pt[:, 2, 0:BLOCK] if (f == m and c == 1) else g_place(pt, g, n)[:, c * BLOCK:(c + 1) * BLOCK]
                            last = nc.tensor.matmul(ps_o[:, hd * BLOCK:(hd + 1) * BLOCK], v_tok[:, 2 * f + c, hd, :], moving,
                                                    start=(f == 0 and c == 0 and pt is pt_hi), stop=(f == m and c == 1 and pt is pt_lo))
                    last.then_inc(g_pv_done, 1)

                pe.sem_inc(pv_done, 1)
                pe.wait_ge(ident_ready, 2)
                for t in range(2):
                    for m in range(3):
                        project((0, t), m, first=(t == 0))
                    if t == 0:
                        transpose_v((0, t))
                for t in range(UNITS):
                    slot((0, t), first=(t == 0))
                with pe.Fori(1, LOCAL_PAIRS) as p:
                    for t in range(UNITS):
                        slot((p, t))
                for b in range(2):
                    g_scores(0, b)
                for f in range(3):
                    transpose_p(before(END), 1, f)
                transpose_v((GLOBAL, 1), ptlo_done, at(END, 6, 0) + 3)
                side(-1)
                for f in range(3):
                    weighted_values(before(END), 1, f)
                for g, (m, hd) in enumerate(G):
                    ahead = g_ways(g) // 2 - 1
                    for f in range(ahead):
                        g_transpose(g, f)
                    for f in range(m + 1):
                        if f + ahead <= m:
                            g_transpose(g, f + ahead)
                        for b in g_share(g, f):
                            g_scores(g + 1, b)
                        if f >= 1:
                            g_values(g, f - 1)
                    side(g)
                    g_values(g, m)

            @block.vector
            def _(dve):
                def weights_high(p, m, first=False):
                    if not first:
                        dve.wait_ge(proj_done, at((p - 1, UNITS - 1), 3, m + 1))
                        dve.wait_ge(w_loaded, p * 48)
                    else:
                        dve.wait_ge(w_first[m], 16)
                    nc.vector.tensor_copy(w_hi[:, m, :, :], w_raw[:, m, :, :]).then_inc(w_hi_done, 1)

                def row_max(unit, j, first=False):
                    lo, hi = job_cols(unit[1], j)
                    if j in (0, 4) and not first:
                        dve.wait_ge(pt_done, at(unit, 6, 3 * (j // 4) - 3))
                    dve.wait_ge(scores_done, at(unit, 8, j + 1))
                    settle(dve, dve_begun)
                    nc.vector.tensor_tensor_reduce(job_prob(j)[:, lo:hi], ps_s[j % 2][:, lo:hi], mask[:, 512 + P - (hi - lo):512 + P],
                                                   NEG_SCALE, 3e38, ALU.add, ALU.min, negmax[:, j:j + 1]).then_inc(max_done, 1)

                def reciprocals(unit, r):
                    dve.wait_ge(exp_done, at(unit, 8, 2 * r + 2))
                    nc.vector.reciprocal(rden[:, 2 * r:2 * r + 2], den[:, 2 * r:2 * r + 2]).then_inc(rden_done, 1)

                def rope_sum(unit):
                    dve.wait_ge(mults_done, at(unit, 2, 2))
                    nc.vector.tensor_tensor(rsum[:, :, :], rsum[:, :, :], rot[:, :, :], ALU.add).then_inc(sum_done, 1)

                def rope_high(unit, first=False):
                    if not first:
                        dve.wait_ge(stacked, at(unit, 128, 0))
                    dve.wait_ge(sum_done, at(unit, 1, 1))
                    nc.vector.tensor_copy(split[:, :, 0, :], rsum[:, :, :]).then_inc(rhi_done, 1)

                def rope_low(unit):
                    dve.wait_ge(rhi_done, at(unit, 1, 1))
                    nc.vector.tensor_tensor(split[:, :, 1, :], rsum[:, :, :], f32(split[:, :, 0, :]), ALU.subtract).then_inc(rlo_done, 1)

                def rope_split(unit, first=False):
                    rope_sum(unit)
                    rope_high(unit, first)
                    rope_low(unit)

                def v_lo(unit):
                    t = unit[1]
                    dve.wait_ge(vhi_done, at(unit, 1, 1))
                    v = v_tok[:, 4 * t:4 * t + 4, :, :]
                    nc.vector.tensor_tensor(v[:, :, :, D:2 * D], ps_v[:, :].rearrange("p (k h d) -> p k h d", k=4, h=2),
                                            f32(v[:, :, :, 0:D]), ALU.subtract).then_inc(vlo_done, 1)

                def p_lo(unit, b, f):
                    t = unit[1]
                    dve.wait_ge(pthi_done, at(unit, 6, 3 * b + f + 1))
                    src = p_bank(f)
                    if f < 2:
                        lo = first_tile(t, b) * BLOCK
                        nc.vector.tensor_tensor(pt_lo[:, f, lo:512], src[:, lo:512], f32(pt_hi[:, f, lo:512]), ALU.subtract).then_inc(ptlo_done, 1)
                    else:
                        hi = pt_hi[:, 2, :].rearrange("p (h q) -> p h q", h=2)[:, :, P:BLOCK]
                        out = pt_lo[:, 2, :].rearrange("p (h q) -> p h q", h=2)[:, :, P:BLOCK]
                        nc.vector.tensor_tensor(out, src[:, 0:BLOCK].rearrange("p (h q) -> p h q", h=2), f32(hi), ALU.subtract).then_inc(ptlo_done, 1)

                def join(unit, b):
                    t = unit[1]
                    cols = slice(b * BLOCK, (b + 1) * BLOCK)
                    if b == 0:
                        dve.wait_ge(a_stored, at(unit, 16, 16))
                    dve.wait_ge(half_done, at(unit, 4, 2 * b + 2))
                    nc.vector.tensor_tensor(a_out[0:D, t % 2, cols], ps_o[0:D, 0:BLOCK], half[0:D, :], ALU.add).then_inc(a_done, 1)
                    nc.vector.tensor_tensor(a_out[D:P, t % 2, cols], ps_o[D:P, BLOCK:2 * BLOCK], half[D:P, :], ALU.add).then_inc(a_done, 1)

                def slot(unit, first=False):
                    p, t = unit
                    last = before(unit)
                    row_max(unit, 0, first)
                    row_max(unit, 1)
                    if not first:
                        join(last, 0)
                        p_lo(last, 1, 0)
                    row_max(unit, 2)
                    if not first:
                        p_lo(last, 1, 1)
                    reciprocals(unit, 0)
                    rope_sum(following(unit))
                    if not first:
                        p_lo(last, 1, 2)
                    rope_high(following(unit))
                    row_max(unit, 3)
                    rope_low(following(unit))
                    reciprocals(unit, 1)
                    if t == 2:
                        weights_high(p + 1, 2)
                    row_max(unit, 4, first)
                    if t == 1:
                        weights_high(p + 1, 0)
                    row_max(unit, 5)
                    if not first:
                        join(last, 1)
                    reciprocals(unit, 2)
                    if t == 1:
                        weights_high(p + 1, 1)
                    p_lo(unit, 0, 0)
                    row_max(unit, 6)
                    row_max(unit, 7)
                    p_lo(unit, 0, 1)
                    p_lo(unit, 0, 2)
                    reciprocals(unit, 3)
                    v_lo(following(unit))

                def g_row_max(g, b):
                    qt, i, (start, width, diagonal), row_done = g_banks(g)[b]
                    n = g_counts(g)[0] + b
                    c = 2 * (g % 2) + qt
                    if b == 0 and g < 2:
                        dve.wait_ge(pt_done, at(END, 6, -3 + 3 * g))
                    if b == 0 and g >= 2:
                        dve.wait_ge(g_pt_done, g_counts(g - 1)[1])
                    if b == 0 and g == 8:
                        dve.wait_ge(sum_done, at((GLOBAL, UNITS), 1, 0))
                        dve.wait_ge(vlo_done, at((GLOBAL, UNITS), 1, 0))
                    if i == 0 and 2 * g + qt > 0:
                        dve.wait_ge(g_min_done, 2 * g + qt)
                    dve.wait_ge(g_scores_done, n + 1)
                    m0 = 512 + P - width if diagonal else 0
                    nc.vector.tensor_tensor_reduce(g_row(g, qt)[:, start:start + width], ps_s[n % 2][:, 0:width], mask[:, m0:m0 + width],
                                                   NEG_SCALE, 3e38, ALU.add, ALU.min, negmax[:, 4 + i:5 + i]).then_inc(g_max_done, 1)
                    if row_done:
                        dve.wait_ge(g_max_done, n + 1)
                        nc.vector.tensor_reduce(negmax[:, c:c + 1], negmax[:, 4:5 + i], AX_X, ALU.min).then_inc(g_min_done, 1)

                def g_reciprocal(g, qt):
                    c = 2 * (g % 2) + qt
                    dve.wait_ge(g_exp_done, 2 * g + qt + 1)
                    nc.vector.reciprocal(rden[:, c:c + 1], den[:, c:c + 1]).then_inc(g_rden_done, 1)

                def g_p_lo(g, f):
                    m = G[g][0]
                    n = g_counts(g)[1] + f
                    src, hi, lo = g_bank(g, n), g_place(pt_hi, g, n), g_place(pt_lo, g, n)
                    dve.wait_ge(g_pthi_done, n + 1)
                    if f < m:
                        nc.vector.tensor_tensor(lo, src[:, :], f32(hi), ALU.subtract).then_inc(g_ptlo_done, 1)
                    else:
                        nc.vector.tensor_tensor(lo[:, 0:BLOCK], src[:, 0:BLOCK], f32(hi[:, 0:BLOCK]), ALU.subtract)
                        nc.vector.tensor_tensor(pt_lo[:, 2, P:BLOCK], src[:, BLOCK:BLOCK + P], f32(pt_hi[:, 2, P:BLOCK]), ALU.subtract).then_inc(g_ptlo_done, 1)

                def g_join(g):
                    m, hd = G[g]
                    t = m // 2
                    rows = slice(D * hd, D * hd + D)
                    if g % 4 == 0:
                        if t < 2:
                            dve.wait_ge(a_stored, at(END, 16, 32))
                        else:
                            dve.wait_ge(g_a_stored[t % 2], 16 * (t // 2))
                    dve.wait_ge(g_half_done, g + 1)
                    nc.vector.tensor_tensor(a_out[rows, t % 2, (m % 2) * BLOCK:(m % 2 + 1) * BLOCK],
                                            ps_o[rows, hd * BLOCK:(hd + 1) * BLOCK], half[rows, :], ALU.add).then_inc(g_a_done, 1)

                dve.sem_inc(max_done, 2)
                dve.sem_inc(ptlo_done, 3)
                dve.sem_inc(a_done, 2)
                for m in range(3):
                    weights_high(0, m, first=True)
                rope_split((0, 0), first=True)
                v_lo((0, 0))
                dve.wait_ge(tables_loaded, 32)
                for t in range(UNITS):
                    slot((0, t), first=(t == 0))
                with dve.Fori(1, LOCAL_PAIRS) as p:
                    for t in range(UNITS):
                        slot((p, t))
                dve.wait_ge(zeros_ready, 2)
                for b in range(2):
                    g_row_max(0, b)
                join(before(END), 0)
                for f in range(2):
                    p_lo(before(END), 1, f)
                for qt in range(2):
                    g_reciprocal(0, qt)
                p_lo(before(END), 1, 2)
                v_lo((GLOBAL, 1))
                rope_split((GLOBAL, 1))
                join(before(END), 1)
                for g, (m, hd) in enumerate(G):
                    banks = g_banks(g + 1)
                    waiting = []
                    for f in range(m + 1):
                        issued = []
                        for b in g_share(g, f):
                            g_row_max(g + 1, b)
                            if banks[b][3]:
                                issued.append(banks[b][0])
                        g_p_lo(g, f)
                        for qt in waiting:
                            g_reciprocal(g + 1, qt)
                        waiting = issued
                        if g - 1 in SIDE and SIDE[g - 1][1] == 3 and f < 2:
                            (rope_high, rope_low)[f](SIDE[g - 1][0])
                    for qt in waiting:
                        g_reciprocal(g + 1, qt)
                    if g in SIDE and SIDE[g][1] == 3:
                        v_lo(SIDE[g][0])
                        rope_sum(SIDE[g][0])
                    g_join(g)


def stage_c(nc, x, wo, bo_rep, mods_dram, aT_dram, x1, hT_hi, hT_lo):
    with ExitStack() as ctx:
        def sb(name, shape, dt=F32):
            return ctx.enter_context(nc.sbuf_tensor(name, shape, dt))

        def sem(name):
            return ctx.enter_context(nc.semaphore(name))

        RC = 4
        PC = PAIRS // RC
        WAYS = 4
        ident = sb("c_ident", [P, P])
        rows = sb("rows", [P, 3, HID])
        bias = sb("bias", [P, HID])
        wo_hi = sb("wo_hi", [P, PAIRS, HID], F32R)
        with nc.sbuf_tensor("wo_unsplit", [P, PAIRS, HID], F32) as wo_unsplit:
            pass
        wo_lo = sb("wo_lo", [P, PAIRS, HID], F32R)
        a_raw = sb("a_raw", [P, RC, PC, P])
        a_hi = sb("a_hi", [P, RC, PC, P], F32R)
        a_lo = sb("a_lo", [P, RC, PC, P], F32R)
        stats = sb("c_stats", [P, 2, 6])
        mv = sb("c_mv", [P, 2, 2])
        std = sb("c_std", [P, 2])
        rstd = sb("c_rstd", [P, 2])
        gated = sb("gated", [P, HID])
        h = sb("c_h", [P, 2, HID])
        ps_y = [ctx.enter_context(nc.psum_tensor(f"ps_y{i}", [P, HID], F32)) for i in range(WAYS)]
        ps_t = [ctx.enter_context(nc.psum_tensor(f"c_ps_t{i}", [P, HID], F32)) for i in range(2)]

        rows_loaded, ident_ready, bias_ready = sem("rows_loaded"), sem("c_ident_ready"), sem("bias_ready")
        wo_loaded = [sem(f"wo_loaded{k}") for k in range(2 * RC)]
        wo_hi_done, wo_split = sem("wo_hi_done"), sem("wo_split")
        a_loaded = [sem(f"a_loaded{r}") for r in range(RC)]
        a_hi_done, a_split, a_used = sem("a_hi_done"), sem("a_split"), sem("a_used")
        x_loaded = [sem(f"c_x_loaded{i}") for i in range(WAYS)]
        xb_done, gated_done, x1_done = sem("xb_done"), sem("gated_done"), sem("x1_done")
        stats_done, mv_done, std_done, rstd_done = sem("c_stats_done"), sem("c_mv_done"), sem("c_std_done"), sem("c_rstd_done")
        h_step, h_done = sem("c_h_step"), sem("c_h_done")
        t_done, hi_done, lo_done = sem("c_t_done"), sem("c_hi_done"), sem("c_lo_done")
        dve_begun, sp_begun, act_begun, pool_begun = sem("c_dve_begun"), sem("c_sp_begun"), sem("c_act_begun"), sem("c_pool_begun")

        FIRST_NORMS = [(4, (0, 1)), (5, (2, 3)), (6, (4, 5)), (7, (6,))]

        def tile(n, i):
            return n * WAYS + i

        def first_items():
            return [(WAYS * r + i, i, r) for r in range(RC) for i in range(WAYS)]

        def wo_half(k):
            return slice(k * PC // 2, (k + 1) * PC // 2)

        with nc.Block() as block:
            @block.sync
            def _(sp):
                def load_a(s, tile_slice, r):
                    sp.dma_start(a_raw[:, s % RC, :, :], aT_dram[tile_slice, :, r * PC:(r + 1) * PC, :].rearrange("a p c n -> p (a c) n")).then_inc(a_loaded[s % RC], 16)

                for s, i, r in first_items():
                    if s >= RC:
                        sp.wait_ge(a_split, s - RC + 1)
                    load_a(s, slice(i, i + 1), r)
                    if i == 0:
                        for k in (2 * r, 2 * r + 1):
                            sp.dma_start(wo_unsplit[:, wo_half(k), :], wo[:, wo_half(k), :]).then_inc(wo_loaded[k], 16)
                for k, j in enumerate((2, 3, 4)):
                    sp.dma_start(rows[:, k, :], mods_dram[j]).then_inc(rows_loaded, 16)
                sp.dma_start(bias[:, :], bo_rep).then_inc(rows_loaded, 16)
                for i in range(WAYS):
                    sp.dma_start(x1[:, i, :], x[i]).then_inc(x_loaded[i], 16)

                with sp.Fori(1, NT // WAYS) as n:
                    for i in range(WAYS):
                        t = sp.snap(tile(n, i))
                        for r in range(RC):
                            sp.wait_ge(a_split, t * RC + (r - RC + 1))
                            settle(sp, sp_begun)
                            load_a(r, bass.ds(t, 1), r)
                        sp.wait_ge(xb_done, t - (WAYS - 1))
                        settle(sp, sp_begun)
                        sp.dma_start(x1[:, bass.ds(t, 1), :].rearrange("p a n -> p (a n)"),
                                     x[bass.ds(t, 1)].rearrange("a p n -> p (a n)")).then_inc(x_loaded[i], 16)

            @block.gpsimd
            def _(pool):
                def a_low(s, slot):
                    pool.wait_ge(a_hi_done, s + 1)
                    nc.gpsimd.tensor_tensor(a_lo[:, slot, :, :], a_raw[:, slot, :, :], f32(a_hi[:, slot, :, :]), ALU.subtract).then_inc(a_split, 1)

                def base(n, i):
                    pool.wait_ge(x_loaded[i], n * 16 + 16)
                    settle(pool, pool_begun)
                    row = x1[:, bass.ds(tile(n, i), 1), :].rearrange("p a n -> p (a n)")
                    nc.gpsimd.tensor_tensor(row, row, bias[:, :], ALU.add).then_inc(xb_done, 1)

                make_identity(pool, ident, ident_ready)
                for s, _, _ in first_items():
                    a_low(s, s % RC)
                pool.wait_ge(bias_ready, 1)
                for i in range(WAYS):
                    base(0, i)
                with pool.Fori(1, NT // WAYS) as n:
                    for i in range(WAYS):
                        for r in range(RC):
                            a_low(tile(n, i) * RC + r, r)
                        base(n, i)

            @block.scalar
            def _(act):
                def a_high(s, slot, turn):
                    act.wait_ge(a_used, s + 1)
                    act.wait_ge(a_loaded[slot], turn * 16 + 16)
                    nc.scalar.activation(a_hi[:, slot, :, :], a_raw[:, slot, :, :], ACT.Copy).then_inc(a_hi_done, 1)

                def a_high_tile(n, i):
                    for r in range(RC):
                        a_high(tile(n, i) * RC + r, r, tile(n, i))

                def deviation(n, i):
                    act.wait_ge(mv_done, tile(n, i) + 1)
                    nc.scalar.activation(std[:, i % 2:i % 2 + 1], mv[:, i % 2, 1:2], ACT.Sqrt).then_inc(std_done, 1)

                def high_part(n, i):
                    act.wait_ge(t_done, tile(n, i) + 1)
                    settle(act, act_begun)
                    nc.scalar.activation(hT_hi[:, :, bass.ds(tile(n, i) * P, P)],
                                         ps_t[i % 2][:, :].rearrange("p (c t) -> p c t", c=HC), ACT.Copy).then_inc(hi_done, 1)

                for s, i, r in first_items():
                    a_high(s, s % RC, r)
                    if i == 0:
                        for k in (2 * r, 2 * r + 1):
                            act.wait_ge(wo_loaded[k], 16)
                            nc.scalar.activation(wo_hi[:, wo_half(k), :], wo_unsplit[:, wo_half(k), :], ACT.Copy).then_inc(wo_hi_done, 1)
                a_high_tile(1, 0)
                for tile_before, after in FIRST_NORMS[:-1]:
                    for i in after:
                        deviation(*divmod(i, WAYS))
                    a_high_tile(*divmod(tile_before + 1, WAYS))
                    for i in after:
                        high_part(*divmod(i, WAYS))
                with act.Fori(2, NT // WAYS) as n:
                    for i in range(WAYS):
                        normed = (n, i - 2) if i >= 2 else (n - 1, i + WAYS - 2)
                        deviation(*normed)
                        a_high_tile(n, i)
                        high_part(*normed)
                for i in (WAYS - 2, WAYS - 1):
                    deviation(NT // WAYS - 1, i)
                    high_part(NT // WAYS - 1, i)

            @block.tensor
            def _(pe):
                def item(way, slot, s, r, first=False):
                    pe.wait_ge(a_split, s + 1)
                    passes = [(a, w, half * PC // 2 + c) for half in range(2) for a, w in ((a_hi, wo_hi), (a_hi, wo_lo), (a_lo, wo_hi)) for c in range(PC // 2)]
                    for k, (a, w, c) in enumerate(passes):
                        if first and k % (len(passes) // 2) == 0:
                            pe.wait_ge(wo_split, 2 * r + 1 + k // (len(passes) // 2))
                        last = nc.tensor.matmul(ps_y[way][:, :], a[:, slot, c, :], w[:, r * PC + c, :],
                                                start=(r == 0 and k == 0), stop=(r == RC - 1 and k == len(passes) - 1))
                    last.then_inc(a_used, 1)

                def product(n, i):
                    pe.wait_ge(x1_done, tile(n, i) + 1)
                    for r in range(RC):
                        item(i, r, tile(n, i) * RC + r, r)

                def transposes(n, i):
                    pe.wait_ge(h_done, tile(n, i) + 1)
                    pe.wait_ge(lo_done, tile(n, i) + 1)
                    for c in range(HC):
                        last = nc.tensor.transpose(ps_t[i % 2][:, c * P:(c + 1) * P], h[:, i % 2, c * P:(c + 1) * P], ident[:, :])
                    last.then_inc(t_done, 1)

                pe.sem_inc(a_used, RC)
                for s, i, r in first_items():
                    item(i, s % RC, s, r, first=(i == 0))
                pe.wait_ge(ident_ready, 2)
                for tile_before, after in FIRST_NORMS:
                    product(*divmod(tile_before, WAYS))
                    for i in after:
                        transposes(*divmod(i, WAYS))
                with pe.Fori(2, NT // WAYS) as n:
                    for i in range(WAYS):
                        product(n, i)
                        transposes(*((n, i - 1) if i > 0 else (n - 1, WAYS - 1)))
                transposes(NT // WAYS - 1, WAYS - 1)

            @block.vector
            def _(dve):
                def residual_norm(n, i):
                    tok_tile = tile(n, i)
                    x1_tile = x1[:, bass.ds(tok_tile, 1), :].rearrange("p a n -> p (a n)")
                    k = i % 2
                    if isinstance(n, int) and n == 0:
                        dve.wait_ge(a_used, (RC - 1) * WAYS + i + 1 + RC)
                    else:
                        dve.wait_ge(a_used, tok_tile * RC + 2 * RC)
                    settle(dve, dve_begun)
                    nc.vector.tensor_tensor(gated[:, :], ps_y[i][:, :], rows[:, 0, :], ALU.mult).then_inc(gated_done, 1)
                    dve.wait_ge(xb_done, tok_tile + 1)
                    dve.wait_ge(gated_done, tok_tile + 1)
                    settle(dve, dve_begun)
                    nc.vector.tensor_tensor(x1_tile, gated[:, :], x1_tile, ALU.add).then_inc(x1_done, 1)
                    dve.wait_ge(x1_done, tok_tile + 1 + WAYS)
                    settle(dve, dve_begun)
                    nc.vector.bn_stats(stats[:, k, :], x1_tile).then_inc(stats_done, 1)
                    dve.wait_ge(stats_done, tok_tile * 2 + 1)
                    settle(dve, dve_begun)
                    nc.vector.bn_aggr(mv[:, k, :], stats[:, k, :]).then_inc(stats_done, 1)
                    dve.wait_ge(stats_done, tok_tile * 2 + 2)
                    nc.vector.tensor_scalar(mv[:, k, 1:2], mv[:, k, 1:2], EPS, None, ALU.add).then_inc(mv_done, 1)
                    dve.wait_ge(std_done, tok_tile + 1)
                    nc.vector.reciprocal(rstd[:, k:k + 1], std[:, k:k + 1]).then_inc(rstd_done, 1)
                    dve.wait_ge(rstd_done, tok_tile + 1)
                    settle(dve, dve_begun)
                    nc.vector.tensor_scalar(h[:, k, :], x1_tile, mv[:, k, 0:1], rstd[:, k:k + 1], ALU.subtract, ALU.mult).then_inc(h_step, 1)
                    dve.wait_ge(h_step, tok_tile * 2 + 1)
                    nc.vector.tensor_tensor(h[:, k, :], h[:, k, :], rows[:, 2, :], ALU.mult).then_inc(h_step, 1)
                    dve.wait_ge(h_step, tok_tile * 2 + 2)
                    nc.vector.tensor_tensor(h[:, k, :], h[:, k, :], rows[:, 1, :], ALU.add).then_inc(h_done, 1)

                def low_part(n, i):
                    cols = bass.ds(tile(n, i) * P, P)
                    dve.wait_ge(hi_done, tile(n, i) + 1)
                    settle(dve, dve_begun)
                    nc.vector.tensor_tensor(hT_lo[:, :, cols], ps_t[i % 2][:, :].rearrange("p (c t) -> p c t", c=HC),
                                            f32(hT_hi[:, :, cols]), ALU.subtract).then_inc(lo_done, 1)

                dve.sem_inc(x1_done, WAYS)
                dve.sem_inc(lo_done, 2)
                for k in range(2 * RC):
                    dve.wait_ge(wo_hi_done, k + 1)
                    nc.vector.tensor_tensor(wo_lo[:, wo_half(k), :], wo_unsplit[:, wo_half(k), :], f32(wo_hi[:, wo_half(k), :]), ALU.subtract).then_inc(wo_split, 1)
                dve.wait_ge(rows_loaded, 64)
                nc.vector.tensor_tensor(bias[:, :], bias[:, :], rows[:, 0, :], ALU.mult).then_inc(bias_ready, 1)
                for _, after in FIRST_NORMS:
                    for i in after:
                        residual_norm(*divmod(i, WAYS))
                    for i in after:
                        low_part(*divmod(i, WAYS))
                with dve.Fori(2, NT // WAYS) as n:
                    for i in range(WAYS):
                        last = (n, i - 1) if i > 0 else (n - 1, WAYS - 1)
                        residual_norm(*last)
                        low_part(*last)
                residual_norm(NT // WAYS - 1, WAYS - 1)
                low_part(NT // WAYS - 1, WAYS - 1)


def stage_d(nc, wg, wu, wd, mods_dram, out, x1, hT_hi, hT_lo):
    with ExitStack() as ctx:
        def sb(name, shape, dt=F32):
            return ctx.enter_context(nc.sbuf_tensor(name, shape, dt))

        def sem(name):
            return ctx.enter_context(nc.semaphore(name))

        def bank(name):
            return ctx.enter_context(nc.psum_tensor(name, [P, UT], F32))

        GC = INNER // (4 * P)
        J = 4
        gate_b = sb("gate_b", [P, HID])
        gu_hi = sb("gu_hi", [P, J, 2, HC, P], F32R)
        with nc.sbuf_tensor("gu_unsplit", [P, J, 2, HC, P], F32) as gu_unsplit:
            pass
        gu_lo = sb("gu_lo", [P, J, 2, HC, P], F32R)
        wd_raw = sb("wd_raw", [P, 2, HID])
        wd_hi = sb("wd_hi", [P, J, HID], F32R)
        wd_lo = sb("wd_lo", [P, J, HID], F32R)
        silu = sb("silu", [P, 2, UT])
        h = sb("d_h", [P, 2, J, UT])
        mag = sb("d_mag", [P, J, UT])
        ge = sb("ge", [P, 6, UT], BF16)
        rank = sb("rank", [P, J, UT], BF16)
        hs_hi = sb("hs_hi", [P, J, UT], F32R)
        hs_lo = sb("hs_lo", [P, J, UT], F32R)
        ps_g = [bank(f"ps_g{i}") for i in range(2)]
        ps_u = [bank(f"ps_u{i}") for i in range(2)]
        ps_d = [bank(f"ps_d{i}") for i in range(2)]

        gate_loaded = sem("gate_loaded")
        gu_loaded = [sem(f"gu_loaded{j}") for j in range(J)]
        gu_hi_done, gu_split = sem("gu_hi_done"), sem("gu_split")
        wd_loaded, wd_scaled, wd_hi_done, wd_split = [sem("wd_loaded0"), sem("wd_loaded1")], sem("wd_scaled"), sem("wd_hi_done"), sem("wd_split")
        g_done, u_done, silu_done, h_done = sem("g_done"), sem("u_done"), sem("silu_done"), sem("d_h_done")
        mag_done, ge_done, rank_step, kept_done = sem("mag_done"), sem("ge_done"), sem("rank_step"), sem("kept_done")
        hs_hi_done, hs_lo_done = sem("hs_hi_done"), sem("hs_lo_done")
        down_done, added, stored = sem("down_done"), sem("added"), sem("stored")
        sp_begun = sem("d_sp_begun")

        def at(unit, per, count):
            g, t = unit
            return g * (UNITS * per) + (t * per + count)

        def following(unit):
            g, t = unit
            return (g, t + 1) if t + 1 < UNITS else (g + 1, 0)

        def last_chunk(g):
            return isinstance(g, int) and g == GC - 1

        with nc.Block() as block:
            @block.sync
            def _(sp):
                def chunk(g):
                    return slice(g, g + 1) if isinstance(g, int) else bass.ds(sp.snap(g), 1)

                def load_gu(g, j, first=False):
                    part = chunk(g)
                    if not first:
                        sp.wait_ge(u_done, at((g - 1, UNITS - 1), J, j + 1))
                        settle(sp, sp_begun)
                    for i, w in enumerate((wg, wu)):
                        sp.dma_start(gu_unsplit[:, j, i, :, :], w[part, :, j, :, :].rearrange("a p c n -> p (a c) n")).then_inc(gu_loaded[j], 16)

                def load_wd(g, j, first=False):
                    part = chunk(g)
                    if not first or j >= 2:
                        sp.wait_ge(wd_split, g * J + (j - 1))
                        settle(sp, sp_begun)
                    sp.dma_start(wd_raw[:, j % 2, :], wd[part, :, j, :].rearrange("a p n -> p (a n)")).then_inc(wd_loaded[j % 2], 16)

                for j in range(J):
                    load_gu(0, j, first=True)
                sp.dma_start(gate_b[:, :], mods_dram[5]).then_inc(gate_loaded, 16)
                for j in range(J):
                    load_wd(0, j, first=True)
                with sp.Fori(0, GC - 1) as g:
                    for j in range(J):
                        load_gu(g + 1, j)
                    for j in range(J):
                        load_wd(g + 1, j)
                for t in range(UNITS):
                    for k in range(4):
                        sp.wait_ge(added, at((GC - 1, t), 4, k + 1) + 2)
                        sp.dma_start(out[4 * t + k], x1[:, 4 * t + k, :]).then_inc(stored, 16)
                sp.wait_ge(stored, 16 * NT)

            @block.gpsimd
            def _(pool):
                def gu_low(g, j):
                    pool.wait_ge(gu_hi_done, g * J + (j + 1))
                    nc.gpsimd.tensor_tensor(gu_lo[:, j], gu_unsplit[:, j], f32(gu_hi[:, j]), ALU.subtract).then_inc(gu_split, 1)

                def wd_scale(g, j):
                    pool.wait_ge(wd_loaded[j % 2], g * 32 + (16 * (j // 2) + 16))
                    nc.gpsimd.tensor_tensor(wd_raw[:, j % 2, :], wd_raw[:, j % 2, :], gate_b[:, :], ALU.mult).then_inc(wd_scaled, 1)

                def wd_low(g, j):
                    pool.wait_ge(wd_hi_done, g * J + (j + 1))
                    nc.gpsimd.tensor_tensor(wd_lo[:, j, :], wd_raw[:, j % 2, :], f32(wd_hi[:, j, :]), ALU.subtract).then_inc(wd_split, 1)

                def split_weights(g, first=False):
                    for j in range(J):
                        if not first:
                            gu_low(g, j)
                    for j0 in (0, 2):
                        for j in (j0, j0 + 1):
                            wd_scale(g, j)
                        for j in (j0, j0 + 1):
                            wd_low(g, j)

                pool.wait_ge(gate_loaded, 16)
                split_weights(0, first=True)
                with pool.Fori(0, GC - 1) as g:
                    split_weights(g + 1)

            @block.scalar
            def _(act):
                def gu_high(g, j):
                    act.wait_ge(gu_loaded[j], g * 32 + 32)
                    nc.scalar.activation(gu_hi[:, j], gu_unsplit[:, j], ACT.Copy).then_inc(gu_hi_done, 1)

                def wd_high(g, j, first=False):
                    if not first:
                        act.wait_ge(down_done, g * (UNITS * 4) + 1)
                    act.wait_ge(wd_scaled, g * J + (j + 1))
                    nc.scalar.activation(wd_hi[:, j, :], wd_raw[:, j % 2, :], ACT.Copy).then_inc(wd_hi_done, 1)

                def silus(unit, j):
                    act.wait_ge(g_done, at(unit, 4, j + 1))
                    act.wait_ge(h_done, at(unit, 4, j + 1))
                    nc.scalar.activation(silu[:, j % 2, :], ps_g[j % 2][:, :], ACT.Silu).then_inc(silu_done, 1)

                def magnitude(unit, j, first=False):
                    if not first:
                        act.wait_ge(ge_done, at(unit, 3, 0))
                    act.wait_ge(h_done, at(unit, 4, j + 1 + 2))
                    nc.scalar.activation(mag[:, j, :], h[:, unit[1] % 2, j, :], ACT.Abs).then_inc(mag_done, 1)

                def kept_high(unit, j):
                    act.wait_ge(down_done, at(unit, 4, 1))
                    act.wait_ge(kept_done, at(unit, 4, j + 1))
                    nc.scalar.activation(hs_hi[:, j, :], h[:, unit[1] % 2, j, :], ACT.Copy).then_inc(hs_hi_done, 1)

                for j in range(J):
                    gu_high(0, j)
                for j in range(J):
                    silus((0, 0), j)
                    magnitude((0, 0), j, first=True)
                    if j % 2 == 1:
                        wd_high(0, j - 1, first=True)
                        wd_high(0, j, first=True)

                def slot(unit, last=False):
                    g, t = unit
                    nxt = following(unit)
                    new_gu = t == UNITS - 2 and not last_chunk(g)
                    new_wd = t == 0 and not (isinstance(g, int) and g == 0)
                    if new_wd:
                        wd_high(g, 0)
                        wd_high(g, 1)
                    if not last:
                        silus(nxt, 0)
                        if t == UNITS - 1:
                            gu_high(g + 1, 3)
                        magnitude(nxt, 0)
                    if new_wd:
                        wd_high(g, 2)
                        wd_high(g, 3)
                    if not last:
                        silus(nxt, 1)
                        if new_gu:
                            gu_high(g + 1, 0)
                        magnitude(nxt, 1)
                    for j in range(J):
                        kept_high(unit, j)
                    if not last:
                        silus(nxt, 2)
                        if new_gu:
                            gu_high(g + 1, 1)
                        magnitude(nxt, 2)
                        if new_gu:
                            gu_high(g + 1, 2)
                        silus(nxt, 3)
                        magnitude(nxt, 3)

                for t in range(UNITS):
                    slot((0, t))
                with act.Fori(1, GC - 1) as g:
                    for t in range(UNITS):
                        slot((g, t))
                for t in range(UNITS):
                    slot((GC - 1, t), last=(t == UNITS - 1))

            @block.tensor
            def _(pe):
                def gate_up(unit, j, which=(0, 1)):
                    g, t = unit
                    cols = slice(t * UT, (t + 1) * UT)
                    if 0 in which:
                        if t == 0:
                            pe.wait_ge(gu_split, g * J + (j + 1))
                        pe.wait_ge(h_done, at(unit, 4, j + 1))
                    for i in which:
                        bank, done = ((ps_g, g_done), (ps_u, u_done))[i]
                        k = 0
                        for w, hT in ((gu_hi, hT_hi), (gu_hi, hT_lo), (gu_lo, hT_hi)):
                            for c in range(HC):
                                last = nc.tensor.matmul(bank[j % 2][:, :], w[:, j, i, c, :], hT[:, c, cols], start=(k == 0), stop=(k == 3 * HC - 1))
                                k += 1
                        last.then_inc(done, 1)

                def down(unit, n):
                    g, t = unit
                    if n == 0:
                        pe.wait_ge(hs_lo_done, at(unit, J, J))
                        if t == 0:
                            pe.wait_ge(wd_split, g * J + J)
                    pe.wait_ge(added, at(unit, 4, n + 1))
                    k = 0
                    for a, w in ((hs_hi, wd_hi), (hs_hi, wd_lo), (hs_lo, wd_hi)):
                        for j in range(J):
                            last = nc.tensor.matmul(ps_d[n % 2][:, :], a[:, j, n * P:(n + 1) * P], w[:, j, :], start=(k == 0), stop=(k == 3 * J - 1))
                            k += 1
                    last.then_inc(down_done, 1)

                def slot(unit):
                    nxt = following(unit)
                    for j in range(J - 1):
                        gate_up(nxt, j)
                    gate_up(nxt, J - 1, (0,))
                    down(unit, 0)
                    down(unit, 1)
                    gate_up(nxt, J - 1, (1,))
                    down(unit, 2)
                    down(unit, 3)

                pe.sem_inc(down_done, 1)
                for j in range(J):
                    gate_up((0, 0), j)
                with pe.Fori(0, GC - 1) as g:
                    for t in range(UNITS):
                        slot((g, t))
                for t in range(UNITS - 2):
                    slot((GC - 1, t))
                for j in range(J):
                    gate_up((GC - 1, UNITS - 1), j)
                for t in (UNITS - 2, UNITS - 1):
                    for n in range(4):
                        down((GC - 1, t), n)

            @block.vector
            def _(dve):
                def gu_low(j):
                    dve.wait_ge(gu_hi_done, j + 1)
                    nc.vector.tensor_tensor(gu_lo[:, j], gu_unsplit[:, j], f32(gu_hi[:, j]), ALU.subtract).then_inc(gu_split, 1)

                def member(unit, j):
                    dve.wait_ge(u_done, at(unit, 4, j + 1))
                    dve.wait_ge(silu_done, at(unit, 4, j + 1))
                    nc.vector.tensor_tensor(h[:, unit[1] % 2, j, :], ps_u[j % 2][:, :], silu[:, j % 2, :], ALU.mult).then_inc(h_done, 1)

                def compare(unit):
                    dve.wait_ge(mag_done, at(unit, J, J))
                    g0 = 0
                    for i, n in ((0, 3), (1, 2), (2, 1)):
                        nc.vector.tensor_tensor(ge[:, g0:g0 + n, :], mag[:, i:i + 1, :].broadcast_to([P, n, UT]), mag[:, i + 1:i + 1 + n, :], ALU.is_ge).then_inc(ge_done, 1)
                        g0 += n

                def count_wins(unit):
                    dve.wait_ge(ge_done, at(unit, 3, 3))
                    for j, a, b, op in ((0, 0, 1, ALU.add), (1, 3, 4, ALU.add), (2, 5, 1, ALU.subtract), (3, 2, 4, ALU.add)):
                        nc.vector.tensor_tensor(rank[:, j, :], ge[:, a, :], ge[:, b, :], op).then_inc(rank_step, 1)
                    for n, (j, b, op) in enumerate(((0, 2, ALU.add), (1, 0, ALU.subtract), (2, 3, ALU.subtract), (3, 5, ALU.add))):
                        dve.wait_ge(rank_step, at(unit, 8, 4 + n))
                        nc.vector.tensor_tensor(rank[:, j, :], rank[:, j, :], ge[:, b, :], op).then_inc(rank_step, 1)

                def keep(unit):
                    tile = h[:, unit[1] % 2, :, :]
                    for n, (j, bound, op) in enumerate(((0, 1.5, ALU.is_ge), (1, 0.5, ALU.is_ge), (2, -0.5, ALU.is_ge), (3, 1.5, ALU.is_le))):
                        if n == 0:
                            dve.wait_ge(rank_step, at(unit, 8, 8))
                        nc.vector.scalar_tensor_tensor(tile[:, j, :], rank[:, j, :], bound, tile[:, j, :], op, ALU.mult).then_inc(kept_done, 1)

                def kept_low(unit, j):
                    dve.wait_ge(hs_hi_done, at(unit, J, j + 1))
                    nc.vector.tensor_tensor(hs_lo[:, j, :], h[:, unit[1] % 2, j, :], f32(hs_hi[:, j, :]), ALU.subtract).then_inc(hs_lo_done, 1)

                def accumulate(unit, n):
                    dve.wait_ge(down_done, at(unit, 4, n + 1 + 1))
                    tile = x1[:, 4 * unit[1] + n, :]
                    nc.vector.tensor_tensor(tile, ps_d[n % 2][:, :], tile, ALU.add).then_inc(added, 1)

                dve.sem_inc(h_done, 2)
                dve.sem_inc(added, 2)
                for j in range(J):
                    gu_low(j)
                for j in range(J):
                    member((0, 0), j)

                def select_beside(unit):
                    nxt = following(unit)
                    compare(unit)
                    member(nxt, 0)
                    count_wins(unit)
                    member(nxt, 1)
                    keep(unit)
                    for j in range(J):
                        kept_low(unit, j)
                    member(nxt, 2)

                def slot(unit):
                    select_beside(unit)
                    accumulate(unit, 0)
                    accumulate(unit, 1)
                    member(following(unit), 3)
                    accumulate(unit, 2)
                    accumulate(unit, 3)

                with dve.Fori(0, GC - 1) as g:
                    for t in range(UNITS):
                        slot((g, t))
                for t in range(UNITS - 2):
                    slot((GC - 1, t))
                last, final = (GC - 1, UNITS - 2), (GC - 1, UNITS - 1)
                select_beside(last)
                member(final, 3)
                compare(final)
                accumulate(last, 0)
                accumulate(last, 1)
                count_wins(final)
                accumulate(last, 2)
                keep(final)
                accumulate(last, 3)
                for j in range(J):
                    kept_low(final, j)
                for n in range(4):
                    accumulate(final, n)


def block_program(nc, x, c_cols, wmod, wq, wk, wv, wo, bo_rep, wg, wu, wd, rope, masks, out):
    mods_dram = nc.dram_tensor("mods_scratch", [6, P, HID], F32, kind="Internal").ap()
    aT_dram = nc.dram_tensor("aT_scratch", [NT, P, PAIRS, P], F32, kind="Internal").ap()
    with ExitStack() as ctx:
        hT_hi = ctx.enter_context(nc.sbuf_tensor("hT_hi", [P, HC, TOK], F32R))
        hT_lo = ctx.enter_context(nc.sbuf_tensor("hT_lo", [P, HC, TOK], F32R))
        stage_a(nc, x, c_cols, wmod, mods_dram, hT_hi, hT_lo)
        stage_b(nc, wq, wk, wv, rope, masks, aT_dram, hT_hi, hT_lo)
        x1 = ctx.enter_context(nc.sbuf_tensor("x1", [P, NT, HID], F32))
        stage_c(nc, x, wo, bo_rep, mods_dram, aT_dram, x1, hT_hi, hT_lo)
        stage_d(nc, wg, wu, wd, mods_dram, out, x1, hT_hi, hT_lo)


def rope_tables():
    inv_freq = (1.0 / 10000.0 ** (np.arange(0, D, 2, dtype=np.float32) / np.float32(D))).astype(np.float32)
    freqs = np.arange(TOK, dtype=np.float32)[None, :] * inv_freq[:, None]
    cos, sin = np.cos(freqs), np.sin(freqs)
    return np.stack([np.tile(cos, (4, 1)), np.tile(np.concatenate([-sin, sin]), (2, 1))]).astype(np.float32)


def mask_table():
    m = np.zeros((P, 512 + P), np.float32)
    m[:, 512:] = np.where(np.arange(P)[:, None] >= np.arange(P)[None, :], 0.0, MASKED)
    return m


def laid_out(x, Wq, Wk, Wv, Wo, bo, w_gate, w_up, w_down, c, wmod):
    def pairs(w):
        return w.reshape(PAIRS, P, HC, P).transpose(0, 3, 2, 1)

    def members(w):
        return w.reshape(HC, P, INNER // (4 * P), P, 4).transpose(2, 1, 4, 0, 3)

    return {
        "x": x.reshape(NT, P, HID),
        "c_cols": c.reshape(HC, P).T,
        "wmod": wmod,
        "wq": pairs(Wq), "wk": pairs(Wk), "wv": pairs(Wv),
        "wo": Wo.T.reshape(PAIRS, P, HID).transpose(1, 0, 2),
        "bo_rep": np.broadcast_to(bo, (P, HID)),
        "wg": members(w_gate), "wu": members(w_up),
        "wd": w_down.reshape(INNER // (4 * P), P, 4, HID),
        "rope": rope_tables(), "masks": mask_table(),
    }


def kernel(L0_attn_hidden_states, L0_attn_Wq, L0_attn_Wk, L0_attn_Wv, L0_attn_Wo, L0_attn_bo,
           L0_ffn_w_gate, L0_ffn_w_up, L0_ffn_w_down, L0_c, L0_wmod):
    import concourse.bacc as bacc
    from concourse.bass_utils import run_bass_kernel_spmd

    nc = bacc.Bacc("TRN2", target_bir_lowering=False, num_devices=1)
    arrays = {n: np.ascontiguousarray(a) for n, a in laid_out(
        np.asarray(L0_attn_hidden_states), np.asarray(L0_attn_Wq), np.asarray(L0_attn_Wk), np.asarray(L0_attn_Wv),
        np.asarray(L0_attn_Wo), np.asarray(L0_attn_bo), np.asarray(L0_ffn_w_gate), np.asarray(L0_ffn_w_up),
        np.asarray(L0_ffn_w_down), np.asarray(L0_c), np.asarray(L0_wmod)).items()}
    args = {n: nc.dram_tensor(n, a.shape, F32, kind="ExternalInput").ap() for n, a in arrays.items()}
    out = nc.dram_tensor("out", (NT, P, HID), F32, kind="ExternalOutput").ap()
    block_program(nc, out=out, **args)
    r = run_bass_kernel_spmd(nc, [arrays], core_ids=[0])
    return r.results[0]["out"].reshape(1, TOK, HID)
```
